# Optimizing a Trainium2 kernel written in Bass

```python
import numpy as np
import jax
import jax.numpy as jnp

def _softmax(x, axis=-1):
    return jax.nn.softmax(x, axis=axis)

def _gelu(x):
    return jax.nn.gelu(x, approximate=True)

def _silu(x):
    return jax.nn.silu(x)

def _sigmoid(x):
    return jax.nn.sigmoid(x)

def _layernorm(x, axis=-1, eps=1e-05):
    m = jnp.mean(x, axis=axis, keepdims=True)
    v = jnp.var(x, axis=axis, keepdims=True)
    return (x - m) / jnp.sqrt(v + eps)

def _scatter_add(tgt, idx, src, axis=0):
    return tgt.at[idx].add(src)

def _segment_sum(src, seg, n):
    return jax.ops.segment_sum(src, seg, n)
kernel_name = 'mk_metaformer_d2_conv_nhwc384_r4_b9c3c1'

def setup_inputs(seed: int=0):
    np.random.seed(seed)
    _w = jnp.asarray

    def _rec_inputs():
        import jax
        import jax.numpy as jnp
        _gk = jax.random.key(seed)
        x = -0.0002221 + 1 * jax.random.normal(jax.random.fold_in(_gk, 1), (16, 32, 32, 96), jnp.float32)
        return x
    x = _rec_inputs()

    def _L0_conv_setup():
        import jax, jax.numpy as jnp
        import numpy as np
        SEG = 8

        def _grouped_mix(y, W2, b2, seg):
            b_, cin, L = y.shape
            cout = W2.shape[0]
            yg = y.reshape(b_, seg, cin // seg, L)
            Wg = W2.reshape(seg, cout // seg, cin // seg)
            z = jnp.einsum('bgcl,goc->bgol', yg, Wg).reshape(b_, cout, L)
            return z + b2[None, :, None]

        def _mix_h(x, W1, b1, W2, b2):
            b_, H, Wd, D = x.shape
            y = jnp.einsum('bhwd,ed->bhwe', x, W1) + b1
            y = jnp.transpose(y, (0, 3, 1, 2)).reshape(b_, -1, Wd)
            z = _grouped_mix(y, W2, b2, SEG)
            attn = jax.nn.softmax(z.reshape(b_, H, H, Wd).transpose(0, 3, 1, 2), axis=-1)
            xr = jnp.transpose(x, (0, 2, 1, 3))
            out = jnp.einsum('bwij,bwjd->bwid', attn, xr)
            return jnp.transpose(out, (0, 2, 1, 3))

        def _mix_w(x, W1, b1, W2, b2):
            b_, H, Wd, D = x.shape
            y = jnp.einsum('bhwd,ed->bhwe', x, W1) + b1
            y = jnp.transpose(y, (0, 3, 2, 1)).reshape(b_, -1, H)
            z = _grouped_mix(y, W2, b2, SEG)
            attn = jax.nn.softmax(z.reshape(b_, Wd, Wd, H).transpose(0, 3, 1, 2), axis=-1)
            return jnp.einsum('bhij,bhjd->bhid', attn, x)
        key = jax.random.key(seed)
        ks = jax.random.split(key, 16)
        B, H, W, D, E = (16, 32, 32, 96, 2)
        s = 0.05
        return {'x': jax.random.normal(ks[0], (B, H, W, D), jnp.float32), 'Wc': jax.random.normal(ks[1], (D, D), jnp.float32) * s, 'bc': jnp.zeros((D,), jnp.float32), 'Wo': jax.random.normal(ks[2], (D, D), jnp.float32) * s, 'bo': jnp.zeros((D,), jnp.float32), 'W1h': jax.random.normal(ks[3], (E, D), jnp.float32) * s, 'b1h': jnp.zeros((E,), jnp.float32), 'W2h': jax.random.normal(ks[4], (H * H, E * H // SEG), jnp.float32) * s, 'b2h': jnp.zeros((H * H,), jnp.float32), 'W1w': jax.random.normal(ks[5], (E, D), jnp.float32) * s, 'b1w': jnp.zeros((E,), jnp.float32), 'W2w': jax.random.normal(ks[6], (W * W, E * W // SEG), jnp.float32) * s, 'b2w': jnp.zeros((W * W,), jnp.float32)}
    _L0_conv_all = _L0_conv_setup()
    _L0_conv_in = {k: v for k, v in _L0_conv_all.items() if k in ('Wc', 'bc', 'Wo', 'bo', 'W1h', 'b1h', 'W2h', 'b2h', 'W1w', 'b1w', 'W2w', 'b2w')}
    del _L0_conv_all

    def _L0_ffn_setup():
        import jax, jax.numpy as jnp
        import numpy as np
        NUM_EXPERTS = 4
        TOP_K = 2
        DIM = 96
        HID = 4 * DIM
        key = jax.random.key(seed)
        ks = jax.random.split(key, 5)
        B, S = (16, 512)
        scale_in = 1.0 / np.sqrt(DIM)
        scale_hid = 1.0 / np.sqrt(HID)
        return {'x': jax.random.normal(ks[0], (B, S, DIM), dtype=jnp.float32), 'gate_w': jax.random.normal(ks[1], (DIM, NUM_EXPERTS), dtype=jnp.float32) * scale_in, 'gate_b': jnp.zeros((NUM_EXPERTS,), dtype=jnp.float32), 'w1': jax.random.normal(ks[2], (NUM_EXPERTS, DIM, HID), dtype=jnp.float32) * scale_in, 'b1': jnp.zeros((NUM_EXPERTS, HID), dtype=jnp.float32), 'w2': jax.random.normal(ks[3], (NUM_EXPERTS, HID, DIM), dtype=jnp.float32) * scale_hid, 'b2': jnp.zeros((NUM_EXPERTS, DIM), dtype=jnp.float32)}
    _L0_ffn_all = _L0_ffn_setup()
    _L0_ffn_in = {k: v for k, v in _L0_ffn_all.items() if k in ('gate_w', 'gate_b', 'w1', 'b1', 'w2', 'b2')}
    del _L0_ffn_all

    def _L1_conv_setup():
        import jax, jax.numpy as jnp
        import numpy as np
        D_MODEL = 96
        D_STATE = 16
        D_CONV = 3
        EXPAND = 2
        D_INNER = EXPAND * D_MODEL
        HEADDIM = 16
        NHEADS = D_INNER // HEADDIM
        NGROUPS = 1
        CHUNK = 16
        D_IN_PROJ = 2 * D_INNER + 2 * NGROUPS * D_STATE + NHEADS
        CONV_DIM = D_INNER + 2 * NGROUPS * D_STATE

        def segsum(x):
            T = x.shape[-1]
            xe = jnp.broadcast_to(x[..., None], x.shape + (T,))
            mask_strict = jnp.tril(jnp.ones((T, T), bool), -1)
            xe = jnp.where(mask_strict, xe, 0.0)
            x_segsum = jnp.cumsum(xe, axis=-2)
            mask_incl = jnp.tril(jnp.ones((T, T), bool), 0)
            return jnp.where(mask_incl, x_segsum, -jnp.inf)

        def ssd_minimal_discrete(X, A, Bm, Cm, block_len):
            b, seqlen, h, p = X.shape
            c = seqlen // block_len
            X = X.reshape(b, c, block_len, h, p)
            Bm = Bm.reshape(b, c, block_len, h, -1)
            Cm = Cm.reshape(b, c, block_len, h, -1)
            A = A.reshape(b, c, block_len, h).transpose(0, 3, 1, 2)
            A_cumsum = jnp.cumsum(A, axis=-1)
            L = jnp.exp(segsum(A))
            Y_diag = jnp.einsum('bclhn,bcshn,bhcls,bcshp->bclhp', Cm, Bm, L, X)
            decay_states = jnp.exp(A_cumsum[:, :, :, -1:] - A_cumsum)
            states = jnp.einsum('bclhn,bhcl,bclhp->bchpn', Bm, decay_states, X)
            init = jnp.zeros_like(states[:, :1])
            states = jnp.concatenate([init, states], axis=1)
            A_last = jnp.pad(A_cumsum[:, :, :, -1], ((0, 0), (0, 0), (1, 0)))
            decay_chunk = jnp.exp(segsum(A_last))
            new_states = jnp.einsum('bhzc,bchpn->bzhpn', decay_chunk, states)
            states, final_state = (new_states[:, :-1], new_states[:, -1])
            state_decay_out = jnp.exp(A_cumsum)
            Y_off = jnp.einsum('bclhn,bchpn,bhcl->bclhp', Cm, states, state_decay_out)
            Y = (Y_diag + Y_off).reshape(b, seqlen, h, p)
            return (Y, final_state)
        key = jax.random.key(seed)
        ks = jax.random.split(key, 10)
        x = jax.random.normal(ks[0], (8, 16, 16, D_MODEL), jnp.float32)
        W_in = jax.random.normal(ks[1], (D_MODEL, D_IN_PROJ), jnp.float32) * 0.02
        W_conv = jax.random.normal(ks[2], (D_CONV, D_CONV, 1, CONV_DIM), jnp.float32) * 0.1
        b_conv = jax.random.normal(ks[3], (CONV_DIM,), jnp.float32) * 0.01
        dt = jnp.exp(jax.random.uniform(ks[4], (NHEADS,)) * (np.log(0.1) - np.log(0.001)) + np.log(0.001))
        dt = jnp.clip(dt, 0.0001, None)
        dt_bias = dt + jnp.log(-jnp.expm1(-dt))
        A_log = jnp.log(jax.random.uniform(ks[5], (NHEADS,), minval=1.0, maxval=16.0))
        D_param = jnp.ones((NHEADS,), jnp.float32)
        gamma = jnp.ones((D_INNER,), jnp.float32)
        beta = jnp.zeros((D_INNER,), jnp.float32)
        W_out = jax.random.normal(ks[6], (D_INNER, D_MODEL), jnp.float32) * 0.02
        return {'x': x, 'W_in': W_in, 'W_conv': W_conv, 'b_conv': b_conv, 'dt_bias': dt_bias, 'A_log': A_log, 'D_param': D_param, 'gamma': gamma, 'beta': beta, 'W_out': W_out}
    _L1_conv_all = _L1_conv_setup()
    _L1_conv_in = {k: v for k, v in _L1_conv_all.items() if k in ('W_in', 'W_conv', 'b_conv', 'dt_bias', 'A_log', 'D_param', 'gamma', 'beta', 'W_out')}
    del _L1_conv_all

    def _L1_ffn_setup():
        import jax, jax.numpy as jnp
        import numpy as np
        NUM_EXPERTS = 4
        TOP_K = 2
        DIM = 96
        HID = 4 * DIM
        key = jax.random.key(seed)
        ks = jax.random.split(key, 5)
        B, S = (16, 512)
        scale_in = 1.0 / np.sqrt(DIM)
        scale_hid = 1.0 / np.sqrt(HID)
        return {'x': jax.random.normal(ks[0], (B, S, DIM), dtype=jnp.float32), 'gate_w': jax.random.normal(ks[1], (DIM, NUM_EXPERTS), dtype=jnp.float32) * scale_in, 'gate_b': jnp.zeros((NUM_EXPERTS,), dtype=jnp.float32), 'w1': jax.random.normal(ks[2], (NUM_EXPERTS, DIM, HID), dtype=jnp.float32) * scale_in, 'b1': jnp.zeros((NUM_EXPERTS, HID), dtype=jnp.float32), 'w2': jax.random.normal(ks[3], (NUM_EXPERTS, HID, DIM), dtype=jnp.float32) * scale_hid, 'b2': jnp.zeros((NUM_EXPERTS, DIM), dtype=jnp.float32)}
    _L1_ffn_all = _L1_ffn_setup()
    _L1_ffn_in = {k: v for k, v in _L1_ffn_all.items() if k in ('gate_w', 'gate_b', 'w1', 'b1', 'w2', 'b2')}
    del _L1_ffn_all
    return {'x': x, 'L0_conv_Wc': _L0_conv_in['Wc'], 'L0_conv_bc': _L0_conv_in['bc'], 'L0_conv_Wo': _L0_conv_in['Wo'], 'L0_conv_bo': _L0_conv_in['bo'], 'L0_conv_W1h': _L0_conv_in['W1h'], 'L0_conv_b1h': _L0_conv_in['b1h'], 'L0_conv_W2h': _L0_conv_in['W2h'], 'L0_conv_b2h': _L0_conv_in['b2h'], 'L0_conv_W1w': _L0_conv_in['W1w'], 'L0_conv_b1w': _L0_conv_in['b1w'], 'L0_conv_W2w': _L0_conv_in['W2w'], 'L0_conv_b2w': _L0_conv_in['b2w'], 'L0_ffn_gate_w': _L0_ffn_in['gate_w'], 'L0_ffn_gate_b': _L0_ffn_in['gate_b'], 'L0_ffn_w1': _L0_ffn_in['w1'], 'L0_ffn_b1': _L0_ffn_in['b1'], 'L0_ffn_w2': _L0_ffn_in['w2'], 'L0_ffn_b2': _L0_ffn_in['b2'], 'L1_conv_W_in': _L1_conv_in['W_in'], 'L1_conv_W_conv': _L1_conv_in['W_conv'], 'L1_conv_b_conv': _L1_conv_in['b_conv'], 'L1_conv_dt_bias': _L1_conv_in['dt_bias'], 'L1_conv_A_log': _L1_conv_in['A_log'], 'L1_conv_D_param': _L1_conv_in['D_param'], 'L1_conv_gamma': _L1_conv_in['gamma'], 'L1_conv_beta': _L1_conv_in['beta'], 'L1_conv_W_out': _L1_conv_in['W_out'], 'L1_ffn_gate_w': _L1_ffn_in['gate_w'], 'L1_ffn_gate_b': _L1_ffn_in['gate_b'], 'L1_ffn_w1': _L1_ffn_in['w1'], 'L1_ffn_b1': _L1_ffn_in['b1'], 'L1_ffn_w2': _L1_ffn_in['w2'], 'L1_ffn_b2': _L1_ffn_in['b2']}

def reference(x, L0_conv_Wc, L0_conv_bc, L0_conv_Wo, L0_conv_bo, L0_conv_W1h, L0_conv_b1h, L0_conv_W2h, L0_conv_b2h, L0_conv_W1w, L0_conv_b1w, L0_conv_W2w, L0_conv_b2w, L0_ffn_gate_w, L0_ffn_gate_b, L0_ffn_w1, L0_ffn_b1, L0_ffn_w2, L0_ffn_b2, L1_conv_W_in, L1_conv_W_conv, L1_conv_b_conv, L1_conv_dt_bias, L1_conv_A_log, L1_conv_D_param, L1_conv_gamma, L1_conv_beta, L1_conv_W_out, L1_ffn_gate_w, L1_ffn_gate_b, L1_ffn_w1, L1_ffn_b1, L1_ffn_w2, L1_ffn_b2):
    import jax
    import jax.numpy as jnp

    def _L0_conv_ref(x, Wc, bc, Wo, bo, W1h, b1h, W2h, b2h, W1w, b1w, W2w, b2w):
        import jax, jax.numpy as jnp
        import numpy as np
        SEG = 8

        def _grouped_mix(y, W2, b2, seg):
            b_, cin, L = y.shape
            cout = W2.shape[0]
            yg = y.reshape(b_, seg, cin // seg, L)
            Wg = W2.reshape(seg, cout // seg, cin // seg)
            z = jnp.einsum('bgcl,goc->bgol', yg, Wg).reshape(b_, cout, L)
            return z + b2[None, :, None]

        def _mix_h(x, W1, b1, W2, b2):
            b_, H, Wd, D = x.shape
            y = jnp.einsum('bhwd,ed->bhwe', x, W1) + b1
            y = jnp.transpose(y, (0, 3, 1, 2)).reshape(b_, -1, Wd)
            z = _grouped_mix(y, W2, b2, SEG)
            attn = jax.nn.softmax(z.reshape(b_, H, H, Wd).transpose(0, 3, 1, 2), axis=-1)
            xr = jnp.transpose(x, (0, 2, 1, 3))
            out = jnp.einsum('bwij,bwjd->bwid', attn, xr)
            return jnp.transpose(out, (0, 2, 1, 3))

        def _mix_w(x, W1, b1, W2, b2):
            b_, H, Wd, D = x.shape
            y = jnp.einsum('bhwd,ed->bhwe', x, W1) + b1
            y = jnp.transpose(y, (0, 3, 2, 1)).reshape(b_, -1, H)
            z = _grouped_mix(y, W2, b2, SEG)
            attn = jax.nn.softmax(z.reshape(b_, Wd, Wd, H).transpose(0, 3, 1, 2), axis=-1)
            return jnp.einsum('bhij,bhjd->bhid', attn, x)
        Y_c = jnp.einsum('bhwd,od->bhwo', x, Wc) + bc
        Y_h = _mix_h(x, W1h, b1h, W2h, b2h)
        Y_w = _mix_w(x, W1w, b1w, W2w, b2w)
        Y = Y_h + Y_w + Y_c
        return jnp.einsum('bhwd,od->bhwo', Y, Wo) + bo

    def _L0_ffn_ref(x, gate_w, gate_b, w1, b1, w2, b2):
        import jax, jax.numpy as jnp
        import numpy as np
        NUM_EXPERTS = 4
        TOP_K = 2
        DIM = 96
        HID = 4 * DIM
        scores = jnp.einsum('bsd,de->bse', x, gate_w) + gate_b
        probs = jax.nn.softmax(scores, axis=-1)
        topk_vals, topk_idx = jax.lax.top_k(probs, TOP_K)
        mask = jnp.sum(jax.nn.one_hot(topk_idx, NUM_EXPERTS, dtype=probs.dtype), axis=-2)
        masked = probs * mask
        masked = masked / (jnp.sum(masked, axis=-1, keepdims=True) + 1e-09)
        h = jax.nn.gelu(jnp.einsum('bsd,edh->ebsh', x, w1) + b1[:, None, None, :], approximate=False)
        y = jnp.einsum('ebsh,ehd->ebsd', h, w2) + b2[:, None, None, :]
        out = jnp.einsum('bse,ebsd->bsd', masked, y)
        return out

    def _L1_conv_ref(x, W_in, W_conv, b_conv, dt_bias, A_log, D_param, gamma, beta, W_out):
        import jax, jax.numpy as jnp
        import numpy as np
        D_MODEL = 96
        D_STATE = 16
        D_CONV = 3
        EXPAND = 2
        D_INNER = EXPAND * D_MODEL
        HEADDIM = 16
        NHEADS = D_INNER // HEADDIM
        NGROUPS = 1
        CHUNK = 16
        D_IN_PROJ = 2 * D_INNER + 2 * NGROUPS * D_STATE + NHEADS
        CONV_DIM = D_INNER + 2 * NGROUPS * D_STATE

        def segsum(x):
            T = x.shape[-1]
            xe = jnp.broadcast_to(x[..., None], x.shape + (T,))
            mask_strict = jnp.tril(jnp.ones((T, T), bool), -1)
            xe = jnp.where(mask_strict, xe, 0.0)
            x_segsum = jnp.cumsum(xe, axis=-2)
            mask_incl = jnp.tril(jnp.ones((T, T), bool), 0)
            return jnp.where(mask_incl, x_segsum, -jnp.inf)

        def ssd_minimal_discrete(X, A, Bm, Cm, block_len):
            b, seqlen, h, p = X.shape
            c = seqlen // block_len
            X = X.reshape(b, c, block_len, h, p)
            Bm = Bm.reshape(b, c, block_len, h, -1)
            Cm = Cm.reshape(b, c, block_len, h, -1)
            A = A.reshape(b, c, block_len, h).transpose(0, 3, 1, 2)
            A_cumsum = jnp.cumsum(A, axis=-1)
            L = jnp.exp(segsum(A))
            Y_diag = jnp.einsum('bclhn,bcshn,bhcls,bcshp->bclhp', Cm, Bm, L, X)
            decay_states = jnp.exp(A_cumsum[:, :, :, -1:] - A_cumsum)
            states = jnp.einsum('bclhn,bhcl,bclhp->bchpn', Bm, decay_states, X)
            init = jnp.zeros_like(states[:, :1])
            states = jnp.concatenate([init, states], axis=1)
            A_last = jnp.pad(A_cumsum[:, :, :, -1], ((0, 0), (0, 0), (1, 0)))
            decay_chunk = jnp.exp(segsum(A_last))
            new_states = jnp.einsum('bhzc,bchpn->bzhpn', decay_chunk, states)
            states, final_state = (new_states[:, :-1], new_states[:, -1])
            state_decay_out = jnp.exp(A_cumsum)
            Y_off = jnp.einsum('bclhn,bchpn,bhcl->bclhp', Cm, states, state_decay_out)
            Y = (Y_diag + Y_off).reshape(b, seqlen, h, p)
            return (Y, final_state)
        Bsz, H, W, C = x.shape
        L = H * W
        xf = x.reshape(Bsz, L, C)
        zxbcdt = xf @ W_in
        z = zxbcdt[..., :D_INNER]
        xBC = zxbcdt[..., D_INNER:D_INNER + CONV_DIM]
        dt = jax.nn.softplus(zxbcdt[..., D_INNER + CONV_DIM:] + dt_bias)
        xBC = xBC.reshape(Bsz, H, W, CONV_DIM)
        xBC = jax.lax.conv_general_dilated(xBC, W_conv, window_strides=(1, 1), padding='SAME', dimension_numbers=('NHWC', 'HWIO', 'NHWC'), feature_group_count=CONV_DIM) + b_conv
        xBC = jax.nn.silu(xBC).reshape(Bsz, L, CONV_DIM)
        x_inner = xBC[..., :D_INNER].reshape(Bsz, L, NHEADS, HEADDIM)
        gn = NGROUPS * D_STATE
        B_state = xBC[..., D_INNER:D_INNER + gn].reshape(Bsz, L, NGROUPS, D_STATE)
        C_state = xBC[..., D_INNER + gn:].reshape(Bsz, L, NGROUPS, D_STATE)
        rep = NHEADS // NGROUPS
        B_state = jnp.broadcast_to(B_state[:, :, :, None, :], (Bsz, L, NGROUPS, rep, D_STATE)).reshape(Bsz, L, NHEADS, D_STATE)
        C_state = jnp.broadcast_to(C_state[:, :, :, None, :], (Bsz, L, NGROUPS, rep, D_STATE)).reshape(Bsz, L, NHEADS, D_STATE)
        A = -jnp.exp(A_log)
        y, _ = ssd_minimal_discrete(x_inner * dt[..., None], A[None, None, :] * dt, B_state, C_state, CHUNK)
        y = y + x_inner * D_param[None, None, :, None]
        y = y.reshape(Bsz, L, D_INNER)
        mu = jnp.mean(y, axis=-1, keepdims=True)
        var = jnp.mean((y - mu) ** 2, axis=-1, keepdims=True)
        y = (y - mu) * jax.lax.rsqrt(var + 1e-05) * gamma + beta
        y = y * jax.nn.silu(z)
        y = y @ W_out
        return y.reshape(Bsz, H, W, D_MODEL)

    def _L1_ffn_ref(x, gate_w, gate_b, w1, b1, w2, b2):
        import jax, jax.numpy as jnp
        import numpy as np
        NUM_EXPERTS = 4
        TOP_K = 2
        DIM = 96
        HID = 4 * DIM
        scores = jnp.einsum('bsd,de->bse', x, gate_w) + gate_b
        probs = jax.nn.softmax(scores, axis=-1)
        topk_vals, topk_idx = jax.lax.top_k(probs, TOP_K)
        mask = jnp.sum(jax.nn.one_hot(topk_idx, NUM_EXPERTS, dtype=probs.dtype), axis=-2)
        masked = probs * mask
        masked = masked / (jnp.sum(masked, axis=-1, keepdims=True) + 1e-09)
        h = jax.nn.gelu(jnp.einsum('bsd,edh->ebsh', x, w1) + b1[:, None, None, :], approximate=False)
        y = jnp.einsum('ebsh,ehd->ebsd', h, w2) + b2[:, None, None, :]
        out = jnp.einsum('bse,ebsd->bsd', masked, y)
        return out

    def _gn(v, G=32, eps=1e-05):
        B_, H_, W_, C_ = v.shape
        g = v.reshape(B_, H_, W_, G, C_ // G)
        m = jnp.mean(g, axis=(1, 2, 4), keepdims=True)
        s = jnp.var(g, axis=(1, 2, 4), keepdims=True)
        return ((g - m) / jnp.sqrt(s + eps)).reshape(v.shape)

    def _ln_c(v, eps=1e-06):
        m = jnp.mean(v, axis=-1, keepdims=True)
        s = jnp.var(v, axis=-1, keepdims=True)
        return (v - m) / jnp.sqrt(s + eps)

    def _ln_t(v, eps=1e-05):
        m = jnp.mean(v, axis=-1, keepdims=True)
        s = jnp.var(v, axis=-1, keepdims=True)
        return (v - m) / jnp.sqrt(s + eps)

    def _to_tokens(v):
        B_, H_, W_, C_ = v.shape
        return v.reshape(B_, H_ * W_, C_)

    def _from_tokens(t, like):
        return t.reshape(like.shape)
    x = x + _L0_conv_ref(_ln_c(x), L0_conv_Wc, L0_conv_bc, L0_conv_Wo, L0_conv_bo, L0_conv_W1h, L0_conv_b1h, L0_conv_W2h, L0_conv_b2h, L0_conv_W1w, L0_conv_b1w, L0_conv_W2w, L0_conv_b2w)
    t = _to_tokens(x)
    t = t + _L0_ffn_ref(_ln_t(t), L0_ffn_gate_w, L0_ffn_gate_b, L0_ffn_w1, L0_ffn_b1, L0_ffn_w2, L0_ffn_b2)
    x = _from_tokens(t, x)
    x = x + _L1_conv_ref(_ln_c(x), L1_conv_W_in, L1_conv_W_conv, L1_conv_b_conv, L1_conv_dt_bias, L1_conv_A_log, L1_conv_D_param, L1_conv_gamma, L1_conv_beta, L1_conv_W_out)
    t = _to_tokens(x)
    t = t + _L1_ffn_ref(_ln_t(t), L1_ffn_gate_w, L1_ffn_gate_b, L1_ffn_w1, L1_ffn_b1, L1_ffn_w2, L1_ffn_b2)
    x = _from_tokens(t, x)
    return x

_drawn_inputs = setup_inputs


def setup_inputs(seed=0):
    import zlib

    import numpy as np

    out = dict(_drawn_inputs(seed))
    spreads = {'L0_conv_bc': (0.0, 0.1),
     'L0_conv_bo': (0.0, 0.1),
     'L0_conv_b1h': (0.0, 0.8),
     'L0_conv_b2h': (0.0, 0.1),
     'L0_conv_b1w': (0.0, 0.561),
     'L0_conv_b2w': (0.0, 0.1),
     'L0_ffn_gate_b': (0.0, 0.1),
     'L0_ffn_b1': (0.0, 0.1),
     'L0_ffn_b2': (0.0, 0.1),
     'L1_conv_D_param': (1.0, 0.6),
     'L1_conv_gamma': (1.0, 0.6),
     'L1_conv_beta': (0.0, 0.792),
     'L1_ffn_gate_b': (0.0, 0.1),
     'L1_ffn_b1': (0.0, 0.1),
     'L1_ffn_b2': (0.0, 0.1)}
    factors = {'L0_conv_W1h': 2.892,
     'L0_conv_W2h': 2.794,
     'L1_conv_b_conv': 4.602,
     'L1_conv_dt_bias': 8.0,
     'L1_conv_A_log': 8.0}
    for name, (base, spread) in spreads.items():
        noise = np.random.default_rng([zlib.crc32(name.encode()), seed]).standard_normal(out[name].shape)
        drawn = base * np.exp(spread * noise) if base else spread * noise
        out[name] = jnp.asarray(drawn.astype(out[name].dtype))
    for name, factor in factors.items():
        out[name] = (out[name] * factor).astype(out[name].dtype)
    return out
```

```python
from contextlib import ExitStack

import concourse.bass as bass
from concourse import mybir

ALU = mybir.AluOpType
ACT = mybir.ActivationFunctionType
AX = mybir.AxisListType
F32 = mybir.dt.float32

P = 128
IMG, SIDE, D = 16, 32, 96
PACK = P // SIDE
G = IMG // PACK
Q = 4
NQ = SIDE // Q
NT = G * NQ
BANK = 512
E0 = 2
SEG = 8
NV = 2 * D + 2 * E0
NEXP, HID = 4, 384
NC = NEXP * HID // P
CPE = HID // P
INNER, NH, HD, NS = 192, 12, 16, 16
CONV = INNER + 2 * NS
XB = CONV + NS
TAPS = 9
CENTRE = TAPS // 2
CONSTS = 4 * P + SIDE + 16
MIXC, FFNC, SSMC = 52, 25, 374


class Chain:

    def __init__(self, eng, sem):
        self.eng, self.sem, self.base, self.n = eng, sem, 0, 0

    def done(self, ins):
        ins.then_inc(self.sem, 1)
        self.n += 1

    def wait(self):
        self.eng.wait_ge(self.sem, self.base + self.n)

    def link(self, ins):
        self.done(ins)
        self.wait()

    def enter(self, i, per):
        self.start = self.base + self.n
        self.base, self.n = i * per + self.start, 0

    def leave(self, rounds, per):
        assert self.n == per, (self.n, per)
        self.base, self.n = self.start + rounds * per, 0


def metaformer(nc, inp, out, stop=9):
    with ExitStack() as ctx:
        def sb(name, shape, dt=F32):
            return ctx.enter_context(nc.sbuf_tensor(name, shape, dt))

        def sem(name):
            return ctx.enter_context(nc.semaphore(name))

        ps = ctx.enter_context(nc.psum_tensor("ps", [P, 8, BANK], F32))

        xr = sb("residual", [P, G, SIDE, D])
        consts = sb("consts", [P, CONSTS])
        ident = consts[:, 0:P]
        upto = consts[:, P:2 * P]
        later = consts[:, 2 * P:3 * P]
        whole = consts[:, 3 * P:4 * P]
        tri = consts[:, 4 * P:4 * P + SIDE]
        lower = consts[:, 4 * P + SIDE:CONSTS].rearrange("p (a b) -> p a b", b=NEXP)
        stats = sb("stats", [P, SIDE, 6])
        moments = sb("moments", [P, 6, SIDE])
        half_neg = sb("half_neg", [P, SIDE])
        eps = sb("eps", [P, 2])
        w1 = sb("w1", [D + 1, NC * P])
        w2 = sb("w2", [P, NC, D])
        b2 = sb("b2", [D, NEXP])
        gw = sb("gw", [D + 1, NEXP])
        xn = sb("xn", [P, SIDE, D])
        arena = sb("arena", [P, 27500])
        top = [0]

        def part(*shape):
            n = 1
            for s in shape:
                n *= s
            ap = arena[:, top[0]:top[0] + n]
            top[0] += n
            assert top[0] <= 27500, top[0]
            names = "abcd"[:len(shape)]
            if len(shape) == 1:
                return ap
            return ap.rearrange(f"p ({' '.join(names)}) -> p {' '.join(names)}", **dict(zip(names[1:], shape[1:])))

        top[0] = 0
        wc = part(D + 1)
        wo_t = part(D)
        bo = part(D)
        rhs0 = part(NV)
        w2z = part(2, SIDE * SIDE)
        xt0 = part(NQ * BANK)
        vc = part(SIDE, NV)
        vh = part(SIDE, D)
        oh = part(SIDE, D)
        yb = part(2, 2 * SIDE)
        ywt = part(2 * SIDE)
        yt = part(2, P)
        row_max = part(SIDE)
        row_sum = part(SIDE)
        row_inv = part(SIDE)
        sc = part(SIDE, SIDE)
        at = part(2, SIDE, SIDE)
        ohw = xn

        top[0] = 0
        xn4 = part(Q, D)
        xt4 = part(BANK)
        hid = part(3, BANK)
        yte = part(2, BANK)
        gd = part(Q, NEXP)
        gth = part(Q, NEXP)
        gn = part(Q, NEXP)
        ge = part(Q, NEXP)
        gmask = part(Q, NEXP)
        gcmp = part(Q, NEXP, NEXP)
        geq = part(Q, NEXP, NEXP)
        gcol = part(4, Q)
        gm = part(Q, NEXP)

        top[0] = 0
        wtap = part(TAPS, CONV + NH)
        wz = part(2, D)
        winx = part(CONV)
        wcv = part(TAPS, CONV)
        x3 = part(3, 4, Q, P)
        xbc = part(2, Q, XB)
        dtr = part(2, Q, NH)
        szt = part(2, 2, BANK)
        th = part(BANK)
        thz = part(BANK)
        neg_a = part(NH)
        d_par = part(NH)
        gamma = part(2)
        beta = part(2)
        wout = part(2, D)
        sp = part(6, Q * NH)
        dt = part(2, Q, NH)
        av = part(2, Q, NH)
        ex3 = part(3, Q, NH)
        wdt = part(Q, NH)
        rr = part(Q, NH, SIDE)
        ll = part(2, NH, SIDE)
        gmk = part(SIDE)
        mm = part(2, NH, SIDE)
        bt = part(Q, SIDE)
        ct = part(Q, SIDE)
        xdt = part(Q, NH, HD)
        xw = part(Q, NH, HD)
        xd = part(Q, NH, HD)
        st = part(NH, HD)
        st1 = part(NH, HD)
        yy = part(2, Q, INNER)
        u4 = part(Q, INNER)
        g4 = part(2, BANK)

        const_in, mix_in, ffn_in, x_in = sem("const_in"), sem("mix_in"), sem("ffn_in"), sem("x_in")
        ssm_in, x_out = sem("ssm_in"), sem("x_out")
        dve_chain, pool_chain, act_chain = sem("dve_chain"), sem("pool_chain"), sem("act_chain")
        ones_set, prep_pe, prep_done = sem("ones_set"), sem("prep_pe"), sem("prep_done")
        stage_end, waited = sem("stage_end"), sem("waited")
        var_ready, rstd_ready = sem("var_ready"), sem("rstd_ready")
        m_ln, m_b01_pe, m_b01_ev = sem("m_ln"), sem("m_b01_pe"), sem("m_b01_ev")
        m_v_pe, m_v_ev, m_yb, m_yt_pe, m_yt_ev = (sem(n) for n in ("m_v_pe", "m_v_ev", "m_yb", "m_yt_pe", "m_yt_ev"))
        m_z_pe, m_sub, m_exp, m_at, m_w_pe, m_w_add = (sem(n) for n in ("m_z_pe", "m_sub", "m_exp", "m_at", "m_w_pe", "m_w_add"))
        ffn_sems = []
        for l in range(2):
            ffn_sems.append({n: sem(f"f{l}_{n}") for n in (
                "ln", "xt_pe", "xt_ev", "gate_pe", "gate_d", "tanh", "mm1", "gelu", "mm2", "y_ev", "yt_pe", "comb")})
        s = {n: sem("s_" + n) for n in (
            "ln", "b0_pe", "b0_ev", "x3", "cv", "cv_th", "cv_ev", "z_pe", "z_th", "z_ev", "raw", "exp_dt", "a", "cs", "ex",
            "w", "bt", "r", "xdt", "xw", "xd", "d_pe", "l", "g_pe", "m", "y_pe", "y", "ds_pe", "s1", "state", "u", "gate", "o_pe", "o_add")}

        block = ctx.enter_context(nc.Block())

        def bank(b, n=1):
            return ps[:, b:b + n, :].rearrange("p a b -> p (a b)")

        def layer_norm(dve, ch, src, dst, n, width, which_eps, count, ready):
            for r in range(n):
                i = dve.bn_stats(stats[:, r, :], src(r))
                ch.done(i)
            ch.wait()
            sv = stats[:, 0:n, :]
            mo = moments[:, :, 0:n]
            ch.done(dve.tensor_tensor(mo[:, 0, :], sv[:, :, 1], sv[:, :, 4], ALU.add))
            ch.done(dve.tensor_tensor(mo[:, 1, :], sv[:, :, 1], sv[:, :, 4], ALU.subtract))
            ch.link(dve.tensor_tensor(mo[:, 2, :], sv[:, :, 2], sv[:, :, 5], ALU.add))
            ch.done(dve.tensor_scalar(mo[:, 0, :], mo[:, 0, :], 0.5, None, ALU.mult))
            ch.link(dve.tensor_tensor(mo[:, 1, :], mo[:, 1, :], mo[:, 1, :], ALU.mult))
            ch.link(dve.scalar_tensor_tensor(mo[:, 3, :], mo[:, 1, :], width / 4.0, mo[:, 2, :], ALU.mult, ALU.add))
            dve.tensor_scalar(mo[:, 4, :], mo[:, 3, :], 1.0 / width, which_eps, ALU.mult, ALU.add).then_inc(var_ready, 1)
            dve.wait_ge(rstd_ready, count)
            for r in range(n):
                i = dve.tensor_scalar(dst(r), src(r), mo[:, 0, r:r + 1], mo[:, 5, r:r + 1], ALU.subtract, ALU.mult)
                if ready is not None and (r + 1) % Q == 0:
                    i.then_inc(ready, 1)

        def rstd(pool, n, count):
            pool.wait_ge(var_ready, count)
            pool.tensor_tensor(moments[:, 5, 0:n], moments[:, 4, 0:n], half_neg[:, 0:n], ALU.pow).then_inc(rstd_ready, 1)

        LN_FFN0 = G
        LN_MIX1 = LN_FFN0 + NT
        LN_FFN1 = LN_MIX1 + G * (NQ + 1)

        BANK0 = ["T0", "T1"]
        for q in range(NQ + 2):
            BANK0 += [f"U{q - 2}", f"U{q - 2}"] * (q >= 2) + [f"T{q + 2}"] * (q + 2 < NQ)

        @block.sync
        def _(sp_):
            sp_.dma_start(consts[:, :], inp["consts"]).then_inc(const_in, 16)
            for g in range(G):
                if g:
                    sp_.wait_ge(x_in, 64 * g)
                for b in range(PACK):
                    sp_.dma_start(xr[b * SIDE:(b + 1) * SIDE, g, :, :],
                                  inp["x"][g * PACK + b].rearrange("h w d -> w h d")).then_inc(x_in, 16)
                if g == 0:
                    sp_.dma_start(wc[0:D, 0:D], inp["Wc"]).then_inc(mix_in, 16)
                    sp_.dma_start(wc[0:D, D:D + 1], inp["bc"]).then_inc(mix_in, 16)
                    sp_.dma_start(wo_t[0:D, :], inp["WoT"]).then_inc(mix_in, 16)
                    sp_.dma_start(bo[D:D + 1, :], inp["bo"]).then_inc(mix_in, 16)
                    sp_.dma_start(rhs0[0:D + 1, 2 * D:NV], inp["W1T"]).then_inc(mix_in, 16)
                    sp_.wait_ge(ones_set, 1)
                    for m in range(2):
                        for c in range(SEG):
                            sp_.dma_start(w2z[8 * c:8 * c + 8, m, c * P:(c + 1) * P], inp["W2T"][m, c]).then_inc(mix_in, 16)
                        sp_.dma_start(w2z[64:65, m, :], inp["b2z"][m]).then_inc(mix_in, 16)

            def ffn_weights(l):
                w = inp["ffn"][l]
                sp_.dma_start(w1[0:D, :].rearrange("p (e h) -> p e h", h=HID), w["w1"].rearrange("e d h -> d e h")).then_inc(ffn_in, 16)
                sp_.dma_start(w1[D:D + 1, :], w["b1"]).then_inc(ffn_in, 16)
                sp_.dma_start(w2[:, :, :], w["w2"].rearrange("e (c p) d -> p (e c) d", p=P)).then_inc(ffn_in, 16)
                sp_.dma_start(b2[:, :], w["b2T"]).then_inc(ffn_in, 16)
                sp_.dma_start(gw[0:D, :], w["gate_w"]).then_inc(ffn_in, 16)
                sp_.dma_start(gw[D:D + 1, :], w["gate_b"]).then_inc(ffn_in, 16)

            ffn_weights(0)
            if stop >= 3:
                sp_.wait_ge(stage_end, 2)
                sp_.dma_start(wz[0:D, :, :], inp["Win_z"]).then_inc(ssm_in, 16)
                sp_.dma_start(wtap[0:D, CENTRE, CONV:CONV + NH], inp["Win_dt"]).then_inc(ssm_in, 16)
                sp_.dma_start(wtap[D:D + 1, CENTRE, CONV:CONV + NH], inp["dt_bias"]).then_inc(ssm_in, 16)
                sp_.dma_start(winx[0:D, :], inp["Win_x"]).then_inc(ssm_in, 16)
                sp_.dma_start(wtap[D:D + 1, CENTRE, 0:CONV], inp["b_conv"]).then_inc(ssm_in, 16)
                sp_.dma_start(wcv[0:D, :, :], inp["W_conv"].partition_broadcast(D)).then_inc(ssm_in, 16)
                sp_.dma_start(neg_a[:, :], inp["A_log"].partition_broadcast(P)).then_inc(ssm_in, 16)
                sp_.dma_start(d_par[:, :], inp["D_param"].partition_broadcast(P)).then_inc(ssm_in, 16)
                sp_.dma_start(gamma[0:D, :], inp["gamma"]).then_inc(ssm_in, 16)
                sp_.dma_start(beta[0:D, :], inp["beta"]).then_inc(ssm_in, 16)
                sp_.dma_start(wout[0:D, :, :], inp["W_out"]).then_inc(ssm_in, 16)
            if stop >= 4:
                ffn_weights(1)
            sp_.wait_ge(stage_end, stop if stop < 4 else 4)
            sp_.wait_ge(ffn_in, 96)
            for g in range(G):
                for b in range(PACK):
                    sp_.dma_start(out[g * PACK + b].rearrange("h w d -> w h d"),
                                  xr[b * SIDE:(b + 1) * SIDE, g, :, :]).then_inc(x_out, 16)
            sp_.wait_ge(x_out, 16 * IMG)

        @block.gpsimd
        def _(pool):
            ch = Chain(pool, pool_chain)
            ch.done(pool.memset(half_neg[:, :], -0.5))
            ch.link(pool.memset(yt[:, :, :], 1.0))
            pool.memset(w2z[:, :, :], 0.0).then_inc(ones_set, 1)
            with pool.Fori(0, G) as g:
                rstd(pool, SIDE, g + 1)
            if stop >= 2:
                with pool.Fori(0, NT) as t:
                    rstd(pool, Q, t + (LN_FFN0 + 1))
            if stop >= 3:
                pool.wait_ge(stage_end, 2)
                ch.done(pool.memset(x3[:, :, :, :, :], 0.0))
                ch.link(pool.memset(xbc[:, :, :, CONV:XB], 0.0))
                pool.memset(x3[D:D + 1, 0, :, :, :], 1.0).then_inc(ones_set, 1)
                pool.wait_ge(prep_done, 2)
                with pool.Fori(0, G) as g:
                    ln = g * (NQ + 1) + LN_MIX1
                    rstd(pool, SIDE, ln + 1)
                    for q in range(NQ + 2):
                        if q >= 2:
                            rstd(pool, Q, ln + q)
                        if not 1 <= q <= NQ:
                            continue
                        c = q - 1
                        k = g * NQ + (c + 1)

                        def steps(i):
                            pool.tensor_tensor(
                                rr[:, i, :, :], av[:, c % 2, i, :].unsqueeze(2).to_broadcast([P, NH, SIDE]),
                                tri.unsqueeze(1).to_broadcast([P, NH, SIDE]), ALU.mult).then_inc(s["r"], 1)

                        xs = xbc[:, c % 2, :, 0:INNER].rearrange("p q (h e) -> p q h e", e=HD)

                        def scaled(dst, by, done):
                            pool.tensor_tensor(dst, xs, by.unsqueeze(3).to_broadcast([P, Q, NH, HD]), ALU.mult).then_inc(s[done], 1)

                        def decayed(i):
                            pool.wait_ge(s["state"], g * (SIDE + 1) + (Q * c + i + 1))
                            pool.tensor_tensor(st1[:, :, :], st[:, :, :],
                                               ex3[:, 2, i, :].unsqueeze(2).to_broadcast([P, NH, HD]), ALU.mult).then_inc(s["s1"], 1)

                        pool.wait_ge(s["a"], k)
                        steps(0)
                        scaled(xdt[:, :, :, :], dt[:, c % 2, :, :], "xdt")
                        pool.wait_ge(s["w"], k)
                        scaled(xw[:, :, :, :], wdt[:, :, :], "xw")
                        steps(1)
                        scaled(xd[:, :, :, :], d_par.unsqueeze(1).to_broadcast([P, Q, NH]), "xd")
                        decayed(0)
                        steps(2)
                        decayed(1)
                        steps(3)
                        decayed(2)
                        decayed(3)
            if stop >= 4:
                with pool.Fori(0, NT) as t:
                    rstd(pool, Q, t + (LN_FFN1 + 1))

        @block.scalar
        def _(act):
            act.sem_inc(m_b01_ev, 2)
            with act.Fori(0, G) as g:
                def evacuate(k, dst):
                    act.wait_ge(m_b01_pe, g * (2 * NQ) + (k + 1))
                    act.copy(dst, bank(k % 2)[0:dst.shape[0], 0:dst.shape[1]]).then_inc(m_b01_ev, 1)

                for q in range(NQ):
                    evacuate(q, xt0[0:D, q * BANK:(q + 1) * BANK])
                for r in range(SIDE // 2):
                    act.wait_ge(m_v_pe, g * (SIDE // 2) + (r + 1))
                    act.copy(vc[:, 2 * r:2 * r + 2, :], bank(2 + r % 2).rearrange("p (a b) -> p a b", a=2)[:, :, 0:NV]).then_inc(m_v_ev, 1)
                act.wait_ge(m_yt_pe, g + 1)
                act.copy(yt[0:64, :, :], bank(4)[0:64, 0:2 * P].rearrange("p (a b) -> p a b", a=2)).then_inc(m_yt_ev, 1)
                for m in range(2):
                    act.wait_ge(m_sub, g * 2 + (m + 1))
                    act.activation(at[:, m, :, :], sc[:, :, :], ACT.Exp).then_inc(m_exp, 1)
                for q in range(NQ):
                    evacuate(NQ + q, oh[:, Q * q:Q * q + Q, :].rearrange("p a b -> p (a b)"))

            def ffn(f):
                act.sem_inc(f["xt_ev"], 1)
                act.sem_inc(f["gelu"], 2)
                act.sem_inc(f["y_ev"], 2)
                with act.Fori(0, NT) as t:
                    act.wait_ge(f["xt_pe"], t + 1)
                    act.copy(xt4[0:D, :], bank(4)[0:D, :]).then_inc(f["xt_ev"], 1)

                    def y_out(e):
                        act.wait_ge(f["mm2"], t * NC + (3 + CPE * (e + 1)))
                        act.wait_ge(f["yt_pe"], t * NEXP + (e + 1))
                        act.activation(yte[0:D, e % 2, :], bank(2 + e % 2)[0:D, :], ACT.Identity, bias=b2[:, e:e + 1]).then_inc(f["y_ev"], 1)

                    for c in range(NC):
                        act.wait_ge(f["mm1"], t * NC + (c + 1))
                        act.wait_ge(f["mm2"], t * NC + (c + 1))
                        act.activation(hid[:, c % 3, :], bank(c % 2), ACT.Gelu).then_inc(f["gelu"], 1)
                        if c == 1:
                            act.wait_ge(f["gate_d"], t + 1)
                            act.activation(gth[:, :, :], gd[:, :, :], ACT.Tanh, scale=0.5).then_inc(f["tanh"], 1)
                        if c % CPE == 0 and c:
                            y_out(c // CPE - 1)
                    y_out(NEXP - 1)

            if stop >= 2:
                act.wait_ge(stage_end, 1)
                act.wait_ge(ffn_in, 16 * 6)
                ffn(ffn_sems[0])
            if stop >= 3:
                act.wait_ge(ssm_in, 16 * 11)
                act.activation(sp[:, 0, 0:NH], neg_a[:, :], ACT.Exp).then_inc(act_chain, 1)
                act.sem_inc(s["b0_ev"], 1)
                act.sem_inc(s["l"], 2)
                act.wait_ge(prep_done, 2)
                with act.Fori(0, G) as g:
                    n0 = [0]

                    def bank0():
                        n0[0] += 1
                        act.wait_ge(s["b0_pe"], g * (3 * NQ) + n0[0])

                    def spread(q):
                        bank0()
                        src = bank(0)[0:D, :].rearrange("p (a w) -> p a w", w=SIDE)
                        for n in range(3):
                            dst = x3[0:D, n, q % 4, :, :].rearrange("p a (b w) -> p (a b) w", w=SIDE)
                            a, b = [(slice(0, SIDE), slice(0, SIDE)), (slice(1, SIDE), slice(0, SIDE - 1)), (slice(0, SIDE - 1), slice(1, SIDE))][n]
                            i = act.copy(dst[:, :, a], src[:, :, b])
                        i.then_inc(s["b0_ev"], 1)

                    def conv_tanh(h):
                        act.wait_ge(s["cv"], g * SIDE + (h + 1))
                        if h >= 1:
                            act.wait_ge(s["cv_ev"], g * SIDE + h)
                        act.activation(th[:, 0:CONV], bank(1 + h % 2)[:, 0:CONV], ACT.Tanh).then_inc(s["cv_th"], 1)

                    def decays(q):
                        act.wait_ge(s["cs"], g * NQ + (q + 1))
                        act.activation(ex3[:, :, :, :].rearrange("p a b c -> p (a b c)"), bank(7)[:, 0:3 * Q * NH], ACT.Exp).then_inc(s["ex"], 1)

                    def pair_decay(h):
                        act.wait_ge(s["d_pe"], g * SIDE + (h + 1))
                        act.activation(ll[:, h % 2, :, :].rearrange("p a b -> p (a b)"), bank(4)[:, 0:NH * SIDE], ACT.Exp).then_inc(s["l"], 1)

                    spread(0)
                    spread(1)
                    for q in range(NQ + 2):
                        c = q - 1
                        if q < NQ:
                            conv_tanh(Q * q)
                        if 0 <= c < NQ:
                            decays(c)
                            pair_decay(Q * c)
                        if q < NQ:
                            conv_tanh(Q * q + 1)
                        if q >= 2:
                            for n in range(2):
                                bank0()
                                act.activation(g4[0:D, n, :], bank(0)[0:D, :], ACT.Identity, bias=beta[0:D, n:n + 1], scale=gamma[0:D, n:n + 1]).then_inc(s["b0_ev"], 1)
                        if 0 <= c < NQ:
                            pair_decay(Q * c + 1)
                        if q < NQ:
                            conv_tanh(Q * q + 2)
                        if q + 2 < NQ:
                            spread(q + 2)
                        if 0 <= c < NQ:
                            pair_decay(Q * c + 2)
                        if q < NQ:
                            conv_tanh(Q * q + 3)
                        if 0 <= c < NQ:
                            pair_decay(Q * c + 3)
                        if q < NQ:
                            for n in range(2):
                                act.wait_ge(s["z_pe"], g * (2 * NQ) + (2 * q + n + 1))
                                if q or n:
                                    act.wait_ge(s["z_ev"], g * (2 * NQ) + (2 * q + n))
                                act.activation(thz[0:D, :], bank(3)[0:D, :], ACT.Tanh).then_inc(s["z_th"], 1)
                            act.wait_ge(s["raw"], g * NQ + (q + 1))
                            act.activation(sp[:, 1, :], sp[:, 0, :], ACT.Exp, scale=-1.0).then_inc(s["exp_dt"], 1)
            if stop >= 4:
                act.wait_ge(stage_end, 3)
                act.wait_ge(ffn_in, 16 * 12)
                ffn(ffn_sems[1])

        @block.tensor
        def _(pe):
            pe.wait_ge(const_in, 16)
            pe.wait_ge(mix_in, 16 * 23)

            held = [0]

            def apart():
                pe.sem_inc(waited, 1)
                held[0] += 1

            pe.matmul(bank(5)[0:D + 1, 0:D], wc[0:D, 0:D + 1], wo_t[0:D, :], start=True, stop=True).then_inc(prep_pe, 1)
            pe.wait_ge(prep_done, 1)
            with pe.Fori(0, G) as g:
                def bank01(k):
                    pe.wait_ge(m_b01_ev, g * (2 * NQ) + (k + 1))

                for q in range(NQ):
                    pe.wait_ge(m_ln, g * NQ + (q + 1))
                    bank01(q)
                    for i in range(Q):
                        ins = pe.transpose(bank(q % 2)[0:D, i * P:(i + 1) * P], xn[:, Q * q + i, :], ident)
                    ins.then_inc(m_b01_pe, 1)
                pe.wait_ge(m_w_add, g * NQ + NQ)
                for r in range(SIDE // 2):
                    if r % 2 == 0:
                        pe.wait_ge(m_b01_ev, g * (2 * NQ) + (2 + r // 2 + 1))
                    if r >= 2:
                        pe.wait_ge(m_v_ev, g * (SIDE // 2) + (r - 1))
                    for i in range(2):
                        h = 2 * r + i
                        ins = pe.matmul(bank(2 + r % 2)[:, i * 256:i * 256 + NV], xt0[0:D + 1, h * P:(h + 1) * P], rhs0[0:D + 1, :], start=True, stop=True)
                    ins.then_inc(m_v_pe, 1)
                pe.wait_ge(m_yb, g + 1)
                apart()
                for m, src in enumerate((yb[:, 0, :], ywt)):
                    ins = pe.transpose(bank(4)[0:64, m * P:(m + 1) * P], src, ident)
                ins.then_inc(m_yt_pe, 1)
                pe.wait_ge(m_yt_ev, g + 1)
                for m in range(2):
                    for n in range(2):
                        ins = pe.matmul(bank(6 - 2 * m + n), yt[0:65, m, :], w2z[0:65, m, n * BANK:(n + 1) * BANK], start=True, stop=True)
                    ins.then_inc(m_z_pe, 1)
                for m in range(2):
                    pe.wait_ge(m_at, g * 2 + (m + 1))
                    for q in range(NQ):
                        if m == 0:
                            bank01(NQ + q)
                        elif q >= 2:
                            pe.wait_ge(m_w_add, g * NQ + (NQ + q - 1))
                        apart()
                        for i in range(Q):
                            w = Q * q + i
                            for b in range(PACK):
                                pb = slice(b * SIDE, (b + 1) * SIDE)
                                val = vh[pb, w, :] if m == 0 else vc[pb, w, 0:D]
                                ins = pe.matmul(bank(2 * m + q % 2)[pb, i * D:(i + 1) * D], at[pb, m, :, w], val, start=True, stop=True)
                        ins.then_inc(m_b01_pe if m == 0 else m_w_pe, 1)

            def ffn(f):
                pe.sem_inc(f["mm2"], 3)
                pe.sem_inc(f["yt_pe"], 2)

                def x_in_columns(t):
                    pe.wait_ge(f["ln"], t + 1)
                    pe.wait_ge(f["xt_ev"], t + 1)
                    for i in range(Q):
                        ins = pe.transpose(bank(4)[0:D, i * P:(i + 1) * P], xn4[:, i, :], ident)
                    ins.then_inc(f["xt_pe"], 1)

                def y_in_rows(t, e):
                    pe.wait_ge(f["y_ev"], t * NEXP + (e + 3))
                    pe.wait_ge(f["comb"], t * NEXP + (e + 1))
                    for i in range(Q):
                        ins = pe.transpose(bank(6 + e % 2)[:, i * D:(i + 1) * D], yte[0:D, e % 2, i * P:(i + 1) * P], ident[0:D, 0:D])
                    ins.then_inc(f["yt_pe"], 1)

                def up(t, c):
                    pe.wait_ge(f["gelu"], t * NC + (c + 1))
                    pe.matmul(bank(c % 2), w1[:, c * P:(c + 1) * P], xt4[0:D + 1, :], start=True, stop=True).then_inc(f["mm1"], 1)

                def down(t, c):
                    e = c // CPE
                    if c % CPE == 0:
                        pe.wait_ge(f["y_ev"], t * NEXP + (e + 1))
                    pe.wait_ge(f["gelu"], t * NC + (c + 3))
                    pe.matmul(bank(2 + e % 2)[0:D, :], w2[:, c, :], hid[:, c % 3, :], start=(c % CPE == 0), stop=(c % CPE == CPE - 1)).then_inc(f["mm2"], 1)

                def tile(t, first):
                    if first:
                        x_in_columns(t)
                    pe.wait_ge(f["xt_ev"], t + 2)
                    for i in range(Q):
                        ins = pe.matmul(bank(5)[:, i * NEXP:(i + 1) * NEXP], xt4[0:D + 1, i * P:(i + 1) * P], gw[:, :], start=True, stop=True)
                    ins.then_inc(f["gate_pe"], 1)
                    for c in range(NC + 1):
                        if c < NC:
                            up(t, c)
                        if c == 0 and not first:
                            y_in_rows(t - 1, NEXP - 1)
                        if c:
                            down(t, c - 1)
                        if c in (5, 8, 11):
                            y_in_rows(t, c // CPE - 1)
                        if c == 10:
                            yield
                    return

                def run(t, first, last):
                    for _ in tile(t, first):
                        if not last:
                            x_in_columns(t + 1)

                run(0, True, False)
                with pe.Fori(1, NT - 1) as t:
                    run(t, False, False)
                run(NT - 1, False, True)
                y_in_rows(NT - 1, NEXP - 1)

            if stop >= 2:
                pe.wait_ge(stage_end, 1)
                pe.wait_ge(ffn_in, 16 * 6)
                ffn(ffn_sems[0])
            if stop >= 3:
                pe.wait_ge(prep_done, 2)
                with pe.Fori(0, G) as g:
                    n0 = [0]

                    def bank0():
                        n0[0] += 1
                        pe.wait_ge(s["b0_ev"], g * (3 * NQ) + n0[0])
                        return n0[0]

                    evac = {}

                    def to_columns(q):
                        pe.wait_ge(s["ln"], g * NQ + (q + 1))
                        evac[q] = bank0() + 1
                        for i in range(Q):
                            ins = pe.transpose(bank(0)[0:D, i * P:(i + 1) * P], xn[:, Q * q + i, :], ident)
                        ins.then_inc(s["b0_pe"], 1)

                    def conv(h):
                        if h % Q == 0:
                            pe.wait_ge(s["b0_ev"], g * (3 * NQ) + evac[min(h // Q + 1, NQ - 1)])
                        if h >= 2:
                            pe.wait_ge(s["cv_ev"], g * SIDE + (h - 1))
                        taps = [(0, 0)] + [(y, x) for y in (-1, 0, 1) for x in (-1, 0, 1) if (x or y) and 0 <= h + y < SIDE]
                        for n, (y, x) in enumerate(taps):
                            src = x3[:, {0: 0, -1: 1, 1: 2}[x], (h + y) // Q % 4, (h + y) % Q, :]
                            t = 3 * (y + 1) + x + 1
                            k = D + 1 if n == 0 else D
                            c = CONV + NH if n == 0 else CONV
                            ins = pe.matmul(bank(1 + h % 2)[:, 0:c], src[0:k, :], wtap[0:k, t, 0:c], start=(n == 0), stop=(n == len(taps) - 1))
                        ins.then_inc(s["cv"], 1)

                    def z_columns(q):
                        for n in range(2):
                            if q or n:
                                pe.wait_ge(s["z_ev"], g * (2 * NQ) + (2 * q + n))
                            pe.matmul(bank(3)[0:D, :], wz[0:D, n, :], x3[0:D, 0, q % 4, :, :].rearrange("p a b -> p (a b)"), start=True, stop=True).then_inc(s["z_pe"], 1)

                    def sums(q):
                        pe.wait_ge(s["a"], g * NQ + (q + 1))
                        a = av[:, q % 2, :, :].rearrange("p a b -> p (a b)")
                        for n, w in enumerate((upto, later, whole)):
                            ins = pe.matmul(bank(7)[:, n * Q * NH:(n + 1) * Q * NH], w, a, start=True, stop=True)
                        ins.then_inc(s["cs"], 1)

                    def pairs(h):
                        q, i = divmod(h, Q)
                        pe.wait_ge(s["r"], g * SIDE + (h + 1))
                        pe.wait_ge(s["l"], g * SIDE + (h + 2))
                        pe.matmul(bank(4)[:, 0:NH * SIDE], later, rr[:, i, :, :].rearrange("p a b -> p (a b)"), start=True, stop=True).then_inc(s["d_pe"], 1)
                        if i == 0:
                            pe.wait_ge(s["bt"], g * NQ + (q + 1))
                        pe.wait_ge(s["state"], g * (SIDE + 1) + (h + 1))
                        apart()
                        for b in range(PACK):
                            pb = slice(b * SIDE, b * SIDE + NS)
                            ins = pe.matmul(bank(6)[b * SIDE:(b + 1) * SIDE, 0:SIDE], bt[pb, i, :], ct[pb, i, :], start=True, stop=True)
                        ins.then_inc(s["g_pe"], 1)

                    def scan(h):
                        q, i = divmod(h, Q)
                        if i == 0:
                            pe.wait_ge(s["xdt"], g * NQ + (q + 1))
                            pe.wait_ge(s["xw"], g * NQ + (q + 1))
                        if h:
                            pe.wait_ge(s["y"], g * SIDE + h)
                        pe.wait_ge(s["m"], g * SIDE + (h + 1))
                        apart()
                        for b in range(PACK):
                            pb = slice(b * SIDE, b * SIDE + NS)
                            pe.matmul(bank(5)[b * SIDE:(b + 1) * SIDE, INNER:2 * INNER], ct[pb, i, :], st[pb, :, :].rearrange("p a b -> p (a b)"), start=True, stop=True)
                        for n in range(NH):
                            for b in range(PACK):
                                pb = slice(b * SIDE, (b + 1) * SIDE)
                                ins = pe.matmul(bank(5)[pb, n * HD:(n + 1) * HD], mm[pb, h % 2, n, :], xdt[pb, i, n, :], start=True, stop=True)
                        ins.then_inc(s["y_pe"], 1)
                        for b in range(PACK):
                            pb = slice(b * SIDE, (b + 1) * SIDE)
                            ins = pe.matmul(bank(6)[pb, 128:128 + INNER], xbc[pb, q % 2, i, INNER:INNER + 2 * NS], xw[pb, i, :, :].rearrange("p a b -> p (a b)"), start=True, stop=True)
                        ins.then_inc(s["ds_pe"], 1)

                    def u_columns(q):
                        pe.wait_ge(s["u"], g * NQ + (q + 1))
                        for n in range(2):
                            bank0()
                            for i in range(Q):
                                ins = pe.transpose(bank(0)[0:D, i * P:(i + 1) * P], u4[:, i, n * D:(n + 1) * D], ident)
                            ins.then_inc(s["b0_pe"], 1)

                    def project(q, y_before):
                        pe.wait_ge(s["gate"], g * NQ + (q + 1))
                        if y_before:
                            pe.wait_ge(s["y"], g * SIDE + y_before)
                        for i in range(Q):
                            for n in range(2):
                                ins = pe.matmul(bank(5)[:, i * D:(i + 1) * D], g4[0:D, n, i * P:(i + 1) * P], wout[0:D, n, :], start=(n == 0), stop=(n == 1))
                        ins.then_inc(s["o_pe"], 1)

                    to_columns(0)
                    to_columns(1)
                    for q in range(NQ + 2):
                        c = q - 1
                        here, back, gone = q < NQ, 0 <= c < NQ, q >= 2
                        if here:
                            conv(Q * q)
                        if back:
                            sums(c)
                            pairs(Q * c)
                        if here:
                            conv(Q * q + 1)
                        if gone:
                            u_columns(q - 2)
                        if back:
                            scan(Q * c)
                            pairs(Q * c + 1)
                        if here:
                            conv(Q * q + 2)
                        if q + 2 < NQ:
                            to_columns(q + 2)
                        if back:
                            scan(Q * c + 1)
                            pairs(Q * c + 2)
                        if gone:
                            project(q - 2, min(Q * c + 2, SIDE))
                        if here:
                            conv(Q * q + 3)
                        if back:
                            if gone:
                                pe.wait_ge(s["o_add"], g * NQ + (q - 1))
                            scan(Q * c + 2)
                            pairs(Q * c + 3)
                        if here:
                            z_columns(q)
                        if back:
                            scan(Q * c + 3)
            if stop >= 4:
                pe.wait_ge(stage_end, 3)
                pe.wait_ge(ffn_in, 16 * 12)
                ffn(ffn_sems[1])
            pe.wait_ge(waited, G * held[0])

        def mixer1(dve, ch):
            dve.wait_ge(ssm_in, 16 * 11)
            dve.wait_ge(act_chain, 1)
            ch.done(dve.tensor_scalar(neg_a, sp[:, 0, 0:NH], -1.0, None, ALU.mult))
            ch.done(dve.tensor_scalar(wz[0:D, :, :], wz[0:D, :, :], 0.5, None, ALU.mult))
            ch.done(dve.tensor_scalar(wtap[D:D + 1, CENTRE, 0:CONV], wtap[D:D + 1, CENTRE, 0:CONV], 0.5, None, ALU.mult))
            for t in range(TAPS):
                ch.done(dve.scalar_tensor_tensor(wtap[0:D, t, 0:CONV], winx[0:D, :], 0.5, wcv[0:D, t, :], ALU.mult, ALU.mult))
            ch.wait()
            dve.wait_ge(ones_set, 2)
            dve.sem_inc(prep_done, 1)
            with dve.Fori(0, G) as g:
                ch.enter(g, SSMC)
                ln = g * (NQ + 1) + LN_MIX1
                layer_norm(dve, ch, lambda r: xr[:, g, r, :], lambda r: xn[:, r, :], SIDE, D, 1e-6, ln + 1, s["ln"])
                dve.memset(st[:, :, :], 0.0).then_inc(s["state"], 1)

                def conv_silu(h):
                    q, i = divmod(h, Q)
                    b = bank(1 + h % 2)
                    dve.wait_ge(s["cv_th"], g * SIDE + (h + 1))
                    ch.done(dve.tensor_copy(dtr[:, q % 2, i, :], b[:, CONV:CONV + NH]))
                    dve.scalar_tensor_tensor(xbc[:, q % 2, i, 0:CONV], th[:, 0:CONV], 1.0, b[:, 0:CONV], ALU.add, ALU.mult).then_inc(s["cv_ev"], 1)

                def weigh(c):
                    dve.wait_ge(s["ex"], g * NQ + (c + 1))
                    dve.tensor_tensor(wdt[:, :, :], dt[:, c % 2, :, :], ex3[:, 1, :, :], ALU.mult).then_inc(s["w"], 1)

                def attend(h):
                    dve.wait_ge(s["g_pe"], g * SIDE + (h + 1))
                    ch.link(dve.tensor_tensor(gmk, bank(6)[:, 0:SIDE], tri, ALU.mult))
                    dve.wait_ge(s["l"], g * SIDE + (h + 3))
                    dve.tensor_tensor(mm[:, h % 2, :, :], ll[:, h % 2, :, :], gmk.unsqueeze(1).to_broadcast([P, NH, SIDE]), ALU.mult).then_inc(s["m"], 1)

                def gather(h):
                    c, i = divmod(h, Q)
                    y = yy[:, c % 2, i, :].rearrange("p (h e) -> p h e", e=HD)
                    heads = bank(5)[:, 0:2 * INNER].rearrange("p (a h e) -> p a h e", a=2, e=HD)
                    dve.wait_ge(s["y_pe"], g * SIDE + (h + 1))
                    ch.link(dve.tensor_tensor(y, heads[:, 1], ex3[:, 0, i, :].unsqueeze(2).to_broadcast([P, NH, HD]), ALU.mult))
                    dve.tensor_tensor(y, y, heads[:, 0], ALU.add).then_inc(s["y"], 1)
                    if i == 0:
                        dve.wait_ge(s["xd"], g * NQ + (c + 1))
                    dve.wait_ge(s["y"], g * SIDE + (h + 1))
                    ch.done(dve.tensor_tensor(y, y, xd[:, i, :, :], ALU.add))
                    dve.wait_ge(s["s1"], g * SIDE + (h + 1))
                    dve.wait_ge(s["ds_pe"], g * SIDE + (h + 1))
                    dve.tensor_tensor(st[:, :, :], st1[:, :, :], bank(6)[:, 128:128 + INNER].rearrange("p (h e) -> p h e", e=HD), ALU.add).then_inc(s["state"], 1)

                def steps_of(q):
                    flat = lambda a: a.rearrange("p a b -> p (a b)")
                    x = flat(dtr[:, q % 2, :, :])
                    ch.wait()
                    dve.scalar_tensor_tensor(sp[:, 0, :], x, -1.0, x, ALU.mult, ALU.max).then_inc(s["raw"], 1)
                    ch.done(dve.tensor_scalar(sp[:, 5, :], x, 0.0, None, ALU.max))
                    dve.wait_ge(s["exp_dt"], g * NQ + (q + 1))
                    u, r, r2, p = sp[:, 1, :], sp[:, 2, :], sp[:, 3, :], sp[:, 4, :]
                    ch.link(dve.tensor_scalar(r, u, 2.0, None, ALU.add))
                    ch.link(dve.reciprocal(r, r))
                    ch.link(dve.tensor_tensor(r, r, u, ALU.mult))
                    ch.link(dve.tensor_tensor(r2, r, r, ALU.mult))
                    ch.link(dve.tensor_scalar(p, r2, 1.0 / 15, None, ALU.mult))
                    for k in (13, 11, 9, 7, 5, 3):
                        ch.link(dve.scalar_tensor_tensor(p, p, 1.0 / k, r2, ALU.add, ALU.mult))
                    ch.link(dve.scalar_tensor_tensor(p, p, 1.0, r, ALU.add, ALU.mult))
                    ch.link(dve.scalar_tensor_tensor(flat(dt[:, q % 2, :, :]), p, 2.0, sp[:, 5, :], ALU.mult, ALU.add))
                    dve.tensor_tensor(av[:, q % 2, :, :], dt[:, q % 2, :, :], neg_a.unsqueeze(1).to_broadcast([P, Q, NH]), ALU.mult).then_inc(s["a"], 1)
                    dve.wait_ge(s["cv_ev"], g * SIDE + (Q * q + Q))
                    ch.done(dve.transpose(bt[:, :, :], xbc[:, q % 2, :, INNER:INNER + SIDE]))
                    dve.transpose(ct[:, :, :], xbc[:, q % 2, :, INNER + NS:INNER + NS + SIDE]).then_inc(s["bt"], 1)

                for q in range(NQ + 2):
                    c = q - 1
                    here, back, gone = q < NQ, 0 <= c < NQ, q >= 2
                    if gone:
                        ch.wait()
                        layer_norm(dve, ch, lambda r: yy[:, q % 2, r, :], lambda r: u4[:, r, :], Q, INNER, 1e-5, ln + q, s["u"])
                    if here:
                        conv_silu(Q * q)
                    if back:
                        weigh(c)
                        attend(Q * c)
                    if here:
                        conv_silu(Q * q + 1)
                    if gone:
                        dve.wait_ge(s["b0_ev"], g * (3 * NQ) + (BANK0.index(f"U{q - 2}") + 3))
                        ch.done(dve.tensor_tensor(g4[0:D, 0, :], g4[0:D, 0, :], szt[0:D, q % 2, 0, :], ALU.mult))
                        dve.tensor_tensor(g4[0:D, 1, :], g4[0:D, 1, :], szt[0:D, q % 2, 1, :], ALU.mult).then_inc(s["gate"], 1)
                    if back:
                        gather(Q * c)
                        attend(Q * c + 1)
                    if here:
                        conv_silu(Q * q + 2)
                    if back:
                        gather(Q * c + 1)
                        attend(Q * c + 2)
                    if gone:
                        dve.wait_ge(s["o_pe"], g * NQ + (q - 1))
                        rows = xr[:, g, Q * (q - 2):Q * (q - 1), :]
                        dve.tensor_tensor(rows, rows, bank(5)[:, 0:Q * D].rearrange("p (a b) -> p a b", b=D), ALU.add).then_inc(s["o_add"], 1)
                    if here:
                        conv_silu(Q * q + 3)
                    if back:
                        gather(Q * c + 2)
                        attend(Q * c + 3)
                    if here:
                        for n in range(2):
                            dve.wait_ge(s["z_th"], g * (2 * NQ) + (2 * q + n + 1))
                            dve.scalar_tensor_tensor(szt[0:D, q % 2, n, :], thz[0:D, :], 1.0, bank(3)[0:D, :], ALU.add, ALU.mult).then_inc(s["z_ev"], 1)
                    if back:
                        gather(Q * c + 3)
                    if here:
                        steps_of(q)
                ch.leave(G, SSMC)
            dve.wait_ge(s["o_add"], G * NQ)

        @block.vector
        def _(dve):
            ch = Chain(dve, dve_chain)
            ch.done(dve.memset(xt0[D:D + 1, :], 1.0))
            ch.done(dve.memset(rhs0[D:D + 1, 0:D], 0.0))
            dve.wait_ge(mix_in, 16 * 23)
            ch.done(dve.tensor_copy(rhs0[0:D, 0:D], wo_t[0:D, :]))
            dve.wait_ge(prep_pe, 1)
            ch.done(dve.tensor_copy(rhs0[0:D, D:2 * D], bank(5)[0:D, 0:D]))
            ch.wait()
            dve.tensor_tensor(rhs0[D:D + 1, D:2 * D], bank(5)[D:D + 1, 0:D], bo[D:D + 1, :], ALU.add).then_inc(prep_done, 1)
            dve.sem_inc(m_w_add, NQ)
            with dve.Fori(0, G) as g:
                ch.enter(g, MIXC)
                dve.wait_ge(x_in, g * 64 + 64)
                layer_norm(dve, ch, lambda r: xr[:, g, r, :], lambda r: xn[:, r, :], SIDE, D, 1e-6, g + 1, m_ln)
                dve.wait_ge(m_v_ev, g * (SIDE // 2) + SIDE // 2)
                ch.done(dve.tensor_copy(yb[:, 0, :].rearrange("p (e h) -> p e h", e=2), vc[:, :, 2 * D:2 * D + 2].rearrange("p h e -> p e h")))
                ch.link(dve.tensor_copy(yb[:, 1, :].rearrange("p (e h) -> p e h", e=2), vc[:, :, 2 * D + 2:NV].rearrange("p h e -> p e h")))
                dve.transpose(ywt, yb[:, 1, :]).then_inc(m_yb, 1)
                ch.done(dve.transpose(vh[:, :, :].rearrange("p w d -> p d w"), vc[:, :, 0:D].rearrange("p h d -> p d h")))
                ch.done(dve.tensor_tensor(xr[:, g, :, :], xr[:, g, :, :], vc[:, :, D:2 * D], ALU.add))
                for m in range(2):
                    z = bank(6 - 2 * m, 2).rearrange("p (i j) -> p i j", j=SIDE)
                    dve.wait_ge(m_z_pe, g * 2 + (m + 1))
                    ch.link(dve.tensor_reduce(row_max, z, AX.X, ALU.max))
                    dve.tensor_tensor(sc[:, :, :], z, row_max.unsqueeze(2).to_broadcast([P, SIDE, SIDE]), ALU.subtract).then_inc(m_sub, 1)
                    dve.wait_ge(m_exp, g * 2 + (m + 1))
                    ch.link(dve.tensor_reduce(row_sum, at[:, m, :, :], AX.X, ALU.add))
                    ch.link(dve.reciprocal(row_inv, row_sum))
                    ch.link(dve.tensor_tensor(sc[:, :, :], at[:, m, :, :], row_inv.unsqueeze(2).to_broadcast([P, SIDE, SIDE]), ALU.mult))
                    dve.transpose(at[:, m, :, :], sc[:, :, :]).then_inc(m_at, 1)
                ch.wait()
                for q in range(NQ):
                    dve.wait_ge(m_w_pe, g * NQ + (q + 1))
                    rows = xr[:, g, Q * q:Q * q + Q, :]
                    dve.tensor_tensor(rows, rows, bank(2 + q % 2)[:, 0:Q * D].rearrange("p (a b) -> p a b", b=D), ALU.add).then_inc(m_w_add, 1)
                dve.wait_ge(m_w_add, g * NQ + 2 * NQ)
                dve.wait_ge(m_b01_ev, g * (2 * NQ) + (2 + 2 * NQ))
                ch.link(dve.transpose(ohw[:, :, :].rearrange("p h d -> p d h"), oh[:, :, :].rearrange("p w d -> p d w")))
                ch.link(dve.tensor_tensor(xr[:, g, :, :], xr[:, g, :, :], ohw[:, :, :], ALU.add))
                ch.leave(G, MIXC)

            def ffn(f, ln_before):
                dve.sem_inc(f["comb"], 2)

                def norm(t):
                    layer_norm(dve, ch, lambda r: xt_rows(t)[:, r, :], lambda r: xn4[:, r, :], Q, D, 1e-5, t + (ln_before + 1), f["ln"])

                def xt_rows(t):
                    return xr[:, :, :, :].rearrange("p g h d -> p (g h) d").rearrange("p (t q) d -> p t q d", q=Q)[:, t, :, :]

                def combine(t, e):
                    dve.wait_ge(f["yt_pe"], t * NEXP + (e + 3))
                    dve.wait_ge(f["comb"], t * NEXP + (e + 2))
                    for i in range(Q):
                        row = xt_rows(t)[:, i, :]
                        ins = dve.scalar_tensor_tensor(row, bank(6 + e % 2)[:, i * D:(i + 1) * D], gm[:, i, e:e + 1], row, ALU.mult, ALU.add)
                    ins.then_inc(f["comb"], 1)

                def gate(t):
                    sco = bank(5)[:, 0:Q * NEXP].rearrange("p (a b) -> p a b", b=NEXP)

                    def over(a):
                        return a.unsqueeze(2).to_broadcast([P, Q, NEXP])

                    dve.wait_ge(f["gate_pe"], t + 1)
                    ch.link(dve.tensor_reduce(gcol[:, 0, :], sco, AX.X, ALU.max))
                    dve.tensor_tensor(gd[:, :, :], sco, over(gcol[:, 0, :]), ALU.subtract).then_inc(f["gate_d"], 1)
                    dve.wait_ge(f["gate_d"], t + 1)
                    other = gd[:, :, :].unsqueeze(2).to_broadcast([P, Q, NEXP, NEXP])
                    own = gd[:, :, :].unsqueeze(3).to_broadcast([P, Q, NEXP, NEXP])
                    ch.done(dve.tensor_tensor(gcmp[:, :, :, :], other, own, ALU.is_gt))
                    ch.link(dve.tensor_tensor(geq[:, :, :, :], other, own, ALU.is_equal))
                    ch.link(dve.tensor_tensor(geq[:, :, :, :], geq[:, :, :, :], lower.unsqueeze(1).to_broadcast([P, Q, NEXP, NEXP]), ALU.mult))
                    ch.link(dve.tensor_tensor(gcmp[:, :, :, :], gcmp[:, :, :, :], geq[:, :, :, :], ALU.add))
                    ch.link(dve.tensor_reduce(gmask[:, :, :], gcmp[:, :, :, :], AX.X, ALU.add))
                    dve.wait_ge(f["tanh"], t + 1)
                    ch.link(dve.tensor_scalar(gn[:, :, :], gth[:, :, :], -1.0, 1.0, ALU.mult, ALU.add))
                    ch.link(dve.reciprocal(gn[:, :, :], gn[:, :, :]))
                    ch.link(dve.scalar_tensor_tensor(ge[:, :, :], gth[:, :, :], 1.0, gn[:, :, :], ALU.add, ALU.mult))
                    ch.done(dve.tensor_reduce(gcol[:, 1, :], ge[:, :, :], AX.X, ALU.add))
                    ch.link(dve.scalar_tensor_tensor(gn[:, :, :], gmask[:, :, :], 2.0, ge[:, :, :], ALU.is_lt, ALU.mult))
                    ch.link(dve.tensor_reduce(gcol[:, 2, :], gn[:, :, :], AX.X, ALU.add))
                    ch.link(dve.scalar_tensor_tensor(gcol[:, 3, :], gcol[:, 1, :], 1e-9, gcol[:, 2, :], ALU.mult, ALU.add))
                    ch.link(dve.reciprocal(gcol[:, 0, :], gcol[:, 3, :]))
                    ch.link(dve.tensor_tensor(gm[:, :, :], gn[:, :, :], over(gcol[:, 0, :]), ALU.mult))

                def tile(t, first, last):
                    if not first:
                        combine(t - 1, NEXP - 1)
                        dve.wait_ge(f["comb"], t * NEXP + 2)
                    gate(t)
                    if not last:
                        dve.wait_ge(f["xt_pe"], t + 1)
                        norm(t + 1)
                    for e in range(NEXP - 1):
                        combine(t, e)

                dve.wait_ge(stage_end, 1 if ln_before == LN_FFN0 else 3)
                ch.link(dve.memset(xt4[D:D + 1, :], 1.0))
                norm(0)
                tile(0, True, False)
                per = FFNC
                with dve.Fori(1, NT - 1) as t:
                    ch.enter(t - 1, per)
                    tile(t, False, False)
                    ch.leave(NT - 2, per)
                tile(NT - 1, False, True)
                combine(NT - 1, NEXP - 1)
                dve.wait_ge(f["comb"], NT * NEXP + 2)

            dve.sem_inc(stage_end, 1)
            if stop >= 2:
                ffn(ffn_sems[0], LN_FFN0)
                dve.sem_inc(stage_end, 1)
            if stop >= 3:
                mixer1(dve, ch)
                dve.sem_inc(stage_end, 1)
            if stop >= 4:
                ffn(ffn_sems[1], LN_FFN1)
                dve.sem_inc(stage_end, 1)


_INPUTS = ["consts", "x", "Wc", "bc", "WoT", "bo", "W1T", "W2T", "b2z", "Win_z", "Win_dt", "dt_bias", "Win_x", "b_conv",
           "W_conv", "A_log", "D_param", "gamma", "beta", "W_out"]
_FFN = ["w1", "b1", "w2", "b2T", "gate_w", "gate_b"]


def kernel(**inputs):
    import numpy as np
    import concourse.bacc as bacc
    from concourse.bass_utils import run_bass_kernel_spmd

    a = {k: np.asarray(v) for k, v in inputs.items()}
    k, l = np.arange(P)[:, None], np.arange(P)[None, :]
    one = k // SIDE == l // SIDE
    e, o = np.arange(NEXP)[:, None], np.arange(NEXP)[None, :]
    consts = np.concatenate([k == l, one & (k <= l), one & (k > l), one, k % SIDE <= np.arange(SIDE)[None, :],
                             np.broadcast_to((o < e).reshape(1, 16), (P, 16))], axis=1).astype(np.float32)

    def mixing(w):
        return w.reshape(SEG, P, SEG).transpose(0, 2, 1)

    w_in = a["L1_conv_W_in"]
    arrays = {
        "consts": consts, "x": a["x"], "Wc": a["L0_conv_Wc"], "bc": a["L0_conv_bc"].reshape(D, 1),
        "WoT": a["L0_conv_Wo"].T, "bo": a["L0_conv_bo"].reshape(1, D),
        "W1T": np.concatenate([np.concatenate([a["L0_conv_W1h"].T, a["L0_conv_W1w"].T], 1),
                               np.concatenate([a["L0_conv_b1h"], a["L0_conv_b1w"]]).reshape(1, 2 * E0)], 0),
        "W2T": np.stack([mixing(a["L0_conv_W2h"]), mixing(a["L0_conv_W2w"])]),
        "b2z": np.stack([a["L0_conv_b2h"], a["L0_conv_b2w"]]).reshape(2, 1, SIDE * SIDE),
        "Win_z": w_in[:, :INNER].reshape(D, 2, D), "Win_x": w_in[:, INNER:INNER + CONV], "Win_dt": w_in[:, INNER + CONV:],
        "dt_bias": a["L1_conv_dt_bias"].reshape(1, NH), "b_conv": a["L1_conv_b_conv"].reshape(1, CONV),
        "W_conv": a["L1_conv_W_conv"].reshape(TAPS, CONV), "A_log": a["L1_conv_A_log"], "D_param": a["L1_conv_D_param"],
        "gamma": a["L1_conv_gamma"].reshape(2, D).T, "beta": a["L1_conv_beta"].reshape(2, D).T,
        "W_out": a["L1_conv_W_out"].reshape(2, D, D).transpose(1, 0, 2),
    }
    for n in range(2):
        w = {x: a[f"L{n}_ffn_{x}"] for x in ("w1", "b1", "w2", "b2", "gate_w", "gate_b")}
        arrays |= {f"{n}_w1": w["w1"], f"{n}_b1": w["b1"].reshape(1, NEXP * HID), f"{n}_w2": w["w2"], f"{n}_b2T": w["b2"].T,
                   f"{n}_gate_w": w["gate_w"], f"{n}_gate_b": w["gate_b"].reshape(1, NEXP)}
    arrays = {f"in_{x}": np.ascontiguousarray(v) for x, v in arrays.items()}
    nc = bacc.Bacc("TRN2", target_bir_lowering=False, num_devices=1)
    aps = {x: nc.dram_tensor(x, v.shape, mybir.dt.from_np(v.dtype), kind="ExternalInput").ap() for x, v in arrays.items()}
    out = nc.dram_tensor("out", (IMG, SIDE, SIDE, D), F32, kind="ExternalOutput").ap()
    inp = {x: aps[f"in_{x}"] for x in _INPUTS}
    inp["ffn"] = [{x: aps[f"in_{n}_{x}"] for x in _FFN} for n in range(2)]
    metaformer(nc, inp, out)
    r = run_bass_kernel_spmd(nc, [arrays], core_ids=[0])
    return r.results[0]["out"]
```

```python
from contextlib import ExitStack

import concourse.bass as bass
from concourse import mybir

ALU = mybir.AluOpType
ACT = mybir.ActivationFunctionType
AX = mybir.AxisListType
F32 = mybir.dt.float32
F32R = mybir.dt.float32r

P = 128
IMG, SIDE, D = 16, 32, 96
PACK = P // SIDE
G = IMG // PACK
Q = 4
NQ = SIDE // Q
NT = G * NQ
BANK = 512
E0 = 2
SEG = 8
NV = 2 * D + 2 * E0
NEXP, HID = 4, 384
NC = NEXP * HID // P
CPE = HID // P
INNER, NH, HD, NS = 192, 12, 16, 16
CONV = INNER + 2 * NS
XB = CONV + NS
TAPS = 9
CENTRE = TAPS // 2
CONSTS = 4 * P + SIDE + 16
ARENA = 20000
RING = 6
LAG = RING - 1
SPLITS = [0, NC * P, NC * P + NC * D, NC * P + NC * D + 2 * BANK, NC * P + NC * D + (2 + RING) * BANK]
SPLITS.append(SPLITS[-1] + NEXP)
SLOTS = 2
CONVD = CONV + NH
SHIFTS = 3 * SLOTS * Q * P
SPLIT = max(SPLITS[-1], SHIFTS + TAPS * CONVD + INNER)
POOL_CHUNKS = [1, 3, 5, 7, 9, 11]
HEAD, TAIL = 2 * Q, SIDE // 2
MIXC, FFNC, SSMC = 52, 26, 416


def need(eng, sem, count):
    if not isinstance(count, int) or count > 0:
        eng.wait_ge(sem, count)


def tiles(eng, tile):
    tile(0)
    tile(1)
    with eng.Fori(1, NT // 2 - 1) as pair:
        tile(pair * 2, 0)
        tile(pair * 2 + 1, 1)
    tile(NT - 2)
    tile(NT - 1)


class Chain:

    def __init__(self, eng, sem):
        self.eng, self.sem, self.base, self.n = eng, sem, 0, 0

    def done(self, ins):
        ins.then_inc(self.sem, 1)
        self.n += 1

    def wait(self):
        self.eng.wait_ge(self.sem, self.base + self.n)

    def link(self, ins):
        self.done(ins)
        self.wait()

    def enter(self, i, per):
        self.start = self.base + self.n
        self.base, self.n = i * per + self.start, 0

    def leave(self, rounds, per):
        assert self.n == per, (self.n, per)
        self.base, self.n = self.start + rounds * per, 0


def metaformer(nc, inp, out, stop=9):
    with ExitStack() as ctx:
        def sb(name, shape, dt=F32):
            return ctx.enter_context(nc.sbuf_tensor(name, shape, dt))

        def sem(name):
            return ctx.enter_context(nc.semaphore(name))

        ps = ctx.enter_context(nc.psum_tensor("ps", [P, 8, BANK], F32))

        xr = sb("residual", [P, G, SIDE, D])
        consts = sb("consts", [P, CONSTS])
        ident = consts[:, 0:P]
        upto = consts[:, P:2 * P]
        later = consts[:, 2 * P:3 * P]
        whole = consts[:, 3 * P:4 * P]
        tri = consts[:, 4 * P:4 * P + SIDE]
        lower = consts[:, 4 * P + SIDE:CONSTS].rearrange("p (a b) -> p a b", b=NEXP)
        stats = sb("stats", [P, SIDE, 6])
        moments = sb("moments", [P, 6, SIDE])
        stats_y = sb("stats_y", [P, Q, 6])
        moments_y = sb("moments_y", [P, 6, Q])
        half_neg = sb("half_neg", [P, SIDE])
        eps = sb("eps", [P, 2])
        w1 = sb("w1", [D + 1, NC * P])
        w2 = sb("w2", [P, NC, D])
        b2 = sb("b2", [D, NEXP])
        gw = sb("gw", [D + 1, NEXP])
        xn = sb("xn", [P, SIDE, D])
        rounded = sb("rounded", [P, 2, SPLIT], F32R)
        w1r, w2r, xtr, hidr, gwr = (rounded[:, :, a:b] for a, b in zip(SPLITS[:-1], SPLITS[1:]))
        w2r = w2r.rearrange("p s (c d) -> p s c d", d=D)
        hidr = hidr.rearrange("p s (r n) -> p s r n", r=RING)
        xtr = xtr.rearrange("p s (t n) -> p s t n", t=2)
        x3 = rounded[:, :, 0:SHIFTS].rearrange("p s (n k t) -> p s n k t", n=3, k=SLOTS)
        wtap = rounded[:, :, SHIFTS:SHIFTS + TAPS * CONVD].rearrange("p s (t c) -> p s t c", t=TAPS)
        wz = rounded[:, :, SHIFTS + TAPS * CONVD:SHIFTS + TAPS * CONVD + INNER].rearrange("p s (n d) -> p s n d", n=2)
        arena = sb("arena", [P, ARENA])
        top = [0]; tops = []

        def part(*shape):
            n = 1
            for s in shape:
                n *= s
            ap = arena[:, top[0]:top[0] + n]
            top[0] += n
            assert top[0] <= ARENA, top[0]
            names = "abcd"[:len(shape)]
            if len(shape) == 1:
                return ap
            return ap.rearrange(f"p ({' '.join(names)}) -> p {' '.join(names)}", **dict(zip(names[1:], shape[1:])))

        tops.append(top[0]); top[0] = 0
        wc = part(D + 1)
        wo_t = part(D)
        bo = part(D)
        rhs0 = part(NV)
        w2z = part(2, SIDE * SIDE)
        xt0 = part(2 * BANK)
        vc = part(SIDE, NV)
        vh = part(SIDE, D)
        oh = part(SIDE, D)
        yb = part(2, 2 * SIDE)
        ywt = part(2 * SIDE)
        yt = part(2, P)
        row_max = part(SIDE)
        row_sum = part(SIDE)
        row_inv = part(SIDE)
        sc = part(SIDE, SIDE)
        at = part(2, SIDE, SIDE)
        ohw = vh

        tops.append(top[0]); top[0] = 0
        xn4 = part(Q, D)
        hid = part(RING, BANK)
        yte = part(2, BANK)
        gd = part(Q, NEXP)
        gth = part(Q, NEXP)
        gn = part(Q, NEXP)
        ge = part(Q, NEXP)
        gmask = part(Q, NEXP)
        gcmp = part(Q, NEXP, NEXP)
        geq = part(Q, NEXP, NEXP)
        gcol = part(4, Q)
        gm = part(2, Q, NEXP)

        tops.append(top[0]); top[0] = 0
        xbc = part(2, Q, XB)
        after = top[0]
        wz0 = part(2, D)
        winx = part(CONV)
        wcv = part(TAPS, CONV)
        wtap0 = part(TAPS, CONVD)
        a_log = part(NH)
        a_exp = part(NH)
        top[0] = after
        szt = part(2, 2, BANK)
        rr = part(Q, NH, SIDE)
        yy = part(2, Q, INNER)
        dtr = part(2, Q, NH)
        th = part(BANK)
        thz = part(BANK)
        neg_a = part(NH)
        d_par = part(NH)
        gamma = part(2)
        beta = part(2)
        wout = part(2, D)
        sp = part(6, Q * NH)
        dt = part(2, Q, NH)
        av = part(2, Q, NH)
        ex3 = part(2, 3, Q, NH)
        wdt = part(Q, NH)
        ll = part(2, NH, SIDE)
        gmk = part(SIDE)
        mm = part(2, NH, SIDE)
        bt = part(2, Q, SIDE)
        ct = part(2, Q, SIDE)
        xdt = part(2, Q, NH, HD)
        xw = part(2, Q, NH, HD)
        xd = part(2, Q, NH, HD)
        st = part(NH, HD)
        st1 = part(NH, HD)
        u4 = part(Q, INNER)
        g4 = part(2, BANK)

        const_in, mix_in, ffn_in, x_in = sem("const_in"), sem("mix_in"), sem("ffn_in"), sem("x_in")
        ssm_in, x_out = sem("ssm_in"), sem("x_out")
        dve_chain, pool_chain, act_chain = sem("dve_chain"), sem("pool_chain"), sem("act_chain")
        ones_set, prep_pe, prep_done = sem("ones_set"), sem("prep_pe"), sem("prep_done")
        stage_end, waited = sem("stage_end"), sem("waited")
        var_ready, rstd_ready = sem("var_ready"), sem("rstd_ready")
        m_ln, m_b01_pe, m_b01_ev = sem("m_ln"), sem("m_b01_pe"), sem("m_b01_ev")
        m_v_pe, m_v_ev, m_yb, m_yt_pe, m_yt_ev = (sem(n) for n in ("m_v_pe", "m_v_ev", "m_yb", "m_yt_pe", "m_yt_ev"))
        m_z_pe, m_sub, m_exp, m_at, m_w_pe, m_w_add = (sem(n) for n in ("m_z_pe", "m_sub", "m_exp", "m_at", "m_w_pe", "m_w_add"))
        ffn_sems = []
        for l in range(2):
            ffn_sems.append({n: sem(f"f{l}_{n}") for n in (
                "ln", "xt_pe", "xt", "gate_pe", "gate_d", "tanh", "up", "gelu", "low", "low_pool", "down", "y_ev", "yt_pe", "comb")})
        s = {n: sem("s_" + n) for n in (
            "ln", "b0_pe", "b0_ev", "hi", "x3", "cv", "cv_th", "cv_ev", "z_pe", "z_th", "z_ev", "raw", "exp_dt", "a", "cs", "ex",
            "w", "bt", "r", "xdt", "xw", "xd", "d_pe", "l", "m", "y_pe", "y", "ds_pe", "s1", "state", "u", "gate", "o_pe", "o_add", "var_y", "rstd_y")}

        block = ctx.enter_context(nc.Block())

        def bank(b, n=1):
            return ps[:, b:b + n, :].rearrange("p a b -> p (a b)")

        def experts_due(t, c, lag):
            first, last = (isinstance(t, int) and t == n for n in (0, NT - 1))
            for before in (0, 1):
                e, n = divmod(c - lag + NC * before, CPE)
                if n == CPE - 1 and 0 <= e < NEXP and not (before and (first or c >= NC)):
                    yield before, e

        def layer_norm(dve, ch, src, dst, n, width, which_eps, count, ready, part=None, own=None):
            if part != 1:
                row_stats(dve, ch, src, n, width, which_eps, own or token_norm)
            if part == 0:
                return
            _, mom, _, has_rstd = own or token_norm
            dve.wait_ge(has_rstd, count)
            mo = mom[:, :, 0:n]
            for r in range(n):
                i = dve.tensor_scalar(dst(r), src(r), mo[:, 0, r:r + 1], mo[:, 5, r:r + 1], ALU.subtract, ALU.mult)
                if ready is not None and (r + 1) % Q == 0:
                    i.then_inc(ready, 1)

        token_norm = (stats, moments, var_ready, rstd_ready)
        y_norm = (stats_y, moments_y, s["var_y"], s["rstd_y"])

        def row_stats(dve, ch, src, n, width, which_eps, own):
            sums, mom, has_var, _ = own
            for r in range(n):
                i = dve.bn_stats(sums[:, r, :], src(r))
                ch.done(i)
            ch.wait()
            sv = sums[:, 0:n, :]
            mo = mom[:, :, 0:n]
            ch.done(dve.tensor_tensor(mo[:, 0, :], sv[:, :, 1], sv[:, :, 4], ALU.add))
            ch.done(dve.tensor_tensor(mo[:, 1, :], sv[:, :, 1], sv[:, :, 4], ALU.subtract))
            ch.link(dve.tensor_tensor(mo[:, 2, :], sv[:, :, 2], sv[:, :, 5], ALU.add))
            ch.done(dve.tensor_scalar(mo[:, 0, :], mo[:, 0, :], 0.5, None, ALU.mult))
            ch.link(dve.tensor_tensor(mo[:, 1, :], mo[:, 1, :], mo[:, 1, :], ALU.mult))
            ch.link(dve.scalar_tensor_tensor(mo[:, 3, :], mo[:, 1, :], width / 4.0, mo[:, 2, :], ALU.mult, ALU.add))
            dve.tensor_scalar(mo[:, 4, :], mo[:, 3, :], 1.0 / width, which_eps, ALU.mult, ALU.add).then_inc(has_var, 1)

        def rstd(pool, n, count, own=None):
            _, mom, has_var, has_rstd = own or token_norm
            pool.wait_ge(has_var, count)
            pool.tensor_tensor(mom[:, 5, 0:n], mom[:, 4, 0:n], half_neg[:, 0:n], ALU.pow).then_inc(has_rstd, 1)

        LN_FFN0 = G
        LN_MIX1 = LN_FFN0 + NT
        LN_FFN1 = LN_MIX1 + NT

        def steps_of_rows(eng, step, enter=None, leave=None):
            for r in range(-HEAD, TAIL):
                step(0, r)
            with eng.Fori(0, G - 1) as g:
                if enter:
                    enter(g)
                for r in range(TAIL, TAIL + SIDE):
                    step(g, r)
                if leave:
                    leave()
            for r in range(TAIL + SIDE * (G - 1), SIDE * G + TAIL):
                step(0, r)

        def row(g, r, lag):
            i = r - lag
            return i if not isinstance(g, int) or 0 <= i < G * SIDE else None

        def quad(g, r, lag):
            i = row(g, r, lag)
            return None if i is None or i % Q else i // Q

        T_AHEAD, U_LAG = 3, 11
        BETWEEN = (T_AHEAD + U_LAG) // Q + 1

        def before_t(g, k):
            return g * (3 * NQ) + (k + 2 * (max(0, k - (BETWEEN - 1)) if isinstance(g, int) else k - (BETWEEN - 1)))

        def before_u(g, c):
            return g * (3 * NQ) + (2 * c + (min(c + BETWEEN, NT) if isinstance(g, int) else c + BETWEEN))

        @block.sync
        def _(sp_):
            sp_.dma_start(consts[:, :], inp["consts"]).then_inc(const_in, 16)
            for g in range(G):
                if g:
                    sp_.wait_ge(x_in, 64 * g)
                for b in range(PACK):
                    sp_.dma_start(xr[b * SIDE:(b + 1) * SIDE, g, :, :],
                                  inp["x"][g * PACK + b].rearrange("h w d -> w h d")).then_inc(x_in, 16)
                if g == 0:
                    sp_.dma_start(wc[0:D, 0:D], inp["Wc"]).then_inc(mix_in, 16)
                    sp_.dma_start(wc[0:D, D:D + 1], inp["bc"]).then_inc(mix_in, 16)
                    sp_.dma_start(wo_t[0:D, :], inp["WoT"]).then_inc(mix_in, 16)
                    sp_.dma_start(bo[D:D + 1, :], inp["bo"]).then_inc(mix_in, 16)
                    sp_.dma_start(rhs0[0:D + 1, 2 * D:NV], inp["W1T"]).then_inc(mix_in, 16)
                    sp_.wait_ge(ones_set, 1)
                    for m in range(2):
                        for c in range(SEG):
                            sp_.dma_start(w2z[8 * c:8 * c + 8, m, c * P:(c + 1) * P], inp["W2T"][m, c]).then_inc(mix_in, 16)
                        sp_.dma_start(w2z[64:65, m, :], inp["b2z"][m]).then_inc(mix_in, 16)

            def ffn_weights(l):
                w = inp["ffn"][l]
                sp_.dma_start(w1[0:D, :].rearrange("p (e h) -> p e h", h=HID), w["w1"].rearrange("e d h -> d e h")).then_inc(ffn_in, 16)
                sp_.dma_start(w1[D:D + 1, :], w["b1"]).then_inc(ffn_in, 16)
                sp_.dma_start(w2[:, :, :], w["w2"].rearrange("e (c p) d -> p (e c) d", p=P)).then_inc(ffn_in, 16)
                sp_.dma_start(b2[:, :], w["b2T"]).then_inc(ffn_in, 16)
                sp_.dma_start(gw[0:D, :], w["gate_w"]).then_inc(ffn_in, 16)
                sp_.dma_start(gw[D:D + 1, :], w["gate_b"]).then_inc(ffn_in, 16)

            ffn_weights(0)
            if stop >= 3:
                sp_.wait_ge(stage_end, 2)
                sp_.dma_start(wz0[0:D, :, :], inp["Win_z"]).then_inc(ssm_in, 16)
                sp_.dma_start(wtap0[0:D, CENTRE, CONV:CONV + NH], inp["Win_dt"]).then_inc(ssm_in, 16)
                sp_.dma_start(wtap0[D:D + 1, CENTRE, CONV:CONV + NH], inp["dt_bias"]).then_inc(ssm_in, 16)
                sp_.dma_start(winx[0:D, :], inp["Win_x"]).then_inc(ssm_in, 16)
                sp_.dma_start(wtap0[D:D + 1, CENTRE, 0:CONV], inp["b_conv"]).then_inc(ssm_in, 16)
                sp_.dma_start(wcv[0:D, :, :], inp["W_conv"].partition_broadcast(D)).then_inc(ssm_in, 16)
                sp_.dma_start(a_log, inp["A_log"].partition_broadcast(P)).then_inc(ssm_in, 16)
                sp_.dma_start(d_par, inp["D_param"].partition_broadcast(P)).then_inc(ssm_in, 16)
                sp_.dma_start(gamma[0:D, :], inp["gamma"]).then_inc(ssm_in, 16)
                sp_.dma_start(beta[0:D, :], inp["beta"]).then_inc(ssm_in, 16)
                sp_.dma_start(wout[0:D, :, :], inp["W_out"]).then_inc(ssm_in, 16)
            if stop >= 4:
                ffn_weights(1)
            sp_.wait_ge(stage_end, stop if stop < 4 else 4)
            sp_.wait_ge(ffn_in, 96)
            for g in range(G):
                for b in range(PACK):
                    sp_.dma_start(out[g * PACK + b].rearrange("h w d -> w h d"),
                                  xr[b * SIDE:(b + 1) * SIDE, g, :, :]).then_inc(x_out, 16)
            sp_.wait_ge(x_out, 16 * IMG)

        @block.gpsimd
        def _(pool):
            ch = Chain(pool, pool_chain)

            def ffn(f, ln_before):
                def tile(t, par=None):
                    par = t % 2 if par is None else par
                    last = isinstance(t, int) and t == NT - 1
                    for n, c in enumerate(POOL_CHUNKS):
                        pool.wait_ge(f["gelu"], t * NC + (c + 1))
                        r = c % RING
                        pool.tensor_tensor(hidr[:, 1, r, :], hid[:, r, :], hidr[:, 0, r, :].bitcast(F32), ALU.subtract).then_inc(f["low_pool"], 1)
                        if n == 0 and not last:
                            rstd(pool, Q, t + (ln_before + 2))

                rstd(pool, Q, ln_before + 1)
                tiles(pool, tile)

            ch.done(pool.memset(half_neg[:, :], -0.5))
            ch.link(pool.memset(yt[:, :, :], 1.0))
            pool.memset(w2z[:, :, :], 0.0).then_inc(ones_set, 1)
            with pool.Fori(0, G) as g:
                rstd(pool, SIDE, g + 1)
            if stop >= 2:
                ffn(ffn_sems[0], LN_FFN0)
            if stop >= 3:
                pool.wait_ge(stage_end, 2)
                ch.done(pool.memset(rounded[:, :, 0:SHIFTS].bitcast(F32), 0.0))
                ch.link(pool.memset(xbc[:, :, :, CONV:XB], 0.0))
                pool.memset(x3[D:D + 1, 0, 0, :, :].bitcast(F32), 1.0).then_inc(ones_set, 1)
                pool.wait_ge(prep_done, 2)

                def steps_from(g, c, i):
                    if i == 0:
                        pool.wait_ge(s["a"], g * NQ + (c + 1))
                    need(pool, s["d_pe"], g * SIDE + (Q * c + i + 1 - Q))
                    pool.tensor_tensor(
                        rr[:, i, :, :], av[:, c % 2, i, :].unsqueeze(2).to_broadcast([P, NH, SIDE]),
                        tri.unsqueeze(1).to_broadcast([P, NH, SIDE]), ALU.mult).then_inc(s["r"], 1)

                def scaled(c, dst, by, done):
                    xs = xbc[:, c % 2, :, 0:INNER].rearrange("p q (h e) -> p q h e", e=HD)
                    pool.tensor_tensor(dst[:, c % 2], xs, by.unsqueeze(3).to_broadcast([P, Q, NH, HD]), ALU.mult).then_inc(s[done], 1)

                def decayed(g, i):
                    pool.wait_ge(s["state"], g * SIDE + (i + 1))
                    if i % Q == 0:
                        pool.wait_ge(s["ex"], g * NQ + (i // Q + 1))
                    pool.tensor_tensor(st1[:, :, :], st[:, :, :],
                                       ex3[:, i // Q % 2, 2, i % Q, :].unsqueeze(2).to_broadcast([P, NH, HD]), ALU.mult).then_inc(s["s1"], 1)

                def step(g, r):
                    if (i := row(g, r, 6)) is not None:
                        decayed(g, i)
                    if (c := quad(g, r, 4)) is not None:
                        steps_from(g, c, 0)
                        scaled(c, xdt, dt[:, c % 2, :, :], "xdt")
                    if (c := quad(g, r, 5)) is not None:
                        steps_from(g, c, 1)
                        pool.wait_ge(s["w"], g * NQ + (c + 1))
                        scaled(c, xw, wdt[:, :, :], "xw")
                        scaled(c, xd, d_par.unsqueeze(1).to_broadcast([P, Q, NH]), "xd")
                    if (c := quad(g, r, 6)) is not None:
                        steps_from(g, c, 2)
                    if (c := quad(g, r, 7)) is not None:
                        steps_from(g, c, 3)
                    if (c := quad(g, r, 9)) is not None:
                        rstd(pool, Q, g * NQ + (c + 1), y_norm)
                    if (k := quad(g, r, -6)) is not None:
                        rstd(pool, Q, g * NQ + (LN_MIX1 + k + 1))

                steps_of_rows(pool, step)
            if stop >= 4:
                ffn(ffn_sems[1], LN_FFN1)

        @block.scalar
        def _(act):
            act.sem_inc(m_b01_ev, 2)
            with act.Fori(0, G) as g:
                def evacuate(k, dst):
                    act.wait_ge(m_b01_pe, g * (2 * NQ) + (k + 1))
                    act.copy(dst, bank(k % 2)[0:dst.shape[0], 0:dst.shape[1]]).then_inc(m_b01_ev, 1)

                evacuate(0, xt0[0:D, 0:BANK])
                for r in range(SIDE // 2):
                    q = r // 2 + 1
                    if r % 2 == 0 and q < NQ:
                        evacuate(q, xt0[0:D, q % 2 * BANK:(q % 2 + 1) * BANK])
                    act.wait_ge(m_v_pe, g * (SIDE // 2) + (r + 1))
                    act.copy(vc[:, 2 * r:2 * r + 2, :], bank(2 + r % 2).rearrange("p (a b) -> p a b", a=2)[:, :, 0:NV]).then_inc(m_v_ev, 1)
                act.wait_ge(m_yt_pe, g + 1)
                act.copy(yt[0:64, :, :], bank(4)[0:64, 0:2 * P].rearrange("p (a b) -> p a b", a=2)).then_inc(m_yt_ev, 1)
                for m in range(2):
                    act.wait_ge(m_sub, g * 2 + (m + 1))
                    act.activation(at[:, m, :, :], sc[:, :, :], ACT.Exp).then_inc(m_exp, 1)
                for q in range(NQ):
                    evacuate(NQ + q, oh[:, Q * q:Q * q + Q, :].rearrange("p a b -> p (a b)"))

            def ffn(f):
                def tile(t, par=None):
                    def y_out(t, e):
                        act.wait_ge(f["down"], t * NC + CPE * (e + 1))
                        need(act, f["yt_pe"], t * NEXP + (e - 1))
                        act.activation(yte[0:D, e % 2, :], bank(2 + e % 2)[0:D, :], ACT.Identity, bias=b2[:, e:e + 1]).then_inc(f["y_ev"], 1)

                    for c in range(NC):
                        act.wait_ge(f["up"], t * NC + (c + 1))
                        need(act, f["down"], t * NC + (c + 1 - RING))
                        act.activation(hidr[:, 0, c % RING, :], bank(c % 2), ACT.Gelu)
                        act.activation(hid[:, c % RING, :], bank(c % 2), ACT.Gelu).then_inc(f["gelu"], 1)
                        if c == 1:
                            act.wait_ge(f["gate_d"], t + 1)
                            act.activation(gth[:, :, :], gd[:, :, :], ACT.Tanh, scale=0.5).then_inc(f["tanh"], 1)
                        for before, e in experts_due(t, c, LAG + 1):
                            y_out(t - before, e)
                    if isinstance(t, int) and t == NT - 1:
                        for c in range(NC, 2 * NC):
                            for before, e in experts_due(t, c, LAG + 1):
                                y_out(t, e)

                tiles(act, tile)

            if stop >= 2:
                act.wait_ge(stage_end, 1)
                act.wait_ge(ffn_in, 16 * 6)
                ffn(ffn_sems[0])
            if stop >= 3:
                act.wait_ge(ssm_in, 16 * 11)
                act.activation(a_exp, a_log, ACT.Exp).then_inc(act_chain, 1)
                act.sem_inc(s["b0_ev"], 1)
                act.wait_ge(prep_done, 2)

                def spread(g, k):
                    act.wait_ge(s["b0_pe"], before_t(g, k) + 1)
                    act.copy(x3[0:D, 0, 0, k % SLOTS, :], bank(0)[0:D, :]).then_inc(s["hi"], 1)

                def shift(g, k):
                    act.wait_ge(s["b0_ev"], before_t(g, k) + 2)
                    src = x3[0:D, :, 0, k % SLOTS, :].rearrange("p s (a w) -> p s a w", w=SIDE).bitcast(F32)
                    for n in (1, 2):
                        dst = x3[0:D, :, n, k % SLOTS, :].rearrange("p s (a w) -> p s a w", w=SIDE)
                        to, frm = (slice(1, SIDE), slice(0, SIDE - 1)) if n == 1 else (slice(0, SIDE - 1), slice(1, SIDE))
                        ins = act.copy(dst[:, :, :, to], src[:, :, :, frm])
                    ins.then_inc(s["x3"], 1)

                def conv_tanh(g, i):
                    act.wait_ge(s["cv"], g * SIDE + (i + 1))
                    need(act, s["cv_ev"], g * SIDE + i)
                    act.activation(th[:, 0:CONV], bank(1 + i % 2)[:, 0:CONV], ACT.Tanh).then_inc(s["cv_th"], 1)

                def decays(g, c):
                    act.wait_ge(s["cs"], g * NQ + (c + 1))
                    act.activation(ex3[:, c % 2, :, :, :].rearrange("p a b c -> p (a b c)"), bank(7)[:, 0:3 * Q * NH], ACT.Exp).then_inc(s["ex"], 1)

                def pair_decay(g, i):
                    act.wait_ge(s["d_pe"], g * SIDE + (i + 1))
                    act.activation(ll[:, i % 2, :, :].rearrange("p a b -> p (a b)"), bank(4)[:, 0:NH * SIDE], ACT.Exp).then_inc(s["l"], 1)

                def z_tanh(g, q, n):
                    act.wait_ge(s["z_pe"], g * (2 * NQ) + (2 * q + n + 1))
                    need(act, s["z_ev"], g * (2 * NQ) + (2 * q + n))
                    act.activation(thz[0:D, :], bank(3)[0:D, :], ACT.Tanh).then_inc(s["z_th"], 1)

                def affine(g, c, n):
                    act.wait_ge(s["b0_pe"], before_u(g, c) + (n + 1))
                    act.activation(g4[0:D, n, :], bank(0)[0:D, :], ACT.Identity, bias=beta[0:D, n:n + 1], scale=gamma[0:D, n:n + 1]).then_inc(s["b0_ev"], 1)

                def step(g, r):
                    if (i := row(g, r, 0)) is not None:
                        conv_tanh(g, i)
                    if (c := quad(g, r, 5)) is not None:
                        decays(g, c)
                    if (c := quad(g, r, U_LAG)) is not None:
                        affine(g, c, 0)
                    if (q := quad(g, r, 4)) is not None:
                        z_tanh(g, q, 0)
                    if (q := quad(g, r, 5)) is not None:
                        z_tanh(g, q, 1)
                    if (c := quad(g, r, U_LAG)) is not None:
                        affine(g, c, 1)
                    if (k := quad(g, r, -T_AHEAD)) is not None:
                        spread(g, k)
                    if (i := row(g, r, 5)) is not None:
                        pair_decay(g, i)
                    if (k := quad(g, r, -T_AHEAD)) is not None:
                        shift(g, k)
                    if (q := quad(g, r, 3)) is not None:
                        act.wait_ge(s["raw"], g * NQ + (q + 1))
                        act.activation(sp[:, 1, :], sp[:, 0, :], ACT.Exp, scale=-1.0).then_inc(s["exp_dt"], 1)

                steps_of_rows(act, step)
            if stop >= 4:
                act.wait_ge(stage_end, 3)
                act.wait_ge(ffn_in, 16 * 12)
                ffn(ffn_sems[1])

        @block.tensor
        def _(pe):
            pe.wait_ge(const_in, 16)
            pe.wait_ge(mix_in, 16 * 23)

            held = [0]

            def apart(g, rounds=G - 1):
                pe.sem_inc(waited, 1)
                held[0] += 1 if isinstance(g, int) else rounds

            pe.matmul(bank(5)[0:D + 1, 0:D], wc[0:D, 0:D + 1], wo_t[0:D, :], start=True, stop=True).then_inc(prep_pe, 1)
            pe.wait_ge(prep_done, 1)
            with pe.Fori(0, G) as g:
                def bank01(k):
                    pe.wait_ge(m_b01_ev, g * (2 * NQ) + (k + 1))

                def to_columns(q):
                    pe.wait_ge(m_ln, g * NQ + (q + 1))
                    bank01(q)
                    for i in range(Q):
                        ins = pe.transpose(bank(q % 2)[0:D, i * P:(i + 1) * P], xn[:, Q * q + i, :], ident)
                    ins.then_inc(m_b01_pe, 1)

                to_columns(0)
                pe.wait_ge(m_w_add, g * NQ + NQ)
                for r in range(SIDE // 2):
                    q = r // 2
                    if r % 2 == 0:
                        if q + 1 < NQ:
                            to_columns(q + 1)
                        pe.wait_ge(m_b01_ev, g * (2 * NQ) + (2 + q + 1))
                    if r >= 2:
                        pe.wait_ge(m_v_ev, g * (SIDE // 2) + (r - 1))
                    for i in range(2):
                        h = 2 * r + i
                        ins = pe.matmul(bank(2 + r % 2)[:, i * 256:i * 256 + NV], xt0[0:D + 1, h % (2 * Q) * P:(h % (2 * Q) + 1) * P], rhs0[0:D + 1, :], start=True, stop=True)
                    ins.then_inc(m_v_pe, 1)
                pe.wait_ge(m_yb, g + 1)
                apart(g, G)
                for m, src in enumerate((yb[:, 0, :], ywt)):
                    ins = pe.transpose(bank(4)[0:64, m * P:(m + 1) * P], src, ident)
                ins.then_inc(m_yt_pe, 1)
                pe.wait_ge(m_yt_ev, g + 1)
                for m in range(2):
                    for n in range(2):
                        ins = pe.matmul(bank(6 - 2 * m + n), yt[0:65, m, :], w2z[0:65, m, n * BANK:(n + 1) * BANK], start=True, stop=True)
                    ins.then_inc(m_z_pe, 1)
                for m in range(2):
                    pe.wait_ge(m_at, g * 2 + (m + 1))
                    for q in range(NQ):
                        if m == 0:
                            bank01(NQ + q)
                        elif q >= 2:
                            pe.wait_ge(m_w_add, g * NQ + (NQ + q - 1))
                        apart(g, G)
                        for i in range(Q):
                            w = Q * q + i
                            for b in range(PACK):
                                pb = slice(b * SIDE, (b + 1) * SIDE)
                                val = vh[pb, w, :] if m == 0 else vc[pb, w, 0:D]
                                ins = pe.matmul(bank(2 * m + q % 2)[pb, i * D:(i + 1) * D], at[pb, m, :, w], val, start=True, stop=True)
                        ins.then_inc(m_b01_pe if m == 0 else m_w_pe, 1)

            def product(dst, left, right, start=True, stop=True):
                pe.matmul(dst, left[0], right[0], start=start, stop=False)
                pe.matmul(dst, left[1], right[0], start=False, stop=False)
                return pe.matmul(dst, left[0], right[1], start=False, stop=stop)

            def halves(a):
                return a[:, 0], a[:, 1]

            def ffn(f):
                def x_in_columns(t):
                    pe.wait_ge(f["ln"], t + 1)
                    need(pe, f["xt"], t)
                    for i in range(Q):
                        ins = pe.transpose(bank(4)[0:D, i * P:(i + 1) * P], xn4[:, i, :], ident)
                    ins.then_inc(f["xt_pe"], 1)

                def y_in_rows(t, e):
                    pe.wait_ge(f["y_ev"], t * NEXP + (e + 1))
                    need(pe, f["comb"], t * NEXP + (e - 1))
                    for i in range(Q):
                        ins = pe.transpose(bank(6 + e % 2)[:, i * D:(i + 1) * D], yte[0:D, e % 2, i * P:(i + 1) * P], ident[0:D, 0:D])
                    ins.then_inc(f["yt_pe"], 1)

                def up(t, par, c):
                    need(pe, f["gelu"], t * NC + (c - 1))
                    product(bank(c % 2), halves(w1r[0:D + 1, :, c * P:(c + 1) * P]), halves(xtr[0:D + 1, :, par, :])).then_inc(f["up"], 1)

                def down(t, c):
                    e, n = divmod(c, CPE)
                    if n == 0:
                        need(pe, f["y_ev"], t * NEXP + (e - 1))
                    mine = [x for x in range(NC) if (x in POOL_CHUNKS) == (c in POOL_CHUNKS)]
                    pe.wait_ge(f["low_pool" if c in POOL_CHUNKS else "low"], t * len(mine) + (mine.index(c) + 1))
                    product(bank(2 + e % 2)[0:D, :], halves(w2r[:, :, c, :]), halves(hidr[:, :, c % RING, :]), n == 0, n == CPE - 1).then_inc(f["down"], 1)

                def tile(t, par=None):
                    first, last = (isinstance(t, int) and t == n for n in (0, NT - 1))
                    par = t % 2 if par is None else par
                    if first:
                        x_in_columns(t)
                    pe.wait_ge(f["xt"], t + 1)
                    for c in range(2 * NC if last else NC):
                        if c < NC:
                            up(t, par, c)
                        if c == 0:
                            for i in range(Q):
                                ins = product(bank(5)[:, i * NEXP:(i + 1) * NEXP], halves(xtr[0:D + 1, :, par, i * P:(i + 1) * P]), halves(gwr[0:D + 1, :, :]))
                            ins.then_inc(f["gate_pe"], 1)
                        if LAG <= c < NC + LAG:
                            down(t, c - LAG)
                        elif c < LAG and not first:
                            down(t - 1, NC + c - LAG)
                        if c == 5 and not last:
                            x_in_columns(t + 1)
                        for before, e in experts_due(t, c, LAG + 2):
                            y_in_rows(t - before, e)

                tiles(pe, tile)

            if stop >= 2:
                pe.wait_ge(stage_end, 1)
                ffn(ffn_sems[0])
            if stop >= 3:
                pe.wait_ge(prep_done, 2)

                def to_columns(g, k):
                    pe.wait_ge(s["ln"], g * NQ + (k + 1))
                    pe.wait_ge(s["b0_ev"], before_t(g, k) + 1)
                    for i in range(Q):
                        ins = pe.transpose(bank(0)[0:D, i * P:(i + 1) * P], xn[:, k % 2 * Q + i, :], ident)
                    ins.then_inc(s["b0_pe"], 1)

                def conv(g, i):
                    h = i % SIDE
                    if h == 0:
                        pe.wait_ge(s["x3"], g * NQ + (i // Q + 1))
                    if h % Q == Q - 1 and h < SIDE - 1:
                        pe.wait_ge(s["x3"], g * NQ + (i // Q + 2))
                    need(pe, s["cv_ev"], g * SIDE + (i - 1))
                    taps = [(0, 0)] + [(y, x) for y in (-1, 0, 1) for x in (-1, 0, 1) if (x or y) and 0 <= h + y < SIDE]
                    for n, (y, x) in enumerate(taps):
                        at_row = (h + y) % Q * P
                        src = x3[:, :, {0: 0, -1: 1, 1: 2}[x], (h + y) // Q % SLOTS, at_row:at_row + P]
                        t = 3 * (y + 1) + x + 1
                        k, c = (D + 1, CONVD) if n == 0 else (D, CONV)
                        ins = product(bank(1 + i % 2)[:, 0:c], halves(src[0:k]), halves(wtap[0:k, :, t, 0:c]), n == 0, n == len(taps) - 1)
                    ins.then_inc(s["cv"], 1)

                def z_columns(g, q, n):
                    need(pe, s["z_ev"], g * (2 * NQ) + (2 * q + n))
                    if n == 0:
                        need(pe, s["o_add"], g * NQ + (q - 2))
                    product(bank(3)[0:D, :], halves(wz[0:D, :, n, :]), halves(x3[0:D, :, 0, q % SLOTS, :])).then_inc(s["z_pe"], 1)

                def sums(g, c):
                    pe.wait_ge(s["a"], g * NQ + (c + 1))
                    a = av[:, c % 2, :, :].rearrange("p a b -> p (a b)")
                    for n, w in enumerate((upto, later, whole)):
                        ins = pe.matmul(bank(7)[:, n * Q * NH:(n + 1) * Q * NH], w, a, start=True, stop=True)
                    ins.then_inc(s["cs"], 1)

                def pairs(g, i):
                    c = i // Q
                    need(pe, s["m"], g * SIDE + i)
                    if i % Q == 0:
                        pe.wait_ge(s["bt"], g * NQ + (c + 1))
                    apart(g)
                    for b in range(PACK):
                        pb = slice(b * SIDE, b * SIDE + NS)
                        pe.matmul(bank(4)[b * SIDE:(b + 1) * SIDE, NH * SIDE:NH * SIDE + SIDE], bt[pb, c % 2, i % Q, :], ct[pb, c % 2, i % Q, :], start=True, stop=True)
                    pe.wait_ge(s["r"], g * SIDE + (i + 1))
                    pe.matmul(bank(4)[:, 0:NH * SIDE], later, rr[:, i % Q, :, :].rearrange("p a b -> p (a b)"), start=True, stop=True).then_inc(s["d_pe"], 1)

                def scan(g, i):
                    c, j = i // Q, i % Q
                    if j == 0:
                        pe.wait_ge(s["xdt"], g * NQ + (c + 1))
                        pe.wait_ge(s["xw"], g * NQ + (c + 1))
                    need(pe, s["y"], g * SIDE + i)
                    pe.wait_ge(s["m"], g * SIDE + (i + 1))
                    pe.wait_ge(s["state"], g * SIDE + (i + 1))
                    apart(g)
                    for b in range(PACK):
                        pb = slice(b * SIDE, b * SIDE + NS)
                        pe.matmul(bank(5)[b * SIDE:(b + 1) * SIDE, INNER:2 * INNER], ct[pb, c % 2, j, :], st[pb, :, :].rearrange("p a b -> p (a b)"), start=True, stop=True)
                    for n in range(NH):
                        for b in range(PACK):
                            pb = slice(b * SIDE, (b + 1) * SIDE)
                            ins = pe.matmul(bank(5)[pb, n * HD:(n + 1) * HD], mm[pb, i % 2, n, :], xdt[pb, c % 2, j, n, :], start=True, stop=True)
                    ins.then_inc(s["y_pe"], 1)
                    for b in range(PACK):
                        pb = slice(b * SIDE, (b + 1) * SIDE)
                        ins = pe.matmul(bank(6)[pb, 0:INNER], xbc[pb, c % 2, j, INNER:INNER + 2 * NS], xw[pb, c % 2, j, :, :].rearrange("p a b -> p (a b)"), start=True, stop=True)
                    ins.then_inc(s["ds_pe"], 1)

                def u_columns(g, c, n):
                    pe.wait_ge(s["u"], g * NQ + (c + 1))
                    pe.wait_ge(s["b0_ev"], before_u(g, c) + (n + 1))
                    for i in range(Q):
                        ins = pe.transpose(bank(0)[0:D, i * P:(i + 1) * P], u4[:, i, n * D:(n + 1) * D], ident)
                    ins.then_inc(s["b0_pe"], 1)

                def project(g, c):
                    pe.wait_ge(s["gate"], g * NQ + (c + 1))
                    last = 2 * (c + 3)
                    pe.wait_ge(s["z_ev"], g * (2 * NQ) + (min(last, 2 * NT) if isinstance(g, int) else last))
                    for i in range(Q):
                        for n in range(2):
                            ins = pe.matmul(bank(3)[:, i * D:(i + 1) * D], g4[0:D, n, i * P:(i + 1) * P], wout[0:D, n, :], start=(n == 0), stop=(n == 1))
                    ins.then_inc(s["o_pe"], 1)

                def step(g, r):
                    if (i := row(g, r, 0)) is not None:
                        conv(g, i)
                    if (c := quad(g, r, 5)) is not None:
                        sums(g, c)
                    if (c := quad(g, r, U_LAG)) is not None:
                        u_columns(g, c, 0)
                    if (q := quad(g, r, 4)) is not None:
                        z_columns(g, q, 0)
                    if (i := row(g, r, 6)) is not None:
                        scan(g, i)
                    if (q := quad(g, r, 5)) is not None:
                        z_columns(g, q, 1)
                    if (c := quad(g, r, U_LAG)) is not None:
                        u_columns(g, c, 1)
                    if (k := quad(g, r, -T_AHEAD)) is not None:
                        to_columns(g, k)
                    if (c := quad(g, r, 14)) is not None:
                        project(g, c)
                    if (i := row(g, r, 5)) is not None:
                        pairs(g, i)

                steps_of_rows(pe, step)
            if stop >= 4:
                pe.wait_ge(stage_end, 3)
                ffn(ffn_sems[1])
            pe.wait_ge(waited, held[0])

        def split(dve, ch, src, dst):
            ch.link(dve.tensor_copy(dst[:, 0], src))
            return dve.tensor_tensor(dst[:, 1], src, dst[:, 0].bitcast(F32), ALU.subtract)

        def mixer1(dve, ch):
            dve.wait_ge(ssm_in, 16 * 11)
            dve.wait_ge(act_chain, 1)
            ch.done(dve.tensor_scalar(neg_a, a_exp, -1.0, None, ALU.mult))
            ch.done(dve.tensor_scalar(wz0[0:D, :, :], wz0[0:D, :, :], 0.5, None, ALU.mult))
            ch.done(dve.tensor_scalar(wtap0[D:D + 1, CENTRE, 0:CONV], wtap0[D:D + 1, CENTRE, 0:CONV], 0.5, None, ALU.mult))
            for t in range(TAPS):
                ch.done(dve.scalar_tensor_tensor(wtap0[0:D, t, 0:CONV], winx[0:D, :], 0.5, wcv[0:D, t, :], ALU.mult, ALU.mult))
            ch.wait()
            ch.done(split(dve, ch, wz0[0:D, :, :], wz[0:D]))
            ch.done(split(dve, ch, wtap0[0:D, :, 0:CONV], wtap[0:D, :, :, 0:CONV]))
            ch.done(split(dve, ch, wtap0[D:D + 1, CENTRE, 0:CONV], wtap[D:D + 1, :, CENTRE, 0:CONV]))
            ch.link(split(dve, ch, wtap0[0:D + 1, CENTRE, CONV:CONVD], wtap[0:D + 1, :, CENTRE, CONV:CONVD]))
            dve.wait_ge(ones_set, 2)
            dve.sem_inc(prep_done, 1)
            dve.memset(st[:, :, :], 0.0).then_inc(s["state"], 1)

            def conv_silu(g, i):
                b = bank(1 + i % 2)
                dve.wait_ge(s["cv_th"], g * SIDE + (i + 1))
                ch.done(dve.tensor_copy(dtr[:, i // Q % 2, i % Q, :], b[:, CONV:CONV + NH]))
                dve.scalar_tensor_tensor(xbc[:, i // Q % 2, i % Q, 0:CONV], th[:, 0:CONV], 1.0, b[:, 0:CONV], ALU.add, ALU.mult).then_inc(s["cv_ev"], 1)

            def weigh(g, c):
                dve.wait_ge(s["ex"], g * NQ + (c + 1))
                dve.tensor_tensor(wdt[:, :, :], dt[:, c % 2, :, :], ex3[:, c % 2, 1, :, :], ALU.mult).then_inc(s["w"], 1)

            def attend(g, i):
                dve.wait_ge(s["l"], g * SIDE + (i + 1))
                ch.link(dve.tensor_tensor(gmk, bank(4)[:, NH * SIDE:NH * SIDE + SIDE], tri, ALU.mult))
                dve.tensor_tensor(mm[:, i % 2, :, :], ll[:, i % 2, :, :], gmk.unsqueeze(1).to_broadcast([P, NH, SIDE]), ALU.mult).then_inc(s["m"], 1)

            def gather(g, i):
                c, j = i // Q, i % Q
                y = yy[:, c % 2, j, :].rearrange("p (h e) -> p h e", e=HD)
                heads = bank(5)[:, 0:2 * INNER].rearrange("p (a h e) -> p a h e", a=2, e=HD)
                dve.wait_ge(s["y_pe"], g * SIDE + (i + 1))
                ch.link(dve.tensor_tensor(y, heads[:, 1], ex3[:, c % 2, 0, j, :].unsqueeze(2).to_broadcast([P, NH, HD]), ALU.mult))
                dve.tensor_tensor(y, y, heads[:, 0], ALU.add).then_inc(s["y"], 1)
                dve.wait_ge(s["s1"], g * SIDE + (i + 1))
                dve.wait_ge(s["ds_pe"], g * SIDE + (i + 1))
                if i % SIDE == SIDE - 1:
                    dve.memset(st[:, :, :], 0.0).then_inc(s["state"], 1)
                else:
                    dve.tensor_tensor(st[:, :, :], st1[:, :, :], bank(6)[:, 0:INNER].rearrange("p (h e) -> p h e", e=HD), ALU.add).then_inc(s["state"], 1)
                if j == 0:
                    dve.wait_ge(s["xd"], g * NQ + (c + 1))
                dve.wait_ge(s["y"], g * SIDE + (i + 1))
                ch.done(dve.tensor_tensor(y, y, xd[:, c % 2, j, :, :], ALU.add))

            flat = lambda a: a.rearrange("p a b -> p (a b)")

            def time_steps_begin(g, q):
                x = flat(dtr[:, q % 2, :, :])
                ch.wait()
                dve.scalar_tensor_tensor(sp[:, 0, :], x, -1.0, x, ALU.mult, ALU.max).then_inc(s["raw"], 1)
                ch.done(dve.tensor_scalar(sp[:, 5, :], x, 0.0, None, ALU.max))
                dve.wait_ge(s["cv_ev"], g * SIDE + (Q * q + Q))
                ch.done(dve.transpose(bt[:, q % 2, :, :], xbc[:, q % 2, :, INNER:INNER + SIDE]))
                dve.transpose(ct[:, q % 2, :, :], xbc[:, q % 2, :, INNER + NS:INNER + NS + SIDE]).then_inc(s["bt"], 1)

            def time_steps(g, q):
                dve.wait_ge(s["exp_dt"], g * NQ + (q + 1))
                u, r, r2, p = sp[:, 1, :], sp[:, 2, :], sp[:, 3, :], sp[:, 4, :]
                ch.link(dve.tensor_scalar(r, u, 2.0, None, ALU.add))
                ch.link(dve.reciprocal(r, r))
                ch.link(dve.tensor_tensor(r, r, u, ALU.mult))
                ch.link(dve.tensor_tensor(r2, r, r, ALU.mult))
                ch.link(dve.tensor_scalar(p, r2, 1.0 / 15, None, ALU.mult))
                for k in (13, 11, 9, 7, 5, 3):
                    ch.link(dve.scalar_tensor_tensor(p, p, 1.0 / k, r2, ALU.add, ALU.mult))
                ch.link(dve.scalar_tensor_tensor(p, p, 1.0, r, ALU.add, ALU.mult))
                ch.link(dve.scalar_tensor_tensor(flat(dt[:, q % 2, :, :]), p, 2.0, sp[:, 5, :], ALU.mult, ALU.add))
                dve.tensor_tensor(av[:, q % 2, :, :], dt[:, q % 2, :, :], neg_a.unsqueeze(1).to_broadcast([P, Q, NH]), ALU.mult).then_inc(s["a"], 1)

            def low(g, k):
                dve.wait_ge(s["hi"], g * NQ + (k + 1))
                dve.tensor_tensor(x3[0:D, 1, 0, k % SLOTS, :], bank(0)[0:D, :], x3[0:D, 0, 0, k % SLOTS, :].bitcast(F32), ALU.subtract).then_inc(s["b0_ev"], 1)

            def z_silu(g, q, n):
                dve.wait_ge(s["z_th"], g * (2 * NQ) + (2 * q + n + 1))
                need(dve, s["gate"], g * NQ + (q - 1))
                dve.scalar_tensor_tensor(szt[0:D, q % 2, n, :], thz[0:D, :], 1.0, bank(3)[0:D, :], ALU.add, ALU.mult).then_inc(s["z_ev"], 1)

            def gate(g, c):
                dve.wait_ge(s["b0_ev"], before_u(g, c) + 3)
                dve.wait_ge(s["z_ev"], g * (2 * NQ) + (2 * c + 2))
                ch.done(dve.tensor_tensor(g4[0:D, 0, :], g4[0:D, 0, :], szt[0:D, c % 2, 0, :], ALU.mult))
                dve.tensor_tensor(g4[0:D, 1, :], g4[0:D, 1, :], szt[0:D, c % 2, 1, :], ALU.mult).then_inc(s["gate"], 1)

            def quad_rows(g, k):
                group = g + k // NQ
                return xr[:, group, k % NQ * Q:(k % NQ + 1) * Q, :]

            def add_output(g, c):
                dve.wait_ge(s["o_pe"], g * NQ + (c + 1))
                rows = quad_rows(g, c)
                dve.tensor_tensor(rows, rows, bank(3)[:, 0:Q * D].rearrange("p (a b) -> p a b", b=D), ALU.add).then_inc(s["o_add"], 1)

            def norm_y(g, c, part):
                if part == 0:
                    ch.wait()
                layer_norm(dve, ch, lambda n: yy[:, c % 2, n, :], lambda n: u4[:, n, :], Q, INNER, 1e-5, g * NQ + (c + 1), s["u"], part, y_norm)

            def norm_x(g, k, part):
                layer_norm(dve, ch, lambda n: quad_rows(g, k)[:, n, :], lambda n: xn[:, k % 2 * Q + n, :], Q, D, 1e-6, g * NQ + (LN_MIX1 + k + 1), s["ln"], part)

            def step(g, r):
                ch.wait()
                if (c := quad(g, r, 12)) is not None:
                    gate(g, c)
                if (i := row(g, r, 0)) is not None:
                    conv_silu(g, i)
                if (c := quad(g, r, 10)) is not None:
                    norm_y(g, c, 1)
                if (k := quad(g, r, -5)) is not None:
                    norm_x(g, k, 1)
                if (c := quad(g, r, 5)) is not None:
                    weigh(g, c)
                if (q := quad(g, r, 4)) is not None:
                    z_silu(g, q, 0)
                if (i := row(g, r, 6)) is not None:
                    gather(g, i)
                if (q := quad(g, r, 5)) is not None:
                    z_silu(g, q, 1)
                if (k := quad(g, r, -T_AHEAD)) is not None:
                    low(g, k)
                if (c := quad(g, r, 14)) is not None:
                    add_output(g, c)
                if (q := quad(g, r, 4)) is not None:
                    time_steps(g, q)
                if (i := row(g, r, 5)) is not None:
                    attend(g, i)
                if (c := quad(g, r, 9)) is not None:
                    norm_y(g, c, 0)
                if (k := quad(g, r, -6)) is not None:
                    norm_x(g, k, 0)
                if (q := quad(g, r, 3)) is not None:
                    time_steps_begin(g, q)

            steps_of_rows(dve, step, lambda g: ch.enter(g, SSMC), lambda: ch.leave(G - 1, SSMC))
            dve.wait_ge(s["o_add"], G * NQ)

        @block.vector
        def _(dve):
            ch = Chain(dve, dve_chain)
            ch.done(dve.memset(xt0[D:D + 1, :], 1.0))
            ch.done(dve.memset(rhs0[D:D + 1, 0:D], 0.0))
            dve.wait_ge(mix_in, 16 * 23)
            ch.done(dve.tensor_copy(rhs0[0:D, 0:D], wo_t[0:D, :]))
            dve.wait_ge(prep_pe, 1)
            ch.done(dve.tensor_copy(rhs0[0:D, D:2 * D], bank(5)[0:D, 0:D]))
            ch.wait()
            dve.tensor_tensor(rhs0[D:D + 1, D:2 * D], bank(5)[D:D + 1, 0:D], bo[D:D + 1, :], ALU.add).then_inc(prep_done, 1)
            dve.sem_inc(m_w_add, NQ)

            def normalise(g):
                dve.wait_ge(x_in, g * 64 + 64)
                layer_norm(dve, ch, lambda r: xr[:, g, r, :], lambda r: xn[:, r, :], SIDE, D, 1e-6, g + 1, m_ln)

            def group(g):
                dve.wait_ge(m_v_ev, g * (SIDE // 2) + SIDE // 2)
                ch.done(dve.tensor_copy(yb[:, 0, :].rearrange("p (e h) -> p e h", e=2), vc[:, :, 2 * D:2 * D + 2].rearrange("p h e -> p e h")))
                ch.link(dve.tensor_copy(yb[:, 1, :].rearrange("p (e h) -> p e h", e=2), vc[:, :, 2 * D + 2:NV].rearrange("p h e -> p e h")))
                dve.transpose(ywt, yb[:, 1, :]).then_inc(m_yb, 1)
                ch.done(dve.transpose(vh[:, :, :].rearrange("p w d -> p d w"), vc[:, :, 0:D].rearrange("p h d -> p d h")))
                ch.done(dve.tensor_tensor(xr[:, g, :, :], xr[:, g, :, :], vc[:, :, D:2 * D], ALU.add))
                for m in range(2):
                    z = bank(6 - 2 * m, 2).rearrange("p (i j) -> p i j", j=SIDE)
                    dve.wait_ge(m_z_pe, g * 2 + (m + 1))
                    ch.link(dve.tensor_reduce(row_max, z, AX.X, ALU.max))
                    dve.tensor_tensor(sc[:, :, :], z, row_max.unsqueeze(2).to_broadcast([P, SIDE, SIDE]), ALU.subtract).then_inc(m_sub, 1)
                    dve.wait_ge(m_exp, g * 2 + (m + 1))
                    ch.link(dve.tensor_reduce(row_sum, at[:, m, :, :], AX.X, ALU.add))
                    ch.link(dve.reciprocal(row_inv, row_sum))
                    ch.link(dve.tensor_tensor(sc[:, :, :], at[:, m, :, :], row_inv.unsqueeze(2).to_broadcast([P, SIDE, SIDE]), ALU.mult))
                    dve.transpose(at[:, m, :, :], sc[:, :, :]).then_inc(m_at, 1)
                ch.wait()
                if not isinstance(g, int):
                    normalise(g + 1)
                for q in range(NQ):
                    dve.wait_ge(m_w_pe, g * NQ + (q + 1))
                    rows = xr[:, g, Q * q:Q * q + Q, :]
                    dve.tensor_tensor(rows, rows, bank(2 + q % 2)[:, 0:Q * D].rearrange("p (a b) -> p a b", b=D), ALU.add).then_inc(m_w_add, 1)
                dve.wait_ge(m_w_add, g * NQ + 2 * NQ)
                dve.wait_ge(m_b01_ev, g * (2 * NQ) + (2 + 2 * NQ))
                ch.link(dve.transpose(ohw[:, :, :].rearrange("p h d -> p d h"), oh[:, :, :].rearrange("p w d -> p d w")))
                ch.link(dve.tensor_tensor(xr[:, g, :, :], xr[:, g, :, :], ohw[:, :, :], ALU.add))

            normalise(0)
            with dve.Fori(0, G - 1) as g:
                ch.enter(g, MIXC)
                group(g)
                ch.leave(G - 1, MIXC)
            group(G - 1)

            def ffn(f, ln_before):
                def token_rows(t):
                    return xr[:, :, :, :].rearrange("p g h d -> p (g h) d").rearrange("p (t q) d -> p t q d", q=Q)[:, t, :, :]

                def norm(t, part):
                    layer_norm(dve, ch, lambda r: token_rows(t)[:, r, :], lambda r: xn4[:, r, :], Q, D, 1e-5, t + (ln_before + 1), f["ln"], part)

                def combine(t, par, e):
                    dve.wait_ge(f["yt_pe"], t * NEXP + (e + 1))
                    need(dve, f["comb"], t * NEXP + e)
                    for i in range(Q):
                        row = token_rows(t)[:, i, :]
                        ins = dve.scalar_tensor_tensor(row, bank(6 + e % 2)[:, i * D:(i + 1) * D], gm[:, par, i, e:e + 1], row, ALU.mult, ALU.add)
                    ins.then_inc(f["comb"], 1)

                def over(a):
                    return a.unsqueeze(2).to_broadcast([P, Q, NEXP])

                def gate_distance(t):
                    sco = bank(5)[:, 0:Q * NEXP].rearrange("p (a b) -> p a b", b=NEXP)
                    dve.wait_ge(f["gate_pe"], t + 1)
                    ch.link(dve.tensor_reduce(gcol[:, 0, :], sco, AX.X, ALU.max))
                    dve.tensor_tensor(gd[:, :, :], sco, over(gcol[:, 0, :]), ALU.subtract).then_inc(f["gate_d"], 1)

                def gate_rank(t):
                    dve.wait_ge(f["gate_d"], t + 1)
                    other = gd[:, :, :].unsqueeze(2).to_broadcast([P, Q, NEXP, NEXP])
                    own = gd[:, :, :].unsqueeze(3).to_broadcast([P, Q, NEXP, NEXP])
                    ch.done(dve.tensor_tensor(gcmp[:, :, :, :], other, own, ALU.is_gt))
                    ch.link(dve.tensor_tensor(geq[:, :, :, :], other, own, ALU.is_equal))
                    ch.link(dve.tensor_tensor(geq[:, :, :, :], geq[:, :, :, :], lower.unsqueeze(1).to_broadcast([P, Q, NEXP, NEXP]), ALU.mult))
                    ch.link(dve.tensor_tensor(gcmp[:, :, :, :], gcmp[:, :, :, :], geq[:, :, :, :], ALU.add))
                    ch.done(dve.tensor_reduce(gmask[:, :, :], gcmp[:, :, :, :], AX.X, ALU.add))

                def gate_exp(t):
                    dve.wait_ge(f["tanh"], t + 1)
                    ch.link(dve.tensor_scalar(gn[:, :, :], gth[:, :, :], -1.0, 1.0, ALU.mult, ALU.add))
                    ch.link(dve.reciprocal(gn[:, :, :], gn[:, :, :]))
                    ch.link(dve.scalar_tensor_tensor(ge[:, :, :], gth[:, :, :], 1.0, gn[:, :, :], ALU.add, ALU.mult))
                    ch.done(dve.tensor_reduce(gcol[:, 1, :], ge[:, :, :], AX.X, ALU.add))
                    ch.link(dve.scalar_tensor_tensor(gn[:, :, :], gmask[:, :, :], 2.0, ge[:, :, :], ALU.is_lt, ALU.mult))

                def gate_weights(t, par):
                    ch.link(dve.tensor_reduce(gcol[:, 2, :], gn[:, :, :], AX.X, ALU.add))
                    ch.link(dve.scalar_tensor_tensor(gcol[:, 3, :], gcol[:, 1, :], 1e-9, gcol[:, 2, :], ALU.mult, ALU.add))
                    ch.link(dve.reciprocal(gcol[:, 0, :], gcol[:, 3, :]))
                    ch.done(dve.tensor_tensor(gm[:, par, :, :], gn[:, :, :], over(gcol[:, 0, :]), ALU.mult))

                def columns(t, par):
                    dve.wait_ge(f["xt_pe"], t + 1)
                    need(dve, f["up"], t * NC - NC)
                    split(dve, ch, bank(4)[0:D, :], xtr[0:D, :, par, :]).then_inc(f["xt"], 1)

                def tile(t, par=None):
                    first, last = (isinstance(t, int) and t == n for n in (0, NT - 1))
                    par = t % 2 if par is None else par
                    if not isinstance(t, int):
                        ch.enter(t - 2, FFNC)
                    for c in range(2 * NC if last else NC):
                        if c < NC and c not in POOL_CHUNKS:
                            dve.wait_ge(f["gelu"], t * NC + (c + 1))
                            r = c % RING
                            dve.tensor_tensor(hidr[:, 1, r, :], hid[:, r, :], hidr[:, 0, r, :].bitcast(F32), ALU.subtract).then_inc(f["low"], 1)
                        if c == 0:
                            gate_distance(t)
                            if not last:
                                norm(t + 1, 0)
                        if c == 2:
                            gate_rank(t)
                            if not last:
                                norm(t + 1, 1)
                        if c == 6:
                            gate_exp(t)
                            gate_weights(t, par)
                        if c == 7 and not last:
                            columns(t + 1, 1 - par)
                        for before, e in experts_due(t, c, LAG + 3):
                            if e == 0:
                                ch.wait()
                            combine(t - before, 1 - par if before else par, e)
                    if not isinstance(t, int):
                        if par == 0:
                            assert ch.n == FFNC, ch.n
                            ch.base, ch.n = ch.start, 0
                        else:
                            ch.leave(NT - 4, FFNC)

                dve.wait_ge(stage_end, 1 if ln_before == LN_FFN0 else 3)
                dve.wait_ge(ffn_in, 96 if ln_before == LN_FFN0 else 192)
                ch.done(dve.memset(xtr[D:D + 1, 0, :, :].bitcast(F32), 1.0))
                ch.done(dve.memset(xtr[D:D + 1, 1, :, :].bitcast(F32), 0.0))
                ch.done(split(dve, ch, w1[:, :], w1r[0:D + 1]))
                ch.done(split(dve, ch, w2[:, :, :], w2r))
                ch.link(split(dve, ch, gw[:, :], gwr[0:D + 1]))
                norm(0, 0)
                norm(0, 1)
                columns(0, 0)
                tiles(dve, tile)
                dve.wait_ge(f["comb"], NT * NEXP)

            dve.sem_inc(stage_end, 1)
            if stop >= 2:
                ffn(ffn_sems[0], LN_FFN0)
                dve.sem_inc(stage_end, 1)
            if stop >= 3:
                mixer1(dve, ch)
                dve.sem_inc(stage_end, 1)
            if stop >= 4:
                ffn(ffn_sems[1], LN_FFN1)
                dve.sem_inc(stage_end, 1)


_INPUTS = ["consts", "x", "Wc", "bc", "WoT", "bo", "W1T", "W2T", "b2z", "Win_z", "Win_dt", "dt_bias", "Win_x", "b_conv",
           "W_conv", "A_log", "D_param", "gamma", "beta", "W_out"]
_FFN = ["w1", "b1", "w2", "b2T", "gate_w", "gate_b"]


def kernel(**inputs):
    import numpy as np
    import concourse.bacc as bacc
    from concourse.bass_utils import run_bass_kernel_spmd

    a = {k: np.asarray(v) for k, v in inputs.items()}
    k, l = np.arange(P)[:, None], np.arange(P)[None, :]
    one = k // SIDE == l // SIDE
    e, o = np.arange(NEXP)[:, None], np.arange(NEXP)[None, :]
    consts = np.concatenate([k == l, one & (k <= l), one & (k > l), one, k % SIDE <= np.arange(SIDE)[None, :],
                             np.broadcast_to((o < e).reshape(1, 16), (P, 16))], axis=1).astype(np.float32)

    def mixing(w):
        return w.reshape(SEG, P, SEG).transpose(0, 2, 1)

    w_in = a["L1_conv_W_in"]
    arrays = {
        "consts": consts, "x": a["x"], "Wc": a["L0_conv_Wc"], "bc": a["L0_conv_bc"].reshape(D, 1),
        "WoT": a["L0_conv_Wo"].T, "bo": a["L0_conv_bo"].reshape(1, D),
        "W1T": np.concatenate([np.concatenate([a["L0_conv_W1h"].T, a["L0_conv_W1w"].T], 1),
                               np.concatenate([a["L0_conv_b1h"], a["L0_conv_b1w"]]).reshape(1, 2 * E0)], 0),
        "W2T": np.stack([mixing(a["L0_conv_W2h"]), mixing(a["L0_conv_W2w"])]),
        "b2z": np.stack([a["L0_conv_b2h"], a["L0_conv_b2w"]]).reshape(2, 1, SIDE * SIDE),
        "Win_z": w_in[:, :INNER].reshape(D, 2, D), "Win_x": w_in[:, INNER:INNER + CONV], "Win_dt": w_in[:, INNER + CONV:],
        "dt_bias": a["L1_conv_dt_bias"].reshape(1, NH), "b_conv": a["L1_conv_b_conv"].reshape(1, CONV),
        "W_conv": a["L1_conv_W_conv"].reshape(TAPS, CONV), "A_log": a["L1_conv_A_log"], "D_param": a["L1_conv_D_param"],
        "gamma": a["L1_conv_gamma"].reshape(2, D).T, "beta": a["L1_conv_beta"].reshape(2, D).T,
        "W_out": a["L1_conv_W_out"].reshape(2, D, D).transpose(1, 0, 2),
    }
    for n in range(2):
        w = {x: a[f"L{n}_ffn_{x}"] for x in ("w1", "b1", "w2", "b2", "gate_w", "gate_b")}
        arrays |= {f"{n}_w1": w["w1"], f"{n}_b1": w["b1"].reshape(1, NEXP * HID), f"{n}_w2": w["w2"], f"{n}_b2T": w["b2"].T,
                   f"{n}_gate_w": w["gate_w"], f"{n}_gate_b": w["gate_b"].reshape(1, NEXP)}
    arrays = {f"in_{x}": np.ascontiguousarray(v) for x, v in arrays.items()}
    nc = bacc.Bacc("TRN2", target_bir_lowering=False, num_devices=1)
    aps = {x: nc.dram_tensor(x, v.shape, mybir.dt.from_np(v.dtype), kind="ExternalInput").ap() for x, v in arrays.items()}
    out = nc.dram_tensor("out", (IMG, SIDE, SIDE, D), F32, kind="ExternalOutput").ap()
    inp = {x: aps[f"in_{x}"] for x in _INPUTS}
    inp["ffn"] = [{x: aps[f"in_{n}_{x}"] for x in _FFN} for n in range(2)]
    metaformer(nc, inp, out)
    r = run_bass_kernel_spmd(nc, [arrays], core_ids=[0])
    return r.results[0]["out"]
```

```python
from contextlib import ExitStack

import concourse.bass as bass
from concourse import mybir

ALU = mybir.AluOpType
ACT = mybir.ActivationFunctionType
AX = mybir.AxisListType
F32 = mybir.dt.float32
F32R = mybir.dt.float32r

P = 128
IMG, SIDE, D = 16, 32, 96
PACK = P // SIDE
G = IMG // PACK
Q = 4
NQ = SIDE // Q
NT = G * NQ
BANK = 512
E0 = 2
SEG = 8
NV = 2 * D + 2 * E0
NEXP, HID = 4, 384
NC = NEXP * HID // P
CPE = HID // P
INNER, NH, HD, NS = 192, 12, 16, 16
CONV = INNER + 2 * NS
XB = CONV + NS
TAPS = 9
CENTRE = TAPS // 2
CONSTS = 4 * P + SIDE + 16
ARENA = 20000
RING = 6
LAG = RING - 1
SPLITS = [0, NC * P, NC * P + NC * D, NC * P + NC * D + 2 * BANK, NC * P + NC * D + (2 + RING) * BANK]
SPLITS.append(SPLITS[-1] + NEXP)
SLOTS = 2
CONVD = CONV + NH
PARTS = [0, 2 * SLOTS * Q * P, 3 * SLOTS * Q * P]
ROWS3 = 3
for n in (2 * ROWS3 * CONVD, ROWS3 * CONVD, ROWS3 * CONV, INNER):
    PARTS.append(PARTS[-1] + n)
SPLIT = max(SPLITS[-1], PARTS[-1])
POOL_CHUNKS = [1, 3, 5, 7, 9, 11]
HEAD, TAIL = 2 * Q, SIDE // 2
CHAIN_MIX0, CHAIN_FFN, CHAIN_MIX1 = 52, 26, 416


def need(eng, sem, count):
    if not isinstance(count, int) or count > 0:
        eng.wait_ge(sem, count)


def tiles(eng, tile):
    tile(0)
    tile(1)
    with eng.Fori(1, NT // 2 - 1) as pair:
        tile(pair * 2, 0)
        tile(pair * 2 + 1, 1)
    tile(NT - 2)
    tile(NT - 1)


class Chain:

    def __init__(self, eng, sem):
        self.eng, self.sem, self.base, self.n = eng, sem, 0, 0

    def done(self, ins):
        ins.then_inc(self.sem, 1)
        self.n += 1

    def wait(self):
        self.eng.wait_ge(self.sem, self.base + self.n)

    def link(self, ins):
        self.done(ins)
        self.wait()

    def enter(self, i, per):
        self.start = self.base + self.n
        self.base, self.n = i * per + self.start, 0

    def leave(self, rounds, per):
        assert self.n == per, (self.n, per)
        self.base, self.n = self.start + rounds * per, 0


def metaformer(nc, inp, out):
    with ExitStack() as ctx:
        def sb(name, shape, dt=F32):
            return ctx.enter_context(nc.sbuf_tensor(name, shape, dt))

        def sem(name):
            return ctx.enter_context(nc.semaphore(name))

        ps = ctx.enter_context(nc.psum_tensor("ps", [P, 8, BANK], F32))

        xr = sb("residual", [P, G, SIDE, D])
        consts = sb("consts", [P, CONSTS])
        ident = consts[:, 0:P]
        upto = consts[:, P:2 * P]
        later = consts[:, 2 * P:3 * P]
        whole = consts[:, 3 * P:4 * P]
        tri = consts[:, 4 * P:4 * P + SIDE]
        lower = consts[:, 4 * P + SIDE:CONSTS].rearrange("p (a b) -> p a b", b=NEXP)
        stats = sb("stats", [P, SIDE, 6])
        moments = sb("moments", [P, 6, SIDE])
        stats_y = sb("stats_y", [P, Q, 6])
        moments_y = sb("moments_y", [P, 6, Q])
        half_neg = sb("half_neg", [P, SIDE])
        w1 = sb("w1", [D + 1, NC * P])
        w2 = sb("w2", [P, NC, D])
        b2 = sb("b2", [D, NEXP])
        gw = sb("gw", [D + 1, NEXP])
        xn = sb("xn", [P, SIDE, D])
        rounded = sb("rounded", [P, 2, SPLIT], F32R)
        w1r, w2r, xtr, hidr, gwr = (rounded[:, :, a:b] for a, b in zip(SPLITS[:-1], SPLITS[1:]))
        w2r = w2r.rearrange("p s (c d) -> p s c d", d=D)
        hidr = hidr.rearrange("p s (r n) -> p s r n", r=RING)
        xtr = xtr.rearrange("p s (t n) -> p s t n", t=2)
        x3, rest, wtap, wrest, wright, wz = (rounded[:, :, a:b] for a, b in zip(PARTS[:-1], PARTS[1:]))
        x3 = x3.rearrange("p s (n k t) -> p s n k t", n=2, k=SLOTS)
        rest = rest[:, 0, :].rearrange("p (k t) -> p k t", k=SLOTS)
        wtap = wtap.rearrange("p s (n y c) -> p s n y c", n=2, y=ROWS3)
        wrest = wrest[:, 0, :].rearrange("p (y c) -> p y c", y=ROWS3)
        wright = wright.rearrange("p s (y c) -> p s y c", y=ROWS3)
        wz = wz.rearrange("p s (n d) -> p s n d", n=2)
        arena = sb("arena", [P, ARENA])
        top = [0]

        def part(*shape):
            n = 1
            for s in shape:
                n *= s
            ap = arena[:, top[0]:top[0] + n]
            top[0] += n
            assert top[0] <= ARENA, top[0]
            names = "abcd"[:len(shape)]
            if len(shape) == 1:
                return ap
            return ap.rearrange(f"p ({' '.join(names)}) -> p {' '.join(names)}", **dict(zip(names[1:], shape[1:])))

        top[0] = 0
        wc = part(D + 1)
        wo_t = part(D)
        bo = part(D)
        rhs0 = part(NV)
        w2z = part(2, SIDE * SIDE)
        xt0 = part(2 * BANK)
        vc = part(SIDE, NV)
        vh = part(SIDE, D)
        oh = part(SIDE, D)
        yb = part(2, 2 * SIDE)
        ywt = part(2 * SIDE)
        yt = part(2, P)
        row_max = part(SIDE)
        row_sum = part(SIDE)
        row_inv = part(SIDE)
        sc = part(SIDE, SIDE)
        at = part(2, SIDE, SIDE)
        ohw = vh

        top[0] = 0
        xn4 = part(Q, D)
        hid = part(RING, BANK)
        yte = part(2, BANK)
        gd = part(Q, NEXP)
        gth = part(Q, NEXP)
        gn = part(Q, NEXP)
        ge = part(Q, NEXP)
        gmask = part(Q, NEXP)
        gcmp = part(Q, NEXP, NEXP)
        geq = part(Q, NEXP, NEXP)
        gcol = part(4, Q)
        gm = part(2, Q, NEXP)

        prep = top[0]
        wz0 = part(2, D)
        winx = part(CONV)
        wcv = part(TAPS, CONV)
        wtap0 = part(TAPS, CONVD)
        a_log = part(NH)
        a_exp = part(NH)
        keep = top[0]
        neg_a = part(NH)
        d_par = part(NH)
        gamma = part(2)
        beta = part(2)
        wout = part(2, D)
        rest_of_arena = top[0]
        top[0] = 0
        xbc = part(2, Q, XB)
        szt = part(2, 2, BANK)
        yy = part(2, Q, INNER)
        dtr = part(2, Q, NH)
        th = part(CONV)
        thz = part(BANK)
        ll = part(2, NH, SIDE)
        mm = part(2, NH, SIDE)
        gmk = part(SIDE)
        st = part(NH, HD)
        st1 = part(NH, HD)
        u4 = part(Q, INNER)
        assert 2 * Q * XB <= prep and top[0] <= keep
        top[0] = rest_of_arena
        sp = part(6, Q * NH)
        dt = part(2, Q, NH)
        av = part(2, Q, NH)
        ex3 = part(2, 3, Q, NH)
        wdt = part(Q, NH)
        bt = part(Q, SIDE)
        ct = part(2, Q, SIDE)
        b_apart = part(2, Q, P)
        xdt = part(2, Q, NH, HD)
        xw = part(2, Q, NH, HD)
        xd = part(2, Q, NH, HD)
        g4 = part(2, BANK)
        rr = part(Q, NH, SIDE)
        spare = xn[:, 2 * Q:, :].rearrange("p a b -> p (a b)")
        b_rows, c_apart = (spare[:, n * 2 * Q * P:(n + 1) * 2 * Q * P].rearrange("p (k q t) -> p k q t", k=2, q=Q) for n in range(2))

        const_in, mix_in, ffn_in, x_in = sem("const_in"), sem("mix_in"), sem("ffn_in"), sem("x_in")
        ssm_in, x_out = sem("ssm_in"), sem("x_out")
        dve_chain, pool_chain, a_exp_ready = sem("dve_chain"), sem("pool_chain"), sem("a_exp_ready")
        ones_set, prep_pe, prep_done = sem("ones_set"), sem("prep_pe"), sem("prep_done")
        stage_end, waited = sem("stage_end"), sem("waited")
        var_ready, rstd_ready = sem("var_ready"), sem("rstd_ready")
        m_ln, m_b01_pe, m_b01_ev = sem("m_ln"), sem("m_b01_pe"), sem("m_b01_ev")
        m_v_pe, m_v_ev, m_yb, m_yt_pe, m_yt_ev = (sem(n) for n in ("m_v_pe", "m_v_ev", "m_yb", "m_yt_pe", "m_yt_ev"))
        m_z_pe, m_sub, m_exp, m_at, m_w_pe, m_w_add = (sem(n) for n in ("m_z_pe", "m_sub", "m_exp", "m_at", "m_w_pe", "m_w_add"))
        ffn_sems = []
        for l in range(2):
            ffn_sems.append({n: sem(f"f{l}_{n}") for n in (
                "parts", "ln", "xt_pe", "xt", "gate_pe", "gate_d", "tanh", "up", "gelu", "low", "low_pool", "down", "y_ev", "yt_pe", "comb")})
        s = {n: sem("s_" + n) for n in (
            "ln", "b0_pe", "b0_ev", "hi", "x3", "cv", "cv_th", "cv_ev", "z_pe", "z_th", "z_ev", "raw", "exp_dt", "a", "cs", "ex",
            "w", "folded", "bt", "apart", "r", "xdt", "xw", "xd", "d_pe", "l", "m", "y_pe", "y", "ds_pe", "s1", "state", "u", "gate", "o_pe", "o_add", "var_y", "rstd_y")}

        block = ctx.enter_context(nc.Block())

        def bank(b, n=1):
            return ps[:, b:b + n, :].rearrange("p a b -> p (a b)")

        def experts_due(t, c, lag):
            first, last = (isinstance(t, int) and t == n for n in (0, NT - 1))
            for before in (0, 1):
                e, n = divmod(c - lag + NC * before, CPE)
                if n == CPE - 1 and 0 <= e < NEXP and not (before and (first or c >= NC)):
                    yield before, e

        def layer_norm(dve, ch, src, dst, n, width, which_eps, count, ready, part=None, own=None, rows=None):
            if part != 1:
                row_stats(dve, ch, src, n, width, which_eps, own or token_norm)
            if part == 0:
                return
            _, mom, _, has_rstd = own or token_norm
            dve.wait_ge(has_rstd, count)
            mo = mom[:, :, 0:n]
            for r in rows or range(n):
                i = dve.tensor_scalar(dst(r), src(r), mo[:, 0, r:r + 1], mo[:, 5, r:r + 1], ALU.subtract, ALU.mult)
                if ready is not None and (r + 1) % Q == 0:
                    i.then_inc(ready, 1)

        token_norm = (stats, moments, var_ready, rstd_ready)
        y_norm = (stats_y, moments_y, s["var_y"], s["rstd_y"])

        def row_stats(dve, ch, src, n, width, which_eps, own):
            sums, mom, has_var, _ = own
            for r in range(n):
                i = dve.bn_stats(sums[:, r, :], src(r))
                ch.done(i)
            ch.wait()
            sv = sums[:, 0:n, :]
            mo = mom[:, :, 0:n]
            ch.done(dve.tensor_tensor(mo[:, 0, :], sv[:, :, 1], sv[:, :, 4], ALU.add))
            ch.done(dve.tensor_tensor(mo[:, 1, :], sv[:, :, 1], sv[:, :, 4], ALU.subtract))
            ch.link(dve.tensor_tensor(mo[:, 2, :], sv[:, :, 2], sv[:, :, 5], ALU.add))
            ch.done(dve.tensor_scalar(mo[:, 0, :], mo[:, 0, :], 0.5, None, ALU.mult))
            ch.link(dve.tensor_tensor(mo[:, 1, :], mo[:, 1, :], mo[:, 1, :], ALU.mult))
            ch.link(dve.scalar_tensor_tensor(mo[:, 3, :], mo[:, 1, :], width / 4.0, mo[:, 2, :], ALU.mult, ALU.add))
            dve.tensor_scalar(mo[:, 4, :], mo[:, 3, :], 1.0 / width, which_eps, ALU.mult, ALU.add).then_inc(has_var, 1)

        def rstd(pool, n, count, own=None):
            _, mom, has_var, has_rstd = own or token_norm
            pool.wait_ge(has_var, count)
            pool.tensor_tensor(mom[:, 5, 0:n], mom[:, 4, 0:n], half_neg[:, 0:n], ALU.pow).then_inc(has_rstd, 1)

        LN_FFN0 = G
        LN_MIX1 = LN_FFN0 + NT
        LN_FFN1 = LN_MIX1 + NT

        def steps_of_rows(eng, step, enter=None, leave=None, weights=None):
            for r in range(-HEAD, TAIL):
                if r == 0 and weights:
                    weights()
                step(0, r)
            with eng.Fori(0, G - 1) as g:
                if enter:
                    enter(g)
                for r in range(TAIL, TAIL + SIDE):
                    step(g, r)
                if leave:
                    leave()
            for r in range(TAIL + SIDE * (G - 1), SIDE * G + TAIL):
                step(0, r)

        def row(g, r, lag):
            i = r - lag
            return i if not isinstance(g, int) or 0 <= i < G * SIDE else None

        def quad(g, r, lag):
            i = row(g, r, lag)
            return None if i is None or i % Q else i // Q

        T_AHEAD, U_LAG = 3, 11
        BETWEEN = (T_AHEAD + U_LAG) // Q + 1

        def before_t(g, k):
            return g * (3 * NQ) + (k + 2 * (max(0, k - (BETWEEN - 1)) if isinstance(g, int) else k - (BETWEEN - 1)))

        def before_u(g, c):
            return g * (3 * NQ) + (2 * c + (min(c + BETWEEN, NT) if isinstance(g, int) else c + BETWEEN))

        def split(eng, ch, src, dst):
            ch.link(eng.tensor_copy(dst[:, 0], src))
            return eng.tensor_tensor(dst[:, 1], src, dst[:, 0].bitcast(F32), ALU.subtract)

        @block.sync
        def _(sp_):
            sp_.dma_start(consts[:, :], inp["consts"]).then_inc(const_in, 16)
            for g in range(G):
                if g:
                    sp_.wait_ge(x_in, 64 * g)
                for b in range(PACK):
                    sp_.dma_start(xr[b * SIDE:(b + 1) * SIDE, g, :, :],
                                  inp["x"][g * PACK + b].rearrange("h w d -> w h d")).then_inc(x_in, 16)
                if g == 0:
                    sp_.dma_start(wc[0:D, 0:D], inp["Wc"]).then_inc(mix_in, 16)
                    sp_.dma_start(wc[0:D, D:D + 1], inp["bc"]).then_inc(mix_in, 16)
                    sp_.dma_start(wo_t[0:D, :], inp["WoT"]).then_inc(mix_in, 16)
                    sp_.dma_start(bo[D:D + 1, :], inp["bo"]).then_inc(mix_in, 16)
                    sp_.dma_start(rhs0[0:D + 1, 2 * D:NV], inp["W1T"]).then_inc(mix_in, 16)
                    sp_.wait_ge(ones_set, 1)
                    for m in range(2):
                        for c in range(SEG):
                            sp_.dma_start(w2z[8 * c:8 * c + 8, m, c * P:(c + 1) * P], inp["W2T"][m, c]).then_inc(mix_in, 16)
                        sp_.dma_start(w2z[64:65, m, :], inp["b2z"][m]).then_inc(mix_in, 16)

            def ffn_weights(l):
                w = inp["ffn"][l]
                sp_.dma_start(w1[0:D, :].rearrange("p (e h) -> p e h", h=HID), w["w1"].rearrange("e d h -> d e h")).then_inc(ffn_in, 16)
                sp_.dma_start(w1[D:D + 1, :], w["b1"]).then_inc(ffn_in, 16)
                sp_.dma_start(w2[:, :, :], w["w2"].rearrange("e (c p) d -> p (e c) d", p=P)).then_inc(ffn_in, 16)
                sp_.dma_start(b2[:, :], w["b2T"]).then_inc(ffn_in, 16)
                sp_.dma_start(gw[0:D, :], w["gate_w"]).then_inc(ffn_in, 16)
                sp_.dma_start(gw[D:D + 1, :], w["gate_b"]).then_inc(ffn_in, 16)

            ffn_weights(0)
            sp_.wait_ge(stage_end, 1)
            sp_.dma_start(wz0[0:D, :, :], inp["Win_z"]).then_inc(ssm_in, 16)
            sp_.dma_start(wtap0[0:D, CENTRE, CONV:CONV + NH], inp["Win_dt"]).then_inc(ssm_in, 16)
            for n in range(2):
                sp_.dma_start(wtap0[D + n:D + n + 1, CENTRE, CONV:CONV + NH], inp["dt_bias"]).then_inc(ssm_in, 16)
            sp_.dma_start(winx[0:D, :], inp["Win_x"]).then_inc(ssm_in, 16)
            for n in range(2):
                sp_.dma_start(wtap0[D + n:D + n + 1, CENTRE, 0:CONV], inp["b_conv"]).then_inc(ssm_in, 16)
            sp_.dma_start(wcv[0:D, :, :], inp["W_conv"].partition_broadcast(D)).then_inc(ssm_in, 16)
            sp_.dma_start(a_log, inp["A_log"].partition_broadcast(P)).then_inc(ssm_in, 16)
            sp_.dma_start(d_par, inp["D_param"].partition_broadcast(P)).then_inc(ssm_in, 16)
            sp_.dma_start(gamma[0:D, :], inp["gamma"]).then_inc(ssm_in, 16)
            sp_.dma_start(beta[0:D, :], inp["beta"]).then_inc(ssm_in, 16)
            sp_.dma_start(wout[0:D, :, :], inp["W_out"]).then_inc(ssm_in, 16)
            sp_.wait_ge(stage_end, 2)
            ffn_weights(1)
            for g in range(G):
                sp_.wait_ge(ffn_sems[1]["comb"], (g + 1) * NQ * NEXP)
                for b in range(PACK):
                    sp_.dma_start(out[g * PACK + b].rearrange("h w d -> w h d"),
                                  xr[b * SIDE:(b + 1) * SIDE, g, :, :]).then_inc(x_out, 16)
            sp_.wait_ge(stage_end, 4)
            sp_.wait_ge(x_out, 16 * IMG)

        @block.gpsimd
        def _(pool):
            ch = Chain(pool, pool_chain)

            def ffn_parts(l):
                pool.wait_ge(ffn_in, 96 * (l + 1))
                ch.link(split(pool, ch, w1[:, :], w1r[0:D + 1]))
                ch.link(split(pool, ch, gw[:, :], gwr[0:D + 1]))
                split(pool, ch, w2[:, :, :], w2r).then_inc(ffn_sems[l]["parts"], 1)

            def ffn(f, ln_before):
                def tile(t, par=None):
                    par = t % 2 if par is None else par
                    last = isinstance(t, int) and t == NT - 1
                    for n, c in enumerate(POOL_CHUNKS):
                        pool.wait_ge(f["gelu"], t * NC + (c + 1))
                        r = c % RING
                        pool.tensor_tensor(hidr[:, 1, r, :], hid[:, r, :], hidr[:, 0, r, :].bitcast(F32), ALU.subtract).then_inc(f["low_pool"], 1)
                        if n == 0 and not last:
                            rstd(pool, Q, t + (ln_before + 2))
                        if ln_before == LN_FFN0 and isinstance(t, int) and t == NT - 2:
                            fold(n)

                def fold(n):
                    if n == 0:
                        pool.wait_ge(ssm_in, 16 * 13)
                        ch.link(pool.tensor_scalar(winx[0:D, :], winx[0:D, :], 0.5, None, ALU.mult))
                        ch.done(pool.tensor_scalar(wz0[0:D, :, :], wz0[0:D, :, :], 0.5, None, ALU.mult))
                    for t in range(2 * n, min(2 * n + 2, TAPS)):
                        ch.done(pool.tensor_tensor(wtap0[0:D, t, 0:CONV], winx[0:D, :], wcv[0:D, t, :], ALU.mult))
                    if 2 * n < TAPS <= 2 * n + 2:
                        ch.wait()
                        pool.sem_inc(s["folded"], 1)

                rstd(pool, Q, ln_before + 1)
                tiles(pool, tile)

            ch.done(pool.memset(half_neg[:, :], -0.5))
            ch.link(pool.memset(yt[:, :, :], 1.0))
            pool.memset(w2z[:, :, :], 0.0).then_inc(ones_set, 1)
            with pool.Fori(0, G) as g:
                rstd(pool, SIDE, g + 1)
            ffn_parts(0)
            ffn(ffn_sems[0], LN_FFN0)
            pool.wait_ge(stage_end, 2)
            edges = rounded[:, :, 0:PARTS[2]].rearrange("p s (a w) -> p s a w", w=SIDE).bitcast(F32)
            for w in (0, SIDE - 1):
                ch.link(pool.memset(edges[:, :, :, w:w + 1], 0.0))
            ch.done(pool.memset(b_rows, 0.0))
            ch.link(pool.memset(xbc[:, :, :, CONV:XB], 0.0))
            pool.memset(rest[D:D + 2, :, :].bitcast(F32), 1.0).then_inc(ones_set, 1)
            pool.wait_ge(ones_set, 2)

            def steps_from(g, c, i):
                if i == 0:
                    pool.wait_ge(s["a"], g * NQ + (c + 1))
                need(pool, s["d_pe"], g * SIDE + (Q * c + i + 1 - Q))
                pool.tensor_tensor(
                    rr[:, i, :, :], av[:, c % 2, i, :].unsqueeze(2).to_broadcast([P, NH, SIDE]),
                    tri.unsqueeze(1).to_broadcast([P, NH, SIDE]), ALU.mult).then_inc(s["r"], 1)

            def images_apart(g, c):
                pool.wait_ge(s["bt"], g * NQ + (c + 1))
                own = whole.rearrange("p (b n) -> p b n", b=PACK).unsqueeze(1)

                def spread(dst, src, n):
                    dst = dst.rearrange("p q (b n) -> p q b n", b=PACK)[:, :, :, 0:n]
                    shape = [P, Q, PACK, n]
                    return pool.tensor_tensor(dst, src.unsqueeze(2).to_broadcast(shape), own[:, :, :, 0:n].to_broadcast(shape), ALU.mult)

                spread(b_apart[:, c % 2], bt[:, :, :], SIDE)
                spread(c_apart[:, c % 2], ct[:, c % 2], SIDE)
                spread(b_rows[:, c % 2], xbc[:, c % 2, :, INNER:INNER + NS], NS).then_inc(s["apart"], 1)

            def scaled(c, dst, by, done):
                xs = xbc[:, c % 2, :, 0:INNER].rearrange("p q (h e) -> p q h e", e=HD)
                pool.tensor_tensor(dst[:, c % 2], xs, by.unsqueeze(3).to_broadcast([P, Q, NH, HD]), ALU.mult).then_inc(s[done], 1)

            def decayed(g, i):
                pool.wait_ge(s["state"], g * SIDE + (i + 1))
                if i % Q == 0:
                    pool.wait_ge(s["ex"], g * NQ + (i // Q + 1))
                pool.tensor_tensor(st1[:, :, :], st[:, :, :],
                                   ex3[:, i // Q % 2, 2, i % Q, :].unsqueeze(2).to_broadcast([P, NH, HD]), ALU.mult).then_inc(s["s1"], 1)

            def step(g, r):
                if (i := row(g, r, 6)) is not None:
                    decayed(g, i)
                if (c := quad(g, r, 4)) is not None:
                    images_apart(g, c)
                    steps_from(g, c, 0)
                    steps_from(g, c, 1)
                if (c := quad(g, r, 5)) is not None:
                    scaled(c, xdt, dt[:, c % 2, :, :], "xdt")
                    pool.wait_ge(s["w"], g * NQ + (c + 1))
                    scaled(c, xw, wdt[:, :, :], "xw")
                    steps_from(g, c, 2)
                    scaled(c, xd, d_par.unsqueeze(1).to_broadcast([P, Q, NH]), "xd")
                if (c := quad(g, r, 6)) is not None:
                    steps_from(g, c, 3)
                if (c := quad(g, r, 9)) is not None:
                    rstd(pool, Q, g * NQ + (c + 1), y_norm)
                if (k := quad(g, r, -6)) is not None:
                    rstd(pool, Q, g * NQ + (LN_MIX1 + k + 1))

            steps_of_rows(pool, step)
            pool.wait_ge(s["cv"], G * SIDE)
            pool.wait_ge(s["z_pe"], 2 * NT)
            ffn_parts(1)
            ffn(ffn_sems[1], LN_FFN1)

        @block.scalar
        def _(act):
            act.sem_inc(m_b01_ev, 2)
            with act.Fori(0, G) as g:
                def evacuate(k, dst):
                    act.wait_ge(m_b01_pe, g * (2 * NQ) + (k + 1))
                    act.copy(dst, bank(k % 2)[0:dst.shape[0], 0:dst.shape[1]]).then_inc(m_b01_ev, 1)

                evacuate(0, xt0[0:D, 0:BANK])
                for r in range(SIDE // 2):
                    q = r // 2 + 1
                    if r % 2 == 0 and q < NQ:
                        evacuate(q, xt0[0:D, q % 2 * BANK:(q % 2 + 1) * BANK])
                    act.wait_ge(m_v_pe, g * (SIDE // 2) + (r + 1))
                    act.copy(vc[:, 2 * r:2 * r + 2, :], bank(2 + r % 2).rearrange("p (a b) -> p a b", a=2)[:, :, 0:NV]).then_inc(m_v_ev, 1)
                act.wait_ge(m_yt_pe, g + 1)
                act.copy(yt[0:64, :, :], bank(4)[0:64, 0:2 * P].rearrange("p (a b) -> p a b", a=2)).then_inc(m_yt_ev, 1)
                for m in range(2):
                    act.wait_ge(m_sub, g * 2 + (m + 1))
                    act.activation(at[:, m, :, :], sc[:, :, :], ACT.Exp).then_inc(m_exp, 1)
                for q in range(NQ):
                    evacuate(NQ + q, oh[:, Q * q:Q * q + Q, :].rearrange("p a b -> p (a b)"))

            def ffn(f):
                def tile(t, par=None):
                    def y_out(t, e):
                        act.wait_ge(f["down"], t * NC + CPE * (e + 1))
                        need(act, f["yt_pe"], t * NEXP + (e - 1))
                        act.activation(yte[0:D, e % 2, :], bank(2 + e % 2)[0:D, :], ACT.Identity, bias=b2[:, e:e + 1]).then_inc(f["y_ev"], 1)

                    for c in range(NC):
                        act.wait_ge(f["up"], t * NC + (c + 1))
                        need(act, f["down"], t * NC + (c + 1 - RING))
                        act.activation(hidr[:, 0, c % RING, :], bank(c % 2), ACT.Gelu)
                        act.activation(hid[:, c % RING, :], bank(c % 2), ACT.Gelu).then_inc(f["gelu"], 1)
                        if c == 1:
                            act.wait_ge(f["gate_d"], t + 1)
                            act.activation(gth[:, :, :], gd[:, :, :], ACT.Tanh, scale=0.5).then_inc(f["tanh"], 1)
                        for before, e in experts_due(t, c, LAG + 1):
                            y_out(t - before, e)
                    if isinstance(t, int) and t == NT - 1:
                        for c in range(NC, 2 * NC):
                            for before, e in experts_due(t, c, LAG + 1):
                                y_out(t, e)

                tiles(act, tile)

            act.wait_ge(stage_end, 1)
            act.wait_ge(ffn_in, 16 * 6)
            ffn(ffn_sems[0])
            act.wait_ge(ssm_in, 16 * 13)
            act.activation(a_exp, a_log, ACT.Exp).then_inc(a_exp_ready, 1)
            act.sem_inc(s["b0_ev"], 1)
            act.wait_ge(ones_set, 2)

            def spread(g, k):
                act.wait_ge(s["b0_pe"], before_t(g, k) + 1)
                act.copy(x3[0:D, 0, 0, k % SLOTS, :], bank(0)[0:D, :]).then_inc(s["hi"], 1)

            def moved(dst, src, side):
                dst, src = (a.rearrange("p s (a w) -> p s a w", w=SIDE) for a in (dst, src))
                to, frm = (slice(1, SIDE), slice(0, SIDE - 1)) if side < 0 else (slice(0, SIDE - 1), slice(1, SIDE))
                return act.copy(dst[:, :, :, to], src[:, :, :, frm].bitcast(F32))

            third = [slice(n * SIDE, (n + 1) * SIDE) for n in range(4)]

            def shift_most(g, k):
                act.wait_ge(s["b0_ev"], before_t(g, k) + 2)
                moved(x3[0:D, :, 1, k % SLOTS, :], x3[0:D, :, 0, k % SLOTS, :], -1)

                moved(x3[third[3], :, 0, k % SLOTS, :], x3[third[0], :, 0, k % SLOTS, :], 1)

            def shift_rest(g, k):
                here = x3[:, :, 0, k % SLOTS, :]
                moved(x3[third[3], :, 1, k % SLOTS, :], here[third[1]], 1)
                for n, half in enumerate((0, 1, 0)):
                    ins = moved(rest[third[n], k % SLOTS, :].unsqueeze(1), here[third[2], half:half + 1], 1)
                ins.then_inc(s["x3"], 1)

            def conv_tanh(g, i):
                act.wait_ge(s["cv"], g * SIDE + (i + 1))
                need(act, s["cv_ev"], g * SIDE + i)
                act.activation(th[:, 0:CONV], bank(1 + i % 2)[:, 0:CONV], ACT.Tanh).then_inc(s["cv_th"], 1)

            def decays(g, c):
                act.wait_ge(s["cs"], g * NQ + (c + 1))
                act.activation(ex3[:, c % 2, :, :, :].rearrange("p a b c -> p (a b c)"), bank(7)[:, 0:3 * Q * NH], ACT.Exp).then_inc(s["ex"], 1)

            def pair_decay(g, i):
                act.wait_ge(s["d_pe"], g * SIDE + (i + 1))
                act.activation(ll[:, i % 2, :, :].rearrange("p a b -> p (a b)"), bank(4)[:, 0:NH * SIDE], ACT.Exp).then_inc(s["l"], 1)

            def z_tanh(g, q, n):
                act.wait_ge(s["z_pe"], g * (2 * NQ) + (2 * q + n + 1))
                need(act, s["z_ev"], g * (2 * NQ) + (2 * q + n))
                act.activation(thz[0:D, :], bank(3)[0:D, :], ACT.Tanh).then_inc(s["z_th"], 1)

            def affine(g, c, n):
                act.wait_ge(s["b0_pe"], before_u(g, c) + (n + 1))
                act.activation(g4[0:D, n, :], bank(0)[0:D, :], ACT.Identity, bias=beta[0:D, n:n + 1], scale=gamma[0:D, n:n + 1]).then_inc(s["b0_ev"], 1)

            def step(g, r):
                if (i := row(g, r, 0)) is not None:
                    conv_tanh(g, i)
                if (k := quad(g, r, 1 - T_AHEAD)) is not None:
                    shift_rest(g, k)
                if (c := quad(g, r, 5)) is not None:
                    decays(g, c)
                if (c := quad(g, r, U_LAG)) is not None:
                    affine(g, c, 0)
                if (q := quad(g, r, 4)) is not None:
                    z_tanh(g, q, 0)
                if (q := quad(g, r, 5)) is not None:
                    z_tanh(g, q, 1)
                if (c := quad(g, r, U_LAG)) is not None:
                    affine(g, c, 1)
                if (k := quad(g, r, -T_AHEAD)) is not None:
                    spread(g, k)
                if (i := row(g, r, 5)) is not None:
                    pair_decay(g, i)
                if (k := quad(g, r, -T_AHEAD)) is not None:
                    shift_most(g, k)
                if (q := quad(g, r, 3)) is not None:
                    act.wait_ge(s["raw"], g * NQ + (q + 1))
                    act.activation(sp[:, 1, :], sp[:, 0, :], ACT.Exp, scale=-1.0).then_inc(s["exp_dt"], 1)

            steps_of_rows(act, step)
            act.wait_ge(stage_end, 3)
            act.wait_ge(ffn_in, 16 * 12)
            ffn(ffn_sems[1])

        @block.tensor
        def _(pe):
            pe.wait_ge(const_in, 16)
            pe.wait_ge(mix_in, 16 * 23)

            held = [0]

            def apart():
                pe.sem_inc(waited, 1)
                held[0] += G

            pe.matmul(bank(5)[0:D + 1, 0:D], wc[0:D, 0:D + 1], wo_t[0:D, :], start=True, stop=True).then_inc(prep_pe, 1)
            pe.wait_ge(prep_done, 1)
            with pe.Fori(0, G) as g:
                def bank01(k):
                    pe.wait_ge(m_b01_ev, g * (2 * NQ) + (k + 1))

                def to_columns(q):
                    pe.wait_ge(m_ln, g * NQ + (q + 1))
                    bank01(q)
                    for i in range(Q):
                        ins = pe.transpose(bank(q % 2)[0:D, i * P:(i + 1) * P], xn[:, Q * q + i, :], ident)
                    ins.then_inc(m_b01_pe, 1)

                to_columns(0)
                pe.wait_ge(m_w_add, g * NQ + NQ)
                for r in range(SIDE // 2):
                    q = r // 2
                    if r % 2 == 0:
                        if q + 1 < NQ:
                            to_columns(q + 1)
                        pe.wait_ge(m_b01_ev, g * (2 * NQ) + (2 + q + 1))
                    if r >= 2:
                        pe.wait_ge(m_v_ev, g * (SIDE // 2) + (r - 1))
                    for i in range(2):
                        h = 2 * r + i
                        ins = pe.matmul(bank(2 + r % 2)[:, i * 256:i * 256 + NV], xt0[0:D + 1, h % (2 * Q) * P:(h % (2 * Q) + 1) * P], rhs0[0:D + 1, :], start=True, stop=True)
                    ins.then_inc(m_v_pe, 1)
                pe.wait_ge(m_yb, g + 1)
                apart()
                for m, src in enumerate((yb[:, 0, :], ywt)):
                    ins = pe.transpose(bank(4)[0:64, m * P:(m + 1) * P], src, ident)
                ins.then_inc(m_yt_pe, 1)
                pe.wait_ge(m_yt_ev, g + 1)
                for m in range(2):
                    for n in range(2):
                        ins = pe.matmul(bank(6 - 2 * m + n), yt[0:65, m, :], w2z[0:65, m, n * BANK:(n + 1) * BANK], start=True, stop=True)
                    ins.then_inc(m_z_pe, 1)
                for m in range(2):
                    pe.wait_ge(m_at, g * 2 + (m + 1))
                    for q in range(NQ):
                        if m == 0:
                            bank01(NQ + q)
                        elif q >= 2:
                            pe.wait_ge(m_w_add, g * NQ + (NQ + q - 1))
                        apart()
                        for i in range(Q):
                            w = Q * q + i
                            for b in range(PACK):
                                pb = slice(b * SIDE, (b + 1) * SIDE)
                                val = vh[pb, w, :] if m == 0 else vc[pb, w, 0:D]
                                ins = pe.matmul(bank(2 * m + q % 2)[pb, i * D:(i + 1) * D], at[pb, m, :, w], val, start=True, stop=True)
                        ins.then_inc(m_b01_pe if m == 0 else m_w_pe, 1)

            def product(dst, left, right, start=True, stop=True):
                pe.matmul(dst, left[0], right[0], start=start, stop=False)
                pe.matmul(dst, left[1], right[0], start=False, stop=False)
                return pe.matmul(dst, left[0], right[1], start=False, stop=stop)

            def halves(a):
                return a[:, 0], a[:, 1]

            def ffn(f):
                def x_in_columns(t):
                    pe.wait_ge(f["ln"], t + 1)
                    need(pe, f["xt"], t)
                    for i in range(Q):
                        ins = pe.transpose(bank(4)[0:D, i * P:(i + 1) * P], xn4[:, i, :], ident)
                    ins.then_inc(f["xt_pe"], 1)

                def y_in_rows(t, e):
                    pe.wait_ge(f["y_ev"], t * NEXP + (e + 1))
                    need(pe, f["comb"], t * NEXP + (e - 1))
                    for i in range(Q):
                        ins = pe.transpose(bank(6 + e % 2)[:, i * D:(i + 1) * D], yte[0:D, e % 2, i * P:(i + 1) * P], ident[0:D, 0:D])
                    ins.then_inc(f["yt_pe"], 1)

                def up(t, par, c):
                    need(pe, f["gelu"], t * NC + (c - 1))
                    product(bank(c % 2), halves(w1r[0:D + 1, :, c * P:(c + 1) * P]), halves(xtr[0:D + 1, :, par, :])).then_inc(f["up"], 1)

                def down(t, c):
                    e, n = divmod(c, CPE)
                    if n == 0:
                        need(pe, f["y_ev"], t * NEXP + (e - 1))
                    mine = [x for x in range(NC) if (x in POOL_CHUNKS) == (c in POOL_CHUNKS)]
                    pe.wait_ge(f["low_pool" if c in POOL_CHUNKS else "low"], t * len(mine) + (mine.index(c) + 1))
                    product(bank(2 + e % 2)[0:D, :], halves(w2r[:, :, c, :]), halves(hidr[:, :, c % RING, :]), n == 0, n == CPE - 1).then_inc(f["down"], 1)

                def tile(t, par=None):
                    first, last = (isinstance(t, int) and t == n for n in (0, NT - 1))
                    par = t % 2 if par is None else par
                    if first:
                        x_in_columns(t)
                    pe.wait_ge(f["xt"], t + 1)
                    for c in range(2 * NC if last else NC):
                        if c < NC:
                            up(t, par, c)
                        if c == 0:
                            for i in range(Q):
                                ins = product(bank(5)[:, i * NEXP:(i + 1) * NEXP], halves(xtr[0:D + 1, :, par, i * P:(i + 1) * P]), halves(gwr[0:D + 1, :, :]))
                            ins.then_inc(f["gate_pe"], 1)
                        if LAG <= c < NC + LAG:
                            down(t, c - LAG)
                        elif c < LAG and not first:
                            down(t - 1, NC + c - LAG)
                        if c == 5 and not last:
                            x_in_columns(t + 1)
                        for before, e in experts_due(t, c, LAG + 2):
                            y_in_rows(t - before, e)

                pe.wait_ge(f["parts"], 1)
                tiles(pe, tile)

            pe.wait_ge(stage_end, 1)
            ffn(ffn_sems[0])

            def to_columns(g, k):
                pe.wait_ge(s["ln"], g * NQ + (k + 1))
                pe.wait_ge(s["b0_ev"], before_t(g, k) + 1)
                for i in range(Q):
                    ins = pe.transpose(bank(0)[0:D, i * P:(i + 1) * P], xn[:, k % 2 * Q + i, :], ident)
                ins.then_inc(s["b0_pe"], 1)

            def conv(g, i):
                h = i % SIDE
                if h == 0:
                    pe.wait_ge(s["x3"], g * NQ + (i // Q + 1))
                if h % Q == Q - 1 and h < SIDE - 1:
                    pe.wait_ge(s["x3"], g * NQ + (i // Q + 2))
                need(pe, s["cv_ev"], g * SIDE + (i - 1))
                rows = [y for y in (0, -1, 1) if 0 <= h + y < SIDE]
                dst = bank(1 + i % 2)
                for y in rows:
                    slot = (h + y) // Q % SLOTS
                    tokens = slice((h + y) % Q * P, ((h + y) % Q + 1) * P)
                    c = CONV if y else CONVD
                    for n in range(2):
                        w = CONV if n else c
                        for x_part, w_part in ((0, 0), (0, 1), (1, 0)):
                            pe.matmul(dst[:, 0:w], x3[:, x_part, n, slot, tokens], wtap[:, w_part, n, y + 1, 0:w],
                                      start=(y == 0 and n == x_part == w_part == 0), stop=False)
                    k = D if y else D + 2
                    ins = pe.matmul(dst[:, 0:c], rest[0:k, slot, tokens], wrest[0:k, y + 1, 0:c], start=False, stop=(y == rows[-1]))
                ins.then_inc(s["cv"], 1)

            def z_columns(g, q, n):
                need(pe, s["z_ev"], g * (2 * NQ) + (2 * q + n))
                if n == 0:
                    need(pe, s["o_add"], g * NQ + (q - 2))
                product(bank(3)[0:D, :], halves(wz[0:D, :, n, :]), halves(x3[0:D, :, 0, q % SLOTS, :])).then_inc(s["z_pe"], 1)

            def sums(g, c):
                pe.wait_ge(s["a"], g * NQ + (c + 1))
                a = av[:, c % 2, :, :].rearrange("p a b -> p (a b)")
                for n, w in enumerate((upto, later, whole)):
                    ins = pe.matmul(bank(7)[:, n * Q * NH:(n + 1) * Q * NH], w, a, start=True, stop=True)
                ins.then_inc(s["cs"], 1)

            def pairs(g, i):
                c = i // Q
                need(pe, s["m"], g * SIDE + i)
                if i % Q == 0:
                    pe.wait_ge(s["apart"], g * NQ + (c + 1))
                pe.matmul(bank(4)[:, NH * SIDE:NH * SIDE + SIDE], b_apart[:, c % 2, i % Q, :], ct[:, c % 2, i % Q, :], start=True, stop=True)
                pe.wait_ge(s["r"], g * SIDE + (i + 1))
                pe.matmul(bank(4)[:, 0:NH * SIDE], later, rr[:, i % Q, :, :].rearrange("p a b -> p (a b)"), start=True, stop=True).then_inc(s["d_pe"], 1)

            def scan(g, i):
                c, j = i // Q, i % Q
                if j == 0:
                    pe.wait_ge(s["xdt"], g * NQ + (c + 1))
                need(pe, s["y"], g * SIDE + i)
                pe.wait_ge(s["m"], g * SIDE + (i + 1))
                pe.wait_ge(s["state"], g * SIDE + (i + 1))
                pe.matmul(bank(5)[:, INNER:2 * INNER], c_apart[:, c % 2, j, :], st[:, :, :].rearrange("p a b -> p (a b)"), start=True, stop=True)
                for n in range(NH):
                    for b in range(PACK):
                        pb = slice(b * SIDE, (b + 1) * SIDE)
                        ins = pe.matmul(bank(5)[pb, n * HD:(n + 1) * HD], mm[pb, i % 2, n, :], xdt[pb, c % 2, j, n, :], start=True, stop=True)
                ins.then_inc(s["y_pe"], 1)
                if j == 0:
                    pe.wait_ge(s["xw"], g * NQ + (c + 1))
                pe.matmul(bank(6)[:, 0:INNER], b_rows[:, c % 2, j, :], xw[:, c % 2, j, :, :].rearrange("p a b -> p (a b)"), start=True, stop=True).then_inc(s["ds_pe"], 1)

            def u_columns(g, c, n):
                pe.wait_ge(s["u"], g * NQ + (c + 1))
                pe.wait_ge(s["b0_ev"], before_u(g, c) + (n + 1))
                for i in range(Q):
                    ins = pe.transpose(bank(0)[0:D, i * P:(i + 1) * P], u4[:, i, n * D:(n + 1) * D], ident)
                ins.then_inc(s["b0_pe"], 1)

            def project(g, c):
                pe.wait_ge(s["gate"], g * NQ + (c + 1))
                last = 2 * (c + 3)
                pe.wait_ge(s["z_ev"], g * (2 * NQ) + (min(last, 2 * NT) if isinstance(g, int) else last))
                for i in range(Q):
                    for n in range(2):
                        ins = pe.matmul(bank(3)[:, i * D:(i + 1) * D], g4[0:D, n, i * P:(i + 1) * P], wout[0:D, n, :], start=(n == 0), stop=(n == 1))
                ins.then_inc(s["o_pe"], 1)

            def step(g, r):
                if (i := row(g, r, 0)) is not None:
                    conv(g, i)
                if (c := quad(g, r, U_LAG)) is not None:
                    u_columns(g, c, 0)
                if (q := quad(g, r, 4)) is not None:
                    z_columns(g, q, 0)
                if (q := quad(g, r, 5)) is not None:
                    z_columns(g, q, 1)
                if (k := quad(g, r, -T_AHEAD)) is not None:
                    to_columns(g, k)
                if (i := row(g, r, 6)) is not None:
                    scan(g, i)
                if (c := quad(g, r, 5)) is not None:
                    sums(g, c)
                if (c := quad(g, r, U_LAG)) is not None:
                    u_columns(g, c, 1)
                if (c := quad(g, r, 14)) is not None:
                    project(g, c)
                if (i := row(g, r, 5)) is not None:
                    pairs(g, i)

            steps_of_rows(pe, step, weights=lambda: pe.wait_ge(prep_done, 2))
            pe.wait_ge(stage_end, 3)
            ffn(ffn_sems[1])
            pe.wait_ge(waited, held[0])

        def mixer1(dve, ch):
            dve.wait_ge(ssm_in, 16 * 13)
            dve.wait_ge(a_exp_ready, 1)
            ch.done(dve.tensor_scalar(neg_a, a_exp, -1.0, None, ALU.mult))
            ch.done(dve.tensor_scalar(wtap0[D:D + 2, CENTRE, 0:CONV], wtap0[D:D + 2, CENTRE, 0:CONV], 0.5, None, ALU.mult))
            def conv_silu(g, i):
                b = bank(1 + i % 2)
                dve.wait_ge(s["cv_th"], g * SIDE + (i + 1))
                ch.done(dve.tensor_copy(dtr[:, i // Q % 2, i % Q, :], b[:, CONV:CONV + NH]))
                dve.scalar_tensor_tensor(xbc[:, i // Q % 2, i % Q, 0:CONV], th[:, 0:CONV], 1.0, b[:, 0:CONV], ALU.add, ALU.mult).then_inc(s["cv_ev"], 1)

            def weigh(g, c):
                dve.wait_ge(s["ex"], g * NQ + (c + 1))
                dve.tensor_tensor(wdt[:, :, :], dt[:, c % 2, :, :], ex3[:, c % 2, 1, :, :], ALU.mult).then_inc(s["w"], 1)

            def attend(g, i):
                dve.wait_ge(s["l"], g * SIDE + (i + 1))
                ch.link(dve.tensor_tensor(gmk, bank(4)[:, NH * SIDE:NH * SIDE + SIDE], tri, ALU.mult))
                dve.tensor_tensor(mm[:, i % 2, :, :], ll[:, i % 2, :, :], gmk.unsqueeze(1).to_broadcast([P, NH, SIDE]), ALU.mult).then_inc(s["m"], 1)

            def gather(g, i):
                c, j = i // Q, i % Q
                y = yy[:, c % 2, j, :].rearrange("p (h e) -> p h e", e=HD)
                heads = bank(5)[:, 0:2 * INNER].rearrange("p (a h e) -> p a h e", a=2, e=HD)
                dve.wait_ge(s["y_pe"], g * SIDE + (i + 1))
                ch.link(dve.tensor_tensor(y, heads[:, 1], ex3[:, c % 2, 0, j, :].unsqueeze(2).to_broadcast([P, NH, HD]), ALU.mult))
                dve.tensor_tensor(y, y, heads[:, 0], ALU.add).then_inc(s["y"], 1)
                dve.wait_ge(s["s1"], g * SIDE + (i + 1))
                dve.wait_ge(s["ds_pe"], g * SIDE + (i + 1))
                if i % SIDE == SIDE - 1:
                    dve.memset(st[:, :, :], 0.0).then_inc(s["state"], 1)
                else:
                    dve.tensor_tensor(st[:, :, :], st1[:, :, :], bank(6)[:, 0:INNER].rearrange("p (h e) -> p h e", e=HD), ALU.add).then_inc(s["state"], 1)
                if j == 0:
                    dve.wait_ge(s["xd"], g * NQ + (c + 1))
                dve.wait_ge(s["y"], g * SIDE + (i + 1))
                ch.done(dve.tensor_tensor(y, y, xd[:, c % 2, j, :, :], ALU.add))

            flat = lambda a: a.rearrange("p a b -> p (a b)")

            def time_steps_begin(g, q):
                x = flat(dtr[:, q % 2, :, :])
                ch.wait()
                dve.scalar_tensor_tensor(sp[:, 0, :], x, -1.0, x, ALU.mult, ALU.max).then_inc(s["raw"], 1)
                ch.done(dve.tensor_scalar(sp[:, 5, :], x, 0.0, None, ALU.max))
                dve.wait_ge(s["cv_ev"], g * SIDE + (Q * q + Q))
                ch.done(dve.transpose(bt[:, :, :], xbc[:, q % 2, :, INNER:INNER + SIDE]))
                dve.transpose(ct[:, q % 2, :, :], xbc[:, q % 2, :, INNER + NS:INNER + NS + SIDE]).then_inc(s["bt"], 1)

            def time_steps(g, q):
                dve.wait_ge(s["exp_dt"], g * NQ + (q + 1))
                u, r, r2, p = sp[:, 1, :], sp[:, 2, :], sp[:, 3, :], sp[:, 4, :]
                ch.link(dve.tensor_scalar(r, u, 2.0, None, ALU.add))
                ch.link(dve.reciprocal(r, r))
                ch.link(dve.tensor_tensor(r, r, u, ALU.mult))
                ch.link(dve.tensor_tensor(r2, r, r, ALU.mult))
                ch.link(dve.tensor_scalar(p, r2, 1.0 / 15, None, ALU.mult))
                for k in (13, 11, 9, 7, 5, 3):
                    ch.link(dve.scalar_tensor_tensor(p, p, 1.0 / k, r2, ALU.add, ALU.mult))
                ch.link(dve.scalar_tensor_tensor(p, p, 1.0, r, ALU.add, ALU.mult))
                ch.link(dve.scalar_tensor_tensor(flat(dt[:, q % 2, :, :]), p, 2.0, sp[:, 5, :], ALU.mult, ALU.add))
                dve.tensor_tensor(av[:, q % 2, :, :], dt[:, q % 2, :, :], neg_a.unsqueeze(1).to_broadcast([P, Q, NH]), ALU.mult).then_inc(s["a"], 1)

            def low(g, k):
                dve.wait_ge(s["hi"], g * NQ + (k + 1))
                dve.tensor_tensor(x3[0:D, 1, 0, k % SLOTS, :], bank(0)[0:D, :], x3[0:D, 0, 0, k % SLOTS, :].bitcast(F32), ALU.subtract).then_inc(s["b0_ev"], 1)

            def z_silu(g, q, n):
                dve.wait_ge(s["z_th"], g * (2 * NQ) + (2 * q + n + 1))
                need(dve, s["gate"], g * NQ + (q - 1))
                dve.scalar_tensor_tensor(szt[0:D, q % 2, n, :], thz[0:D, :], 1.0, bank(3)[0:D, :], ALU.add, ALU.mult).then_inc(s["z_ev"], 1)

            def gate(g, c):
                dve.wait_ge(s["b0_ev"], before_u(g, c) + 3)
                dve.wait_ge(s["z_ev"], g * (2 * NQ) + (2 * c + 2))
                ch.done(dve.tensor_tensor(g4[0:D, 0, :], g4[0:D, 0, :], szt[0:D, c % 2, 0, :], ALU.mult))
                dve.tensor_tensor(g4[0:D, 1, :], g4[0:D, 1, :], szt[0:D, c % 2, 1, :], ALU.mult).then_inc(s["gate"], 1)

            def quad_rows(g, k):
                group = g + k // NQ
                return xr[:, group, k % NQ * Q:(k % NQ + 1) * Q, :]

            def add_output(g, c):
                dve.wait_ge(s["o_pe"], g * NQ + (c + 1))
                rows = quad_rows(g, c)
                dve.tensor_tensor(rows, rows, bank(3)[:, 0:Q * D].rearrange("p (a b) -> p a b", b=D), ALU.add).then_inc(s["o_add"], 1)

            def norm_y(g, c, part):
                if part == 0:
                    ch.wait()
                layer_norm(dve, ch, lambda n: yy[:, c % 2, n, :], lambda n: u4[:, n, :], Q, INNER, 1e-5, g * NQ + (c + 1), s["u"], part, y_norm)

            def norm_x(g, k, part):
                layer_norm(dve, ch, lambda n: quad_rows(g, k)[:, n, :], lambda n: xn[:, k % 2 * Q + n, :], Q, D, 1e-6, g * NQ + (LN_MIX1 + k + 1), s["ln"], part)

            def step(g, r):
                ch.wait()
                if (c := quad(g, r, 12)) is not None:
                    gate(g, c)
                if (i := row(g, r, 0)) is not None:
                    conv_silu(g, i)
                if (c := quad(g, r, 10)) is not None:
                    norm_y(g, c, 1)
                if (k := quad(g, r, -5)) is not None:
                    norm_x(g, k, 1)
                if (c := quad(g, r, 5)) is not None:
                    weigh(g, c)
                if (q := quad(g, r, 4)) is not None:
                    z_silu(g, q, 0)
                if (i := row(g, r, 6)) is not None:
                    gather(g, i)
                if (i := row(g, r, 5)) is not None:
                    attend(g, i)
                if (k := quad(g, r, -T_AHEAD)) is not None:
                    low(g, k)
                if (q := quad(g, r, 5)) is not None:
                    z_silu(g, q, 1)
                if (q := quad(g, r, 4)) is not None:
                    time_steps(g, q)
                if (c := quad(g, r, 9)) is not None:
                    norm_y(g, c, 0)
                if (k := quad(g, r, -6)) is not None:
                    norm_x(g, k, 0)
                if (c := quad(g, r, 14)) is not None:
                    add_output(g, c)
                if (q := quad(g, r, 3)) is not None:
                    time_steps_begin(g, q)

            def weights():
                dve.wait_ge(s["folded"], 1)
                ch.done(dve.memset(wtap[D:P, :, 0, 1, CONV:CONVD].bitcast(F32), 0.0))
                ch.done(dve.memset(wrest[0:D, 1, CONV:CONVD].bitcast(F32), 0.0))
                ch.done(split(dve, ch, wz0[0:D, :, :], wz[0:D]))
                by_row = wtap0[0:D].rearrange("p (y x) c -> p y x c", y=ROWS3)
                for n in range(2):
                    ch.done(split(dve, ch, by_row[:, :, 1 - n, 0:CONV], wtap[0:D, :, n, :, 0:CONV]))
                ch.done(split(dve, ch, by_row[:, 1, 1, CONV:CONVD], wtap[0:D, :, 0, 1, CONV:CONVD]))
                ch.link(split(dve, ch, by_row[:, :, 2, 0:CONV], wright[0:D]))
                third = [slice(n * SIDE, (n + 1) * SIDE) for n in range(4)]
                for n in range(2):
                    ch.done(dve.tensor_copy(wtap[third[3], :, n, :, 0:CONV], wright[third[n]].bitcast(F32)))
                for n, half in enumerate((0, 0, 1)):
                    ch.done(dve.tensor_copy(wrest[third[n], :, 0:CONV], wright[third[2], half].bitcast(F32)))
                bias, parts, picked = wtap0[D:D + 2, CENTRE, :], wrest[D:D + 2, 1, :], wtap0[D:D + 2, 0, :]
                ch.link(dve.tensor_copy(parts, bias))
                ch.link(dve.tensor_tensor(picked, bias, parts.bitcast(F32), ALU.subtract))
                ch.link(dve.tensor_scalar(picked, picked, ident[D:D + 2, D + 1:D + 2], None, ALU.mult))
                ch.link(dve.scalar_tensor_tensor(parts, parts.bitcast(F32), ident[D:D + 2, D:D + 1], picked, ALU.mult, ALU.add))
                dve.sem_inc(prep_done, 1)
                dve.memset(st[:, :, :], 0.0).then_inc(s["state"], 1)

            steps_of_rows(dve, step, lambda g: ch.enter(g, CHAIN_MIX1), lambda: ch.leave(G - 1, CHAIN_MIX1), weights)
            dve.wait_ge(s["o_add"], G * NQ)

        @block.vector
        def _(dve):
            ch = Chain(dve, dve_chain)
            ch.done(dve.memset(xt0[D:D + 1, :], 1.0))
            ch.done(dve.memset(rhs0[D:D + 1, 0:D], 0.0))
            dve.wait_ge(mix_in, 16 * 23)
            ch.done(dve.tensor_copy(rhs0[0:D, 0:D], wo_t[0:D, :]))
            dve.wait_ge(prep_pe, 1)
            ch.done(dve.tensor_copy(rhs0[0:D, D:2 * D], bank(5)[0:D, 0:D]))
            ch.wait()
            dve.tensor_tensor(rhs0[D:D + 1, D:2 * D], bank(5)[D:D + 1, 0:D], bo[D:D + 1, :], ALU.add).then_inc(prep_done, 1)
            dve.sem_inc(m_w_add, NQ)

            def normalise(g, part=None, rows=None):
                if part != 1:
                    dve.wait_ge(x_in, g * 64 + 64)
                layer_norm(dve, ch, lambda r: xr[:, g, r, :], lambda r: xn[:, r, :], SIDE, D, 1e-6, g + 1, m_ln, part, rows=rows)

            def group(g):
                dve.wait_ge(m_v_ev, g * (SIDE // 2) + SIDE // 2)
                ch.done(dve.tensor_copy(yb[:, 0, :].rearrange("p (e h) -> p e h", e=2), vc[:, :, 2 * D:2 * D + 2].rearrange("p h e -> p e h")))
                ch.link(dve.tensor_copy(yb[:, 1, :].rearrange("p (e h) -> p e h", e=2), vc[:, :, 2 * D + 2:NV].rearrange("p h e -> p e h")))
                dve.transpose(ywt, yb[:, 1, :]).then_inc(m_yb, 1)
                ch.done(dve.transpose(vh[:, :, :].rearrange("p w d -> p d w"), vc[:, :, 0:D].rearrange("p h d -> p d h")))
                ch.done(dve.tensor_tensor(xr[:, g, :, :], xr[:, g, :, :], vc[:, :, D:2 * D], ALU.add))
                for m in range(2):
                    z = bank(6 - 2 * m, 2).rearrange("p (i j) -> p i j", j=SIDE)
                    dve.wait_ge(m_z_pe, g * 2 + (m + 1))
                    ch.link(dve.tensor_reduce(row_max, z, AX.X, ALU.max))
                    dve.tensor_tensor(sc[:, :, :], z, row_max.unsqueeze(2).to_broadcast([P, SIDE, SIDE]), ALU.subtract).then_inc(m_sub, 1)
                    dve.wait_ge(m_exp, g * 2 + (m + 1))
                    ch.link(dve.tensor_reduce(row_sum, at[:, m, :, :], AX.X, ALU.add))
                    ch.link(dve.reciprocal(row_inv, row_sum))
                    ch.link(dve.tensor_tensor(sc[:, :, :], at[:, m, :, :], row_inv.unsqueeze(2).to_broadcast([P, SIDE, SIDE]), ALU.mult))
                    dve.transpose(at[:, m, :, :], sc[:, :, :]).then_inc(m_at, 1)
                ch.wait()
                if not isinstance(g, int):
                    normalise(g + 1, 0)
                for q in range(NQ):
                    dve.wait_ge(m_w_pe, g * NQ + (q + 1))
                    rows = xr[:, g, Q * q:Q * q + Q, :]
                    dve.tensor_tensor(rows, rows, bank(2 + q % 2)[:, 0:Q * D].rearrange("p (a b) -> p a b", b=D), ALU.add).then_inc(m_w_add, 1)
                    if not isinstance(g, int) and q:
                        normalise(g + 1, 1, range(Q * (q - 1), Q * (q + 1 if q == NQ - 1 else q)))
                dve.wait_ge(m_w_add, g * NQ + 2 * NQ)
                dve.wait_ge(m_b01_ev, g * (2 * NQ) + (2 + 2 * NQ))
                ch.link(dve.transpose(ohw[:, :, :].rearrange("p h d -> p d h"), oh[:, :, :].rearrange("p w d -> p d w")))
                ch.link(dve.tensor_tensor(xr[:, g, :, :], xr[:, g, :, :], ohw[:, :, :], ALU.add))

            normalise(0)
            with dve.Fori(0, G - 1) as g:
                ch.enter(g, CHAIN_MIX0)
                group(g)
                ch.leave(G - 1, CHAIN_MIX0)
            group(G - 1)

            def ffn(f, ln_before):
                def token_rows(t):
                    return xr[:, :, :, :].rearrange("p g h d -> p (g h) d").rearrange("p (t q) d -> p t q d", q=Q)[:, t, :, :]

                def norm(t, part):
                    layer_norm(dve, ch, lambda r: token_rows(t)[:, r, :], lambda r: xn4[:, r, :], Q, D, 1e-5, t + (ln_before + 1), f["ln"], part)

                def combine(t, par, e):
                    dve.wait_ge(f["yt_pe"], t * NEXP + (e + 1))
                    need(dve, f["comb"], t * NEXP + e)
                    for i in range(Q):
                        row = token_rows(t)[:, i, :]
                        ins = dve.scalar_tensor_tensor(row, bank(6 + e % 2)[:, i * D:(i + 1) * D], gm[:, par, i, e:e + 1], row, ALU.mult, ALU.add)
                    ins.then_inc(f["comb"], 1)

                def over(a):
                    return a.unsqueeze(2).to_broadcast([P, Q, NEXP])

                def gate_distance(t):
                    sco = bank(5)[:, 0:Q * NEXP].rearrange("p (a b) -> p a b", b=NEXP)
                    dve.wait_ge(f["gate_pe"], t + 1)
                    ch.link(dve.tensor_reduce(gcol[:, 0, :], sco, AX.X, ALU.max))
                    dve.tensor_tensor(gd[:, :, :], sco, over(gcol[:, 0, :]), ALU.subtract).then_inc(f["gate_d"], 1)

                def gate_rank(t):
                    dve.wait_ge(f["gate_d"], t + 1)
                    other = gd[:, :, :].unsqueeze(2).to_broadcast([P, Q, NEXP, NEXP])
                    own = gd[:, :, :].unsqueeze(3).to_broadcast([P, Q, NEXP, NEXP])
                    ch.done(dve.tensor_tensor(gcmp[:, :, :, :], other, own, ALU.is_gt))
                    ch.link(dve.tensor_tensor(geq[:, :, :, :], other, own, ALU.is_equal))
                    ch.link(dve.tensor_tensor(geq[:, :, :, :], geq[:, :, :, :], lower.unsqueeze(1).to_broadcast([P, Q, NEXP, NEXP]), ALU.mult))
                    ch.link(dve.tensor_tensor(gcmp[:, :, :, :], gcmp[:, :, :, :], geq[:, :, :, :], ALU.add))
                    ch.done(dve.tensor_reduce(gmask[:, :, :], gcmp[:, :, :, :], AX.X, ALU.add))

                def gate_exp(t):
                    dve.wait_ge(f["tanh"], t + 1)
                    ch.link(dve.tensor_scalar(gn[:, :, :], gth[:, :, :], -1.0, 1.0, ALU.mult, ALU.add))
                    ch.link(dve.reciprocal(gn[:, :, :], gn[:, :, :]))
                    ch.link(dve.scalar_tensor_tensor(ge[:, :, :], gth[:, :, :], 1.0, gn[:, :, :], ALU.add, ALU.mult))
                    ch.done(dve.tensor_reduce(gcol[:, 1, :], ge[:, :, :], AX.X, ALU.add))
                    ch.link(dve.scalar_tensor_tensor(gn[:, :, :], gmask[:, :, :], 2.0, ge[:, :, :], ALU.is_lt, ALU.mult))

                def gate_weights(t, par):
                    ch.link(dve.tensor_reduce(gcol[:, 2, :], gn[:, :, :], AX.X, ALU.add))
                    ch.link(dve.scalar_tensor_tensor(gcol[:, 3, :], gcol[:, 1, :], 1e-9, gcol[:, 2, :], ALU.mult, ALU.add))
                    ch.link(dve.reciprocal(gcol[:, 0, :], gcol[:, 3, :]))
                    ch.done(dve.tensor_tensor(gm[:, par, :, :], gn[:, :, :], over(gcol[:, 0, :]), ALU.mult))

                def columns(t, par):
                    dve.wait_ge(f["xt_pe"], t + 1)
                    need(dve, f["up"], t * NC - NC)
                    split(dve, ch, bank(4)[0:D, :], xtr[0:D, :, par, :]).then_inc(f["xt"], 1)

                def tile(t, par=None):
                    first, last = (isinstance(t, int) and t == n for n in (0, NT - 1))
                    par = t % 2 if par is None else par
                    if not isinstance(t, int):
                        ch.enter(t - 2, CHAIN_FFN)
                    for c in range(2 * NC if last else NC):
                        if c < NC and c not in POOL_CHUNKS:
                            dve.wait_ge(f["gelu"], t * NC + (c + 1))
                            r = c % RING
                            dve.tensor_tensor(hidr[:, 1, r, :], hid[:, r, :], hidr[:, 0, r, :].bitcast(F32), ALU.subtract).then_inc(f["low"], 1)
                        if c == 0:
                            gate_distance(t)
                            if not last:
                                norm(t + 1, 0)
                        if c == 2:
                            gate_rank(t)
                            if not last:
                                norm(t + 1, 1)
                        if c == 6:
                            gate_exp(t)
                            gate_weights(t, par)
                        if c == 7 and not last:
                            columns(t + 1, 1 - par)
                        for before, e in experts_due(t, c, LAG + 3):
                            if e == 0:
                                ch.wait()
                            combine(t - before, 1 - par if before else par, e)
                    if not isinstance(t, int):
                        if par == 0:
                            assert ch.n == CHAIN_FFN, ch.n
                            ch.base, ch.n = ch.start, 0
                        else:
                            ch.leave(NT - 4, CHAIN_FFN)

                dve.wait_ge(stage_end, 1 if ln_before == LN_FFN0 else 3)
                ch.done(dve.memset(xtr[D:D + 1, 0, :, :].bitcast(F32), 1.0))
                ch.done(dve.memset(xtr[D:D + 1, 1, :, :].bitcast(F32), 0.0))
                norm(0, 0)
                norm(0, 1)
                columns(0, 0)
                tiles(dve, tile)
                dve.wait_ge(f["comb"], NT * NEXP)

            dve.sem_inc(stage_end, 1)
            ffn(ffn_sems[0], LN_FFN0)
            dve.sem_inc(stage_end, 1)
            mixer1(dve, ch)
            dve.sem_inc(stage_end, 1)
            ffn(ffn_sems[1], LN_FFN1)
            dve.sem_inc(stage_end, 1)


_INPUTS = ["consts", "x", "Wc", "bc", "WoT", "bo", "W1T", "W2T", "b2z", "Win_z", "Win_dt", "dt_bias", "Win_x", "b_conv",
           "W_conv", "A_log", "D_param", "gamma", "beta", "W_out"]
_FFN = ["w1", "b1", "w2", "b2T", "gate_w", "gate_b"]


def kernel(**inputs):
    import numpy as np
    import concourse.bacc as bacc
    from concourse.bass_utils import run_bass_kernel_spmd

    a = {k: np.asarray(v) for k, v in inputs.items()}
    k, l = np.arange(P)[:, None], np.arange(P)[None, :]
    one = k // SIDE == l // SIDE
    e, o = np.arange(NEXP)[:, None], np.arange(NEXP)[None, :]
    consts = np.concatenate([k == l, one & (k <= l), one & (k > l), one, k % SIDE <= np.arange(SIDE)[None, :],
                             np.broadcast_to((o < e).reshape(1, 16), (P, 16))], axis=1).astype(np.float32)

    def mixing(w):
        return w.reshape(SEG, P, SEG).transpose(0, 2, 1)

    w_in = a["L1_conv_W_in"]
    arrays = {
        "consts": consts, "x": a["x"], "Wc": a["L0_conv_Wc"], "bc": a["L0_conv_bc"].reshape(D, 1),
        "WoT": a["L0_conv_Wo"].T, "bo": a["L0_conv_bo"].reshape(1, D),
        "W1T": np.concatenate([np.concatenate([a["L0_conv_W1h"].T, a["L0_conv_W1w"].T], 1),
                               np.concatenate([a["L0_conv_b1h"], a["L0_conv_b1w"]]).reshape(1, 2 * E0)], 0),
        "W2T": np.stack([mixing(a["L0_conv_W2h"]), mixing(a["L0_conv_W2w"])]),
        "b2z": np.stack([a["L0_conv_b2h"], a["L0_conv_b2w"]]).reshape(2, 1, SIDE * SIDE),
        "Win_z": w_in[:, :INNER].reshape(D, 2, D), "Win_x": w_in[:, INNER:INNER + CONV], "Win_dt": w_in[:, INNER + CONV:],
        "dt_bias": a["L1_conv_dt_bias"].reshape(1, NH), "b_conv": a["L1_conv_b_conv"].reshape(1, CONV),
        "W_conv": a["L1_conv_W_conv"].reshape(TAPS, CONV), "A_log": a["L1_conv_A_log"], "D_param": a["L1_conv_D_param"],
        "gamma": a["L1_conv_gamma"].reshape(2, D).T, "beta": a["L1_conv_beta"].reshape(2, D).T,
        "W_out": a["L1_conv_W_out"].reshape(2, D, D).transpose(1, 0, 2),
    }
    for n in range(2):
        w = {x: a[f"L{n}_ffn_{x}"] for x in ("w1", "b1", "w2", "b2", "gate_w", "gate_b")}
        arrays |= {f"{n}_w1": w["w1"], f"{n}_b1": w["b1"].reshape(1, NEXP * HID), f"{n}_w2": w["w2"], f"{n}_b2T": w["b2"].T,
                   f"{n}_gate_w": w["gate_w"], f"{n}_gate_b": w["gate_b"].reshape(1, NEXP)}
    arrays = {f"in_{x}": np.ascontiguousarray(v) for x, v in arrays.items()}
    nc = bacc.Bacc("TRN2", target_bir_lowering=False, num_devices=1)
    aps = {x: nc.dram_tensor(x, v.shape, mybir.dt.from_np(v.dtype), kind="ExternalInput").ap() for x, v in arrays.items()}
    out = nc.dram_tensor("out", (IMG, SIDE, SIDE, D), F32, kind="ExternalOutput").ap()
    inp = {x: aps[f"in_{x}"] for x in _INPUTS}
    inp["ffn"] = [{x: aps[f"in_{n}_{x}"] for x in _FFN} for n in range(2)]
    metaformer(nc, inp, out)
    r = run_bass_kernel_spmd(nc, [arrays], core_ids=[0])
    return r.results[0]["out"]
```
